# Optimizing a Trainium2 kernel written in Bass

```python
import numpy as np
import jax
import jax.numpy as jnp

def _softmax(x, axis=-1):
    return jax.nn.softmax(x, axis=axis)

def _gelu(x):
    return jax.nn.gelu(x, approximate=True)

def _silu(x):
    return jax.nn.silu(x)

def _sigmoid(x):
    return jax.nn.sigmoid(x)

def _layernorm(x, axis=-1, eps=1e-05):
    m = jnp.mean(x, axis=axis, keepdims=True)
    v = jnp.var(x, axis=axis, keepdims=True)
    return (x - m) / jnp.sqrt(v + eps)

def _scatter_add(tgt, idx, src, axis=0):
    return tgt.at[idx].add(src)

def _segment_sum(src, seg, n):
    return jax.ops.segment_sum(src, seg, n)
kernel_name = 'mk_xattn_ffn_d1_seqx_r4_d72ffb'

def setup_inputs(seed: int=0):
    np.random.seed(seed)
    _w = jnp.asarray

    def _rec_inputs():
        import jax
        import jax.numpy as jnp
        _rk = jax.random.key(seed)
        x = -0.000125 + 0.9999 * jax.random.normal(jax.random.fold_in(_rk, 1), (8, 112, 512), jnp.float32)
        _lenS = 112 - jax.random.randint(jax.random.fold_in(_rk, 7), (8,), 0, max(1, 112 // 4) + 1, jnp.int32)
        _lenS2 = 375 - jax.random.randint(jax.random.fold_in(_rk, 8), (8,), 0, max(1, 375 // 4) + 1, jnp.int32)
        _ctx_2048P = jax.random.normal(jax.random.fold_in(_rk, 11), (8, 16, 512), jnp.float32)
        _ctx_2048c = jax.random.dirichlet(jax.random.fold_in(_rk, 511), 0.3 * jnp.ones((16,), jnp.float32), (8, 375))
        _ctx_2048t = jnp.einsum('bsk,bkd->bsd', _ctx_2048c, _ctx_2048P)
        _ctx_2048t = _ctx_2048t * jax.lax.rsqrt(jnp.mean(jnp.square(_ctx_2048t)) + 1e-12) * 0.953939
        ctx_2048 = 1.72703e-05 + 1.00003 * (_ctx_2048t + 0.3 * jax.random.normal(jax.random.fold_in(_rk, 611), (8, 375, 512), jnp.float32))
        return (x, ctx_2048)
    x, ctx_2048 = _rec_inputs()

    def _L0_xattn_setup():
        import jax, jax.numpy as jnp
        import numpy as np
        DIM = 512
        NH = 16
        HD = DIM // NH
        EPS = 1e-06
        IMG_LEN = 257

        def rms_norm(x, w, eps=EPS):
            xf = x.astype(jnp.float32)
            y = xf * jax.lax.rsqrt(jnp.mean(xf * xf, axis=-1, keepdims=True) + eps)
            return y.astype(x.dtype) * w

        def linear(x, w, b):
            return jnp.einsum('blc,oc->blo', x, w) + b

        def attention(q, k, v):
            scale = 1.0 / jnp.sqrt(jnp.asarray(HD, q.dtype))
            scores = jnp.einsum('bqhd,bkhd->bhqk', q, k) * scale
            probs = jax.nn.softmax(scores, axis=-1)
            return jnp.einsum('bhqk,bkhd->bqhd', probs, v)
        key = jax.random.key(seed)
        ks = jax.random.split(key, 12)
        B, L = (2, 2048)
        s = 0.02
        inp = {'x': jax.random.normal(ks[0], (B, L, DIM), jnp.float32), 'context': jax.random.normal(ks[1], (B, 769, DIM), jnp.float32), 'q_w': jax.random.normal(ks[2], (DIM, DIM), jnp.float32) * s, 'q_b': jnp.zeros((DIM,), jnp.float32), 'k_w': jax.random.normal(ks[3], (DIM, DIM), jnp.float32) * s, 'k_b': jnp.zeros((DIM,), jnp.float32), 'v_w': jax.random.normal(ks[4], (DIM, DIM), jnp.float32) * s, 'v_b': jnp.zeros((DIM,), jnp.float32), 'k_img_w': jax.random.normal(ks[5], (DIM, DIM), jnp.float32) * s, 'k_img_b': jnp.zeros((DIM,), jnp.float32), 'v_img_w': jax.random.normal(ks[6], (DIM, DIM), jnp.float32) * s, 'v_img_b': jnp.zeros((DIM,), jnp.float32), 'o_w': jax.random.normal(ks[7], (DIM, DIM), jnp.float32) * s, 'o_b': jnp.zeros((DIM,), jnp.float32), 'norm_q_w': jnp.ones((DIM,), jnp.float32), 'norm_k_w': jnp.ones((DIM,), jnp.float32), 'norm_k_img_w': jnp.ones((DIM,), jnp.float32)}
        return inp
    _L0_xattn_all = _L0_xattn_setup()
    _L0_xattn_in = {k: v for k, v in _L0_xattn_all.items() if k in ('q_w', 'q_b', 'k_w', 'k_b', 'v_w', 'v_b', 'k_img_w', 'k_img_b', 'v_img_w', 'v_img_b', 'o_w', 'o_b', 'norm_q_w', 'norm_k_w', 'norm_k_img_w')}
    del _L0_xattn_all

    def _L0_ffn_setup():
        import jax, jax.numpy as jnp
        import numpy as np
        B, S, D = (4, 256, 512)
        H = 1024
        NE = 8
        TOPK = 2
        key = jax.random.key(seed)
        ks = jax.random.split(key, 9)
        s = lambda fan_in: 1.0 / np.sqrt(fan_in)
        return {'x': jax.random.normal(ks[0], (B, S, D), dtype=jnp.float32), 'W1': jax.random.normal(ks[1], (NE, D, H), dtype=jnp.float32) * s(D), 'b1': jnp.zeros((NE, H), dtype=jnp.float32), 'W2': jax.random.normal(ks[2], (NE, H, H), dtype=jnp.float32) * s(H), 'b2': jnp.zeros((NE, H), dtype=jnp.float32), 'W3': jax.random.normal(ks[3], (NE, H, D), dtype=jnp.float32) * s(H), 'b3': jnp.zeros((NE, D), dtype=jnp.float32), 'Wg': jax.random.normal(ks[4], (D, NE), dtype=jnp.float32) * s(D), 'bg': jnp.zeros((NE,), dtype=jnp.float32)}
    _L0_ffn_all = _L0_ffn_setup()
    _L0_ffn_in = {k: v for k, v in _L0_ffn_all.items() if k in ('W1', 'b1', 'W2', 'b2', 'W3', 'b3', 'Wg', 'bg')}
    del _L0_ffn_all
    return {'x': x, 'ctx_2048': ctx_2048, 'L0_xattn_q_w': _L0_xattn_in['q_w'], 'L0_xattn_q_b': _L0_xattn_in['q_b'], 'L0_xattn_k_w': _L0_xattn_in['k_w'], 'L0_xattn_k_b': _L0_xattn_in['k_b'], 'L0_xattn_v_w': _L0_xattn_in['v_w'], 'L0_xattn_v_b': _L0_xattn_in['v_b'], 'L0_xattn_k_img_w': _L0_xattn_in['k_img_w'], 'L0_xattn_k_img_b': _L0_xattn_in['k_img_b'], 'L0_xattn_v_img_w': _L0_xattn_in['v_img_w'], 'L0_xattn_v_img_b': _L0_xattn_in['v_img_b'], 'L0_xattn_o_w': _L0_xattn_in['o_w'], 'L0_xattn_o_b': _L0_xattn_in['o_b'], 'L0_xattn_norm_q_w': _L0_xattn_in['norm_q_w'], 'L0_xattn_norm_k_w': _L0_xattn_in['norm_k_w'], 'L0_xattn_norm_k_img_w': _L0_xattn_in['norm_k_img_w'], 'L0_ffn_W1': _L0_ffn_in['W1'], 'L0_ffn_b1': _L0_ffn_in['b1'], 'L0_ffn_W2': _L0_ffn_in['W2'], 'L0_ffn_b2': _L0_ffn_in['b2'], 'L0_ffn_W3': _L0_ffn_in['W3'], 'L0_ffn_b3': _L0_ffn_in['b3'], 'L0_ffn_Wg': _L0_ffn_in['Wg'], 'L0_ffn_bg': _L0_ffn_in['bg']}

def reference(x, ctx_2048, L0_xattn_q_w, L0_xattn_q_b, L0_xattn_k_w, L0_xattn_k_b, L0_xattn_v_w, L0_xattn_v_b, L0_xattn_k_img_w, L0_xattn_k_img_b, L0_xattn_v_img_w, L0_xattn_v_img_b, L0_xattn_o_w, L0_xattn_o_b, L0_xattn_norm_q_w, L0_xattn_norm_k_w, L0_xattn_norm_k_img_w, L0_ffn_W1, L0_ffn_b1, L0_ffn_W2, L0_ffn_b2, L0_ffn_W3, L0_ffn_b3, L0_ffn_Wg, L0_ffn_bg):
    import jax
    import jax.numpy as jnp

    def _L0_xattn_ref(x, context, q_w, q_b, k_w, k_b, v_w, v_b, k_img_w, k_img_b, v_img_w, v_img_b, o_w, o_b, norm_q_w, norm_k_w, norm_k_img_w):
        import jax, jax.numpy as jnp
        import numpy as np
        DIM = 512
        NH = 16
        HD = DIM // NH
        EPS = 1e-06
        IMG_LEN = 257

        def rms_norm(x, w, eps=EPS):
            xf = x.astype(jnp.float32)
            y = xf * jax.lax.rsqrt(jnp.mean(xf * xf, axis=-1, keepdims=True) + eps)
            return y.astype(x.dtype) * w

        def linear(x, w, b):
            return jnp.einsum('blc,oc->blo', x, w) + b

        def attention(q, k, v):
            scale = 1.0 / jnp.sqrt(jnp.asarray(HD, q.dtype))
            scores = jnp.einsum('bqhd,bkhd->bhqk', q, k) * scale
            probs = jax.nn.softmax(scores, axis=-1)
            return jnp.einsum('bhqk,bkhd->bqhd', probs, v)
        B, L, _ = x.shape
        ctx_img = context[:, :IMG_LEN]
        ctx_txt = context[:, IMG_LEN:]
        q = rms_norm(linear(x, q_w, q_b), norm_q_w).reshape(B, L, NH, HD)
        k = rms_norm(linear(ctx_txt, k_w, k_b), norm_k_w).reshape(B, -1, NH, HD)
        v = linear(ctx_txt, v_w, v_b).reshape(B, -1, NH, HD)
        k_img = rms_norm(linear(ctx_img, k_img_w, k_img_b), norm_k_img_w).reshape(B, -1, NH, HD)
        v_img = linear(ctx_img, v_img_w, v_img_b).reshape(B, -1, NH, HD)
        img_x = attention(q, k_img, v_img)
        txt_x = attention(q, k, v)
        out = (txt_x + img_x).reshape(B, L, DIM)
        return linear(out, o_w, o_b)

    def _L0_ffn_ref(x, W1, b1, W2, b2, W3, b3, Wg, bg):
        import jax, jax.numpy as jnp
        import numpy as np
        B, S, D = (4, 256, 512)
        H = 1024
        NE = 8
        TOPK = 2
        gate_logits = jnp.einsum('bsd,dn->bsn', x, Wg) + bg
        gate_weights = jax.nn.softmax(gate_logits, axis=-1)
        topv, topi = jax.lax.top_k(gate_weights, TOPK)
        h = jax.nn.gelu(jnp.einsum('bsd,ndh->nbsh', x, W1) + b1[:, None, None, :], approximate=False)
        h = jax.nn.gelu(jnp.einsum('nbsh,nhf->nbsf', h, W2) + b2[:, None, None, :], approximate=False)
        eo = jnp.einsum('nbsf,nfd->nbsd', h, W3) + b3[:, None, None, :]
        comb = jnp.sum(jax.nn.one_hot(topi, NE, dtype=x.dtype) * topv[..., None], axis=-2)
        out = jnp.einsum('nbsd,bsn->bsd', eo, comb)
        return out
    x = x + _L0_xattn_ref(_layernorm(x, axis=-1), ctx_2048, L0_xattn_q_w, L0_xattn_q_b, L0_xattn_k_w, L0_xattn_k_b, L0_xattn_v_w, L0_xattn_v_b, L0_xattn_k_img_w, L0_xattn_k_img_b, L0_xattn_v_img_w, L0_xattn_v_img_b, L0_xattn_o_w, L0_xattn_o_b, L0_xattn_norm_q_w, L0_xattn_norm_k_w, L0_xattn_norm_k_img_w)
    x = x + _L0_ffn_ref(_layernorm(x, axis=-1), L0_ffn_W1, L0_ffn_b1, L0_ffn_W2, L0_ffn_b2, L0_ffn_W3, L0_ffn_b3, L0_ffn_Wg, L0_ffn_bg)
    return x

_drawn_inputs = setup_inputs


def setup_inputs(seed=0):
    import zlib

    import numpy as np

    out = dict(_drawn_inputs(seed))
    spreads = {'L0_xattn_q_b': (0.0, 0.455),
     'L0_xattn_k_b': (0.0, 0.8),
     'L0_xattn_v_b': (0.0, 0.1),
     'L0_xattn_k_img_b': (0.0, 0.8),
     'L0_xattn_v_img_b': (0.0, 0.1),
     'L0_xattn_o_b': (0.0, 0.1),
     'L0_xattn_norm_q_w': (1.0, 0.6),
     'L0_xattn_norm_k_w': (1.0, 0.6),
     'L0_xattn_norm_k_img_w': (1.0, 0.6),
     'L0_ffn_b1': (0.0, 0.445),
     'L0_ffn_b2': (0.0, 0.302),
     'L0_ffn_b3': (0.0, 0.1),
     'L0_ffn_bg': (0.0, 0.1)}
    factors = {}
    for name, (base, spread) in spreads.items():
        noise = np.random.default_rng([zlib.crc32(name.encode()), seed]).standard_normal(out[name].shape)
        drawn = base * np.exp(spread * noise) if base else spread * noise
        out[name] = jnp.asarray(drawn.astype(out[name].dtype))
    for name, factor in factors.items():
        out[name] = (out[name] * factor).astype(out[name].dtype)
    return out
```

```python
from contextlib import ExitStack

import concourse.bass as bass
from concourse import mybir

F32 = mybir.dt.float32
F32R = mybir.dt.float32r
U32 = mybir.dt.uint32
I32 = mybir.dt.int32
ALU = mybir.AluOpType
ACT = mybir.ActivationFunctionType
AX = mybir.AxisListType

P = 128
B, L, D = 8, 112, 512
NC = D // P
NH, HD = 16, 32
IMG, KEYS = 257, 375
TXT = KEYS - IMG
IMGE = IMG + 1
KT = 3
TAIL = KEYS - 2 * P
TOK = L + KEYS
E, H = 8, 1024
T = B * L
BLOCK = 256
MAX_BLOCKS = (2 * T - E) // BLOCK + E
PIECE = 2048
PIECES = 8
LN_EPS, RMS_EPS = 1e-5, 1e-6
WQ, WKI, WK, WVI, WV, WO = range(6)
V_QB, V_KB, V_KIB, V_VB, V_VIB, V_NQ, V_NK, V_NKI = range(8)
SLOT = {"k0": 0, "k1": 1, "xT": 2, "o": 3, "k2": 4, "q": 5, "k3": 6, "v0": 7, "ms": 8, "v1": 9, "rb": 10, "v2": 11}
STAGE_AT = {1: ["k0"], 2: ["k1"], 3: ["xT"], 4: ["o"], 5: ["k2"], 6: ["q"], 7: ["k3"], 8: ["v0"],
            10: ["ms"], 11: ["v1"], 12: ["rb"], 13: ["v2"]}
CHUNKS = [range(0, 4), range(4, 8)] + [range(8 + 2 * i, 10 + 2 * i) for i in range(4)]
LAG = 2
FIRST, LAST, DONE = 0, B - 1, B


def tile_use(name, b):
    i = SLOT[name]
    short = i - (i > SLOT["o"])
    if isinstance(b, int) and b <= FIRST:
        g = (b + 1) * (len(SLOT) - 1) + short
        return g % 3, g // 3
    if isinstance(b, int) and b >= LAST:
        g = 12 * LAST + 10 + (b - LAST)
        return g % 3, g // 3
    return (10 + i) % 3, 4 * b + (10 + i) // 3


AFTER = 12 * LAST + 12
ROWS = (MAX_BLOCKS + 1) * BLOCK // P
ZERO_STORES = 2 * -(-ROWS // B)


def cross_attention_moe(nc, x, ctxT, ctx_last, wT, vecs, o_b, wg, bg, experts, b12, b3, out):
    with ExitStack() as ctx:
        def sb(name, shape, dt=F32):
            return ctx.enter_context(nc.sbuf_tensor(name, shape, dt))

        def psum(name, shape):
            return ctx.enter_context(nc.psum_tensor(name, shape, F32))

        def sem(name):
            return ctx.enter_context(nc.semaphore(name))

        slots_d = nc.dram_tensor("slots_d", ((MAX_BLOCKS + 1) * BLOCK, D), F32).ap()
        y_d = nc.dram_tensor("y_d", (MAX_BLOCKS * BLOCK, D), F32).ap()
        x1_d = nc.dram_tensor("x1_d", (B, L, D), F32).ap()
        vlast_d = nc.dram_tensor("vlast_d", (B, D), F32).ap()

        w2 = sb("w2", [P, 12 * PIECE], F32R)
        c2 = sb("c2", [P, 3000], F32R)
        scr = sb("scr", [P, 14768])
        xn2 = sb("xn2", [P, B, D])
        xb, xn, xr, x1 = sb("xb", [P, D]), sb("xn", [P, D]), sb("xr", [P, D]), sb("x1", [P, D])
        xs2 = sb("xs2", [P, 2, NC, L], F32R)
        qn = sb("qn", [P, 2, NC, L])
        a2 = sb("a2", [P, 2, NC, L], F32R)
        ident, ones = sb("ident", [P, P]), sb("ones", [P, P])
        upper, iota = sb("upper", [P, P]), sb("iota", [P, P])
        vec = sb("vec", [P, 8, NC])
        vbias, nq = sb("vbias", [P, NC]), sb("nq", [P, NC])
        obr = sb("obr", [P, D])
        wgs, bgr = sb("wgs", [P, NC, E]), sb("bgr", [P, E])
        b12s = sb("b12s", [P, E, 16])
        pidx, lneps, mhalf = sb("pidx", [P, 1]), sb("lneps", [P, 1]), sb("mhalf", [P, 4])
        st1, mv1, ve1, rs1 = sb("st1", [P, 6]), sb("mv1", [P, 2]), sb("ve1", [P, 1]), sb("rs1", [P, 1])
        st2, mv2, ve2, rs2 = sb("st2", [P, 6]), sb("mv2", [P, 2]), sb("ve2", [P, 1]), sb("rs2", [P, 1])
        msb, rr = sb("msb", [P, 4]), sb("rr", [P, 4])
        nmax, sums, rsum = sb("nmax", [P, 4, 2]), sb("sums", [P, 4, 2]), sb("rsum", [P, 4, 2])
        xlT = sb("xlT", [P, NC, B])
        xl2 = sb("xl2", [P, 2, NC, B], F32R)
        vlast = x1[0:B, :]

        off = [0]

        def part(n):
            off[0] += n
            return scr[:, off[0] - n:off[0]]

        kn = part(2 * NC * KEYS).rearrange("p (b c k) -> p b c k", b=2, c=NC)
        vn = part(2 * KT * D).rearrange("p (b t d) -> p b t d", b=2, t=KT)
        cr = part(NC * KEYS).rearrange("p (c k) -> p c k", c=NC)
        sq = part(NC * TOK).rearrange("p (c k) -> p c k", c=NC)
        ssum = part(512)
        diag = part(512)
        probs_at = off[0]
        probs = part(4 * KT * P).rearrange("p (s k) -> p s k", s=4)
        probT = part(8 * KT * L).rearrange("p (s t q) -> p s t q", s=8, t=KT)
        assert off[0] <= 14768
        raw_w = [scr[:, probs_at + i * PIECE:probs_at + (i + 1) * PIECE] for i in range(2)]

        wH = lambda m: w2[:, 2 * m * PIECE:(2 * m + 1) * PIECE]
        wL = lambda m: w2[:, (2 * m + 1) * PIECE:(2 * m + 2) * PIECE]
        wv = lambda m: (wH(m).rearrange("p (c o) -> p c o", c=NC), wL(m).rearrange("p (c o) -> p c o", c=NC))
        cH = c2[:, 0:1500].rearrange("p (c k) -> p c k", c=NC)
        cL = c2[:, 1500:3000].rearrange("p (c k) -> p c k", c=NC)

        lg, ex, gw = (scr[:, 64 * i:64 * i + 64].rearrange("p (b e) -> p b e", b=B) for i in range(3))
        mx, sm, rc = (scr[:, 192 + 8 * i:200 + 8 * i] for i in range(3))
        top = scr[:, 256:320].rearrange("p (b e) -> p b e", b=B)
        tif, sel1, sel2, msk, slotm, tmp1, tmp2 = (
            scr[:, 320 + 64 * i:384 + 64 * i].rearrange("p (b e) -> p b e", b=B) for i in range(7))
        pre = scr[:, 768:840].rearrange("p (b e) -> p b e", b=B + 1)
        nblk, ends, base = scr[:, 840:848], scr[:, 848:856], scr[:, 856:864]
        slotf = scr[:, 864:880].rearrange("p (c b) -> p c b", c=2)
        cmpb = scr[:, 896:896 + 16 * E].rearrange("p (j e) -> p j e", e=E)
        ebf = scr[:, 1024:1040]
        xt = scr[:, 1056:1056 + 2 * NC * L].rearrange("p (s c q) -> p s c q", s=2, c=NC)
        topi = sb("topi", [P, B, E], U32)
        slotu = sb("slotu", [P, 2, B], U32)
        topw = sb("topw", [P, 2, B])
        ebi = sb("ebi", [1, 16], I32)

        off[0] = 2048
        raw = [part(PIECE) for _ in range(4)]
        xs = part(2 * D).rearrange("p (t d) -> p t d", t=2)
        ys = part(2 * D).rearrange("p (t d) -> p t d", t=2)
        gel = part(4 * BLOCK).rearrange("p (s n) -> p s n", s=4)
        assert off[0] <= 14768
        EH = [w2[:, i * PIECE:(i + 1) * PIECE] for i in range(4)]
        EL = [w2[:, (4 + i) * PIECE:(5 + i) * PIECE] for i in range(4)]
        hH = [w2[:, (8 + 2 * i) * PIECE:(9 + 2 * i) * PIECE].rearrange("p (c n) -> p c n", c=8) for i in range(2)]
        hL = [w2[:, (9 + 2 * i) * PIECE:(10 + 2 * i) * PIECE].rearrange("p (c n) -> p c n", c=8) for i in range(2)]
        xTH = c2[:, 0:1024].rearrange("p (c n) -> p c n", c=NC)
        xTL = c2[:, 1024:2048].rearrange("p (c n) -> p c n", c=NC)
        b3s = xn2
        fin = [[scr[:, 2048 + (3 * s + i) * D:2048 + (3 * s + i + 1) * D] for i in range(3)] for s in range(4)]

        tiles = psum("tiles", [P, 3, 512])
        scores = psum("scores", [P, 2, 512])
        ptb = psum("ptb", [P, 2, 512])
        pvb = psum("pvb", [P, 512])
        hid = [tiles[:, 0, :], tiles[:, 1, :], tiles[:, 2, :], pvb[:, :]]
        xTb = scores
        yb = ptb

        S = {n: sem(n) for n in (
            "vec_in", "small_in", "aggr", "held", "experts_over", "wh_done", "wl_done", "xl_in", "xlh", "xll", "consts", "zeroed", "zero_stored",
            "vbias_done", "nq_done", "vlast_mm", "vlast_sb", "vlast_out",
            "x_in", "c_in", "ch_done", "cl_done", "xr_in", "xr_ob", "ln1_stats", "ln1_mv", "ln1_var", "ln1_rstd", "xn_done",
            "ln2_stats", "ln2_mv", "ln2_var", "ln2_rstd", "xn2_done", "xh_done", "xl_done",
            "squares", "sum_a", "sum_b", "r_done", "diag_done", "qk_done",
            "vrow_in", "s_ready", "max_done", "exp_done", "rsum_done", "p_ready", "t_ready", "pt_done",
            "pv_ready", "ah_done", "al_done", "x1_stored",
            "xt_done", "gate_ready", "route", "g_exp", "rank_ready", "slots_done", "scattered", "b3_in",
            "eh_done", "el_done", "y_piece", "hid_ready", "gel_done", "hh_done", "hl_done",
            "xs_in", "xT_ready", "xTh_done", "xTl_done", "y_sb", "y_out", "fin_a", "fin_b")}
        tile_ready = [sem(f"tile_ready{i}") for i in range(3)]
        tile_free = [sem(f"tile_free{i}") for i in range(3)]

        wraw_in = [sem(f"wraw_in{i}") for i in range(2)]
        raw_in = [sem(f"raw_in{i}") for i in range(4)]
        fin_in = [sem(f"fin_in{i}") for i in range(4)]
        x1_in = [sem(f"x1_in{i}") for i in range(4)]
        out_done = [sem(f"out_done{i}") for i in range(4)]

        def taken(eng, name, b):
            bank, cnt = tile_use(name, b)
            eng.wait_ge(tile_free[bank], cnt + 1)

        block = ctx.enter_context(nc.Block())

        def bodies(eng, body):
            body(-1, 1)
            body(FIRST, 0)
            with eng.Fori(0, (B - 2) // 2) as i:
                body(2 * i + 1, 1)
                body(2 * i + 2, 0)
            body(LAST, 1)
            body(DONE, 0)

        fixed = lambda b, v: isinstance(b, int) and b == v
        has_prep = lambda b: not (fixed(b, LAST) or fixed(b, DONE))
        has_tail = lambda b: not (fixed(b, -1) or fixed(b, FIRST))
        has_heads = lambda b: not (fixed(b, -1) or fixed(b, DONE))

        def split_ctx(act, n):
            act.wait_ge(S["c_in"], 16 * n)
            act.activation(cH, cr, ACT.Copy).then_inc(S["ch_done"], 1)

        @block.sync
        def _(sp):
            sp.dma_start(vec[:, :, :], vecs).then_inc(S["vec_in"], 16)
            order = (WKI, WK, WQ, WVI, WV, WO)
            for i, m in enumerate(order):
                if i >= 2:
                    sp.wait_ge(S["wh_done"], i - 1)
                    sp.wait_ge(S["wl_done"], i - 1)
                sp.dma_start(raw_w[i % 2], wT[m]).then_inc(wraw_in[i % 2], 16)
                if i == 1:
                    sp.dma_start(cr, ctxT[0]).then_inc(S["c_in"], 16)
                    sp.dma_start(xb[0:L, :], x[0]).then_inc(S["x_in"], 16)
                    sp.dma_start(xlT[:, :, :], ctx_last).then_inc(S["xl_in"], 16)
            sp.wait_ge(S["zeroed"], 1)
            zero = xn2[:, :, :].rearrange("p b d -> p (b d)")
            for dst in (slots_d, y_d):
                rows = dst.shape[0] // P
                flat = dst.rearrange("(p r) d -> p (r d)", r=rows)
                for r in range(0, rows, B):
                    n = min(B, rows - r) * D
                    sp.dma_start(flat[:, r * D:r * D + n], zero[:, 0:n]).then_inc(S["zero_stored"], 16)
            sp.wait_ge(S["vlast_sb"], 1)
            sp.dma_start(vlast_d, vlast).then_inc(S["vlast_out"], 16)
            sp.wait_ge(S["vlast_out"], 16)

            def body(b, p):
                if has_prep(b):
                    if not isinstance(b, int) or b < LAST - 1:
                        sp.wait_ge(S["ch_done"], b + 2)
                        sp.wait_ge(S["cl_done"], b + 2)
                        sp.dma_start(cr, ctxT[bass.ds(b + 2, 1)].rearrange("a p c k -> (a p) c k")).then_inc(S["c_in"], 16)
                        sp.wait_ge(S["xn_done"], b + 2)
                        sp.dma_start(xb[0:L, :], x[bass.ds(b + 2, 1)].rearrange("a p d -> (a p) d")).then_inc(S["x_in"], 16)
                if has_tail(b):
                    taken(sp, "o", b)
                    sp.dma_start(x1_d[bass.ds(b - 1, 1)].rearrange("a p d -> (a p) d"), x1[0:L, :]).then_inc(S["x1_stored"], 16)
                if has_heads(b):
                    sp.dma_start(xr[0:L, :], x[bass.ds(b, 1)].rearrange("a p d -> (a p) d")).then_inc(S["xr_in"], 16)
                if has_prep(b):
                    taken(sp, "v2", b)
                    sp.dma_start(vn[0:1, 1 - p, KT - 1, :], vlast_d[bass.ds(b + 1, 1), :]).then_inc(S["vrow_in"], 16)

            body(-1, 1)
            body(FIRST, 0)
            with sp.Fori(0, (B - 2) // 2 - 1) as i:
                body(2 * i + 1, 1)
                body(2 * i + 2, 0)
            body(LAST - 2, 1)
            body(LAST - 1, 0)
            body(LAST, 1)
            body(DONE, 0)

            sp.wait_ge(S["scattered"], 16 * 2 * B)
            sp.dma_start(b3s[:, :, :].rearrange("p e d -> p (e d)"), b3.rearrange("(a e) d -> a (e d)", a=1).partition_broadcast(P)).then_inc(S["b3_in"], 16)
            sp.dma_start(xs, slots_d[0:BLOCK, :].rearrange("(t p) d -> p t d", p=P)).then_inc(S["xs_in"], 16)
            e0 = sp.value_load(ebi[0:1, 0:1], min_val=0, max_val=E - 1)
            for pc in range(PIECES):
                if pc >= 4:
                    sp.wait_ge(S["eh_done"], pc - 3)
                    sp.wait_ge(S["el_done"], pc - 3)
                sp.dma_start(raw[pc % 4], experts[bass.ds(e0, 1), pc].rearrange("a p n -> (a p) n")).then_inc(raw_in[pc % 4], 16)
            used = sp.value_load(ebi[0:1, MAX_BLOCKS + 1:MAX_BLOCKS + 2], min_val=1, max_val=MAX_BLOCKS)
            with sp.Fori(0, MAX_BLOCKS) as j:
                with sp.If(j < used):
                    e = sp.value_load(ebi[0:1, bass.ds(j + 1, 1)], min_val=0, max_val=E - 1)
                    sp.wait_ge(S["xT_ready"], j + 1)
                    sp.dma_start(xs, slots_d[bass.ds((j + 1) * BLOCK, BLOCK), :].rearrange("(t p) d -> p t d", p=P)).then_inc(S["xs_in"], 16)
                    for pc in range(PIECES):
                        sp.wait_ge(S["eh_done"], PIECES * j + pc + 5)
                        sp.wait_ge(S["el_done"], PIECES * j + pc + 5)
                        sp.dma_start(raw[pc % 4], experts[bass.ds(e, 1), pc].rearrange("a p n -> (a p) n")).then_inc(raw_in[pc % 4], 16)
                    sp.wait_ge(S["y_sb"], j + 1)
                    sp.dma_start(y_d[bass.ds(j * BLOCK, BLOCK), :].rearrange("(t p) d -> p t d", p=P), ys).then_inc(S["y_out"], 16)
                    sp.wait_ge(S["y_out"], 16 * (j + 1))
                    sp.sem_inc(S["held"], 1)
            for slot in range(4):
                sp.wait_ge(raw_in[slot], 16 * 2 * (used + 1))
                sp.sem_inc(S["held"], 1)
            for name, value in (("xs_in", 16 * (used + 1)), ("xT_ready", used + 1), ("el_done", PIECES * used + 4),
                                ("hl_done", 16 * used + 4), ("y_out", 16 * used)):
                sp.wait_ge(S[name], value)
                sp.sem_inc(S["held"], 1)
            sp.sem_inc(S["experts_over"], 1)
            for b in range(B):
                if b >= 4:
                    sp.wait_ge(S["fin_b"], b - 3)
                    sp.wait_ge(out_done[b % 4], 16)
                sp.dma_start(fin[b % 4][0][0:L, :], x1_d[b]).then_inc(x1_in[b % 4], 16)
                if b >= 2:
                    sp.wait_ge(S["fin_b"], b - 1)
                    sp.dma_start(out[b - 2], fin[(b - 2) % 4][0][0:L, :]).then_inc(out_done[(b - 2) % 4], 16)
            for b in (B - 2, B - 1):
                sp.wait_ge(S["fin_b"], b + 1)
                sp.dma_start(out[b], fin[b % 4][0][0:L, :]).then_inc(out_done[b % 4], 16)
            for i in range(4):
                sp.wait_ge(out_done[i], 16 * B // 4)

        @block.gpsimd
        def _(pool):
            pool.memset(xn2[:, :, :], 0.0).then_inc(S["zeroed"], 1)
            pool.iota(iota[:, :], [[1, P]], base=0, channel_multiplier=0, allow_small_or_imprecise_dtypes=True)
            pool.iota(pidx[:, :], [[1, 1]], base=0, channel_multiplier=1, allow_small_or_imprecise_dtypes=True)
            pool.memset(ones[:, :], 1.0)
            pool.memset(mhalf[:, :], -0.5)
            pool.memset(lneps[:, :], LN_EPS)
            pool.memset(ssum[:, TOK:512], 0.0)
            pool.dma_start(obr[:, :], o_b.rearrange("(a d) -> a d", a=1).partition_broadcast(P)).then_inc(S["small_in"], 16)
            pool.dma_start(wgs[:, :, :], wg).then_inc(S["small_in"], 16)
            pool.dma_start(bgr[:, :], bg.rearrange("(a d) -> a d", a=1).partition_broadcast(P)).then_inc(S["small_in"], 16)
            pool.dma_start(b12s[:, :, :], b12).then_inc(S["small_in"], 16)
            pool.memset(rs1[:, :], 0.0).then_inc(S["consts"], 1)
            pool.wait_ge(S["consts"], 1)

            def rstd(b_count, mv, ve, rs, tag):
                pool.wait_ge(S[tag + "_mv"], b_count)
                pool.tensor_tensor(ve[0:L, :], mv[0:L, 1:2], lneps[0:L, :], ALU.add).then_inc(S[tag + "_var"], 1)
                pool.wait_ge(S[tag + "_var"], b_count)
                pool.tensor_tensor(rs[0:L, :], ve[0:L, :], mhalf[0:L, 0:1], ALU.pow).then_inc(S[tag + "_rstd"], 1)

            def body(b, p):
                if has_prep(b):
                    rstd(b + 2, mv1, ve1, rs1, "ln1")
                if has_tail(b):
                    rstd(b, mv2, ve2, rs2, "ln2")
                if has_heads(b):
                    if fixed(b, FIRST):
                        pool.wait_ge(S["small_in"], 64)
                    pool.wait_ge(S["xr_in"], 16 * (b + 1))
                    pool.tensor_tensor(xr[0:L, :], xr[0:L, :], obr[0:L, :], ALU.add).then_inc(S["xr_ob"], 1)
                if has_prep(b):
                    n = b + 1
                    pool.wait_ge(S["squares"], n + 1)
                    pool.tensor_tensor(sq[:, 0:2, :], sq[:, 0:2, :], sq[:, 2:4, :], ALU.add).then_inc(S["sum_a"], 1)
                    pool.wait_ge(S["sum_a"], n + 1)
                    pool.tensor_tensor(ssum[:, 0:TOK], sq[:, 0, :], sq[:, 1, :], ALU.add).then_inc(S["sum_b"], 1)
                    taken(pool, "ms", b)
                    pool.tensor_tensor(rr[:, :], msb[:, :], mhalf[:, :], ALU.pow).then_inc(S["r_done"], 1)
                    pool.wait_ge(S["r_done"], n + 1)
                    if fixed(b, -1):
                        pool.wait_ge(S["nq_done"], 3)
                    pool.tensor_tensor(diag.rearrange("p (t n) -> p t n", t=4), ident[:, :].unsqueeze(1).to_broadcast([P, 4, P]),
                                       rr[:, :].unsqueeze(2).to_broadcast([P, 4, P]), ALU.mult).then_inc(S["diag_done"], 1)

            bodies(pool, body)

            pool.wait_ge(S["slots_done"], 1)
            pool.wait_ge(S["zero_stored"], 16 * ZERO_STORES)
            for c in range(2):
                for b in range(B):
                    pool.indirect_dma_start(
                        out=slots_d, out_offset=bass.IndirectOffsetOnAxis(ap=slotu[0:L, c, b:b + 1], axis=0),
                        in_=xn2[0:L, b, :], in_offset=None).then_inc(S["scattered"], 16)
            pool.wait_ge(S["experts_over"], 1)
            for b in range(B):
                if b >= 4:
                    pool.wait_ge(S["fin_b"], b - 3)
                for c in range(2):
                    pool.indirect_dma_start(
                        out=fin[b % 4][1 + c][0:L, :], out_offset=None, in_=y_d,
                        in_offset=bass.IndirectOffsetOnAxis(ap=slotu[0:L, c, b:b + 1], axis=0)).then_inc(fin_in[b % 4], 16)

        @block.scalar
        def _(act):
            for i, m in enumerate((WKI, WK, WQ, WVI, WV, WO)):
                act.wait_ge(wraw_in[i % 2], 16 * (i // 2 + 1))
                act.activation(wH(m), raw_w[i % 2], ACT.Copy).then_inc(S["wh_done"], 1)
                if i == 1:
                    split_ctx(act, 1)
                    act.wait_ge(S["xl_in"], 16)
                    act.activation(xl2[:, 0, :, :], xlT[:, :, :], ACT.Copy).then_inc(S["xlh"], 1)

            def stage(name, b, p):
                n = b + 1
                if name == "o":
                    return
                bank, cnt = tile_use(name, b)
                if name == "xT":
                    act.wait_ge(tile_ready[bank], cnt + 1)
                    act.activation(xs2[:, 0, :, :], tiles[:, bank, 0:NC * L].rearrange("p (c q) -> p c q", c=NC),
                                   ACT.Copy).then_inc(S["xh_done"], 1)
                if name in ("v0", "v1", "v2"):
                    t = int(name[1])
                    rows = P if t < 2 else TAIL
                    act.wait_ge(tile_ready[bank], cnt + 1)
                    act.activation(vn[0:rows, 1 - p, t, :], tiles[0:rows, bank, :], ACT.Copy).then_inc(tile_free[bank], 1)
                if name == "k3":
                    taken(act, "k3", b)
                    act.activation(sq[:, :, L:TOK], kn[:, 1 - p, :, :], ACT.Square)
                    act.activation(sq[:, :, 0:L], qn[:, 1 - p, :, :], ACT.Square).then_inc(S["squares"], 1)

            def weigh(b, p, h):
                s = h % 4
                act.wait_ge(S["max_done"], NH * b + h + 1)
                act.activation(probs[0:L, s, 0:IMG], scores[0:L, h % 2, 0:IMG], ACT.Exp,
                               bias=nmax[0:L, s, 0:1], accum_out=sums[0:L, s, 0:1])
                act.activation(probs[0:L, s, IMG:KEYS], scores[0:L, h % 2, IMG:KEYS], ACT.Exp,
                               bias=nmax[0:L, s, 1:2], accum_out=sums[0:L, s, 1:2]).then_inc(S["exp_done"], 1)

            def take_transposed(b, h):
                act.wait_ge(S["t_ready"], NH * b + h + 1)
                if not (fixed(b, 0) and h < 8):
                    act.wait_ge(S["pv_ready"], NC * b + h // 4 - 1)
                act.activation(probT[:, h % 8, :, :], ptb[:, h % 2, 0:KT * L].rearrange("p (t q) -> p t q", t=KT),
                               ACT.Copy).then_inc(S["pt_done"], 1)

            def take_attended(b, g):
                act.wait_ge(S["pv_ready"], NC * b + g + 1)
                act.activation(a2[:, 0, g, :], pvb[:, 0:L], ACT.Identity, bias=vbias[:, g:g + 1]).then_inc(S["ah_done"], 1)

            def body(b, p):
                for h in range(NH):
                    if has_heads(b):
                        weigh(b, p, h)
                    if h < LAG:
                        if has_tail(b):
                            take_transposed(b - 1, NH - LAG + h)
                    elif has_heads(b):
                        take_transposed(b, h - LAG)
                    if h == 2 and has_tail(b):
                        take_attended(b - 1, 3)
                    if h in (6, 10, 14) and has_heads(b):
                        take_attended(b, (h - 6) // 4)
                    if h == 0 and has_prep(b) and not fixed(b, -1):
                        split_ctx(act, b + 2)
                    for name in STAGE_AT.get(h, ()):
                        if has_prep(b):
                            stage(name, b, p)
                    if fixed(b, -1) and h == 15:
                        act.wait_ge(S["vlast_mm"], 1)
                        act.activation(vlast, pvb[0:B, :], ACT.Copy).then_inc(S["vlast_sb"], 1)
                        act.wait_ge(S["vbias_done"], 1)

            bodies(act, body)

            for b in range(B):
                g = AFTER + b
                act.wait_ge(tile_ready[g % 3], g // 3 + 1)
                if b >= 2:
                    act.wait_ge(S["gate_ready"], b - 1)
                act.activation(xt[:, b % 2, :, :], tiles[:, g % 3, 0:NC * L].rearrange("p (c q) -> p c q", c=NC),
                               ACT.Copy).then_inc(tile_free[g % 3], 1)
            act.wait_ge(S["route"], 3)
            act.activation(ex[0:L], lg[0:L], ACT.Exp).then_inc(S["g_exp"], 1)

            act.wait_ge(S["slots_done"], 1)
            e = act.value_load(ebi[0:1, 0:1], min_val=0, max_val=E - 1)

            def convert(use, slot):
                act.wait_ge(raw_in[slot], 16 * (use + 1))
                act.activation(EH[slot], raw[slot], ACT.Copy).then_inc(S["eh_done"], 1)

            def split_input(j):
                act.wait_ge(S["xT_ready"], j + 1)
                act.activation(xTH, xTb[:, :, :].rearrange("p b (c n) -> p (b c) n", n=BLOCK), ACT.Copy).then_inc(S["xTh_done"], 1)

            act.sem_inc(S["gel_done"], 4)
            for pc in range(4):
                convert(0, pc)
            split_input(0)
            act.wait_ge(S["small_in"], 64)
            used = act.value_load(ebi[0:1, MAX_BLOCKS + 1:MAX_BLOCKS + 2], min_val=1, max_val=MAX_BLOCKS)
            with act.Fori(0, MAX_BLOCKS) as j:
                with act.If(j < used):
                    e = act.value_load(ebi[0:1, bass.ds(j, 1)], min_val=0, max_val=E - 1)
                    for pc in range(PIECES):
                        if pc < 6:
                            for m in CHUNKS[pc]:
                                act.wait_ge(S["hid_ready"], 16 * j + m + 1)
                                act.wait_ge(S["hl_done"], 16 * j + m + 1)
                                act.activation(gel[:, m % 4, :], hid[m % 4][:, 0:BLOCK], ACT.Gelu,
                                               bias=b12s[:, bass.ds(e, 1), m:m + 1].rearrange("p a o -> p (a o)")
                                               ).then_inc(S["gel_done"], 1)
                        if pc < 6:
                            act.wait_ge(S["hid_ready"], 16 * j + CHUNKS[pc][-1] + 1)
                        else:
                            act.wait_ge(S["y_piece"], 2 * j + pc - 5)
                        convert(2 * j + pc // 4 + 1, pc % 4)
                        if pc == 5:
                            split_input(j + 1)

        @block.vector
        def _(dve):
            dve.wait_ge(S["consts"], 1)
            dve.tensor_scalar(ident[:, :], iota[:, :], pidx[:, 0:1], None, ALU.is_equal).then_inc(S["nq_done"], 1)
            dve.tensor_scalar(upper[:, :], iota[:, :], pidx[:, 0:1], None, ALU.is_gt).then_inc(S["nq_done"], 1)
            dve.wait_ge(S["vec_in"], 16)
            dve.tensor_scalar(nq[:, :], vec[:, V_NQ, :], float(HD) ** -0.5, None, ALU.mult).then_inc(S["nq_done"], 1)
            dve.tensor_tensor(vbias[:, :], vec[:, V_VB, :], vec[:, V_VIB, :], ALU.add).then_inc(S["vbias_done"], 1)

            def split_ctx_low(n):
                dve.wait_ge(S["ch_done"], n)
                dve.tensor_tensor(cL, cr, cH.bitcast(F32), ALU.subtract).then_inc(S["cl_done"], 1)

            def ln_stats(count, src, st, mv, tag):
                dve.bn_stats(st[0:L, :], src[0:L, :]).then_inc(S[tag + "_stats"], 1)
                dve.wait_ge(S[tag + "_stats"], count)
                dve.sem_inc(S["aggr"], 1)
                dve.bn_aggr(mv[0:L, :], st[0:L, :]).then_inc(S[tag + "_mv"], 1)

            def ln_apply(count, dst, src, mv, rs, tag, done):
                dve.wait_ge(S[tag + "_rstd"], count)
                dve.tensor_scalar(dst, src[0:L, :], mv[0:L, 0:1], rs[0:L, 0:1], ALU.subtract, ALU.mult).then_inc(S[done], 1)

            for i, m in enumerate((WKI, WK, WQ, WVI, WV, WO)):
                dve.wait_ge(S["wh_done"], i + 1)
                dve.tensor_tensor(wL(m), raw_w[i % 2], wH(m).bitcast(F32), ALU.subtract).then_inc(S["wl_done"], 1)
                if i == 1:
                    split_ctx_low(1)
                    dve.wait_ge(S["xlh"], 1)
                    dve.tensor_tensor(xl2[:, 1, :, :], xlT[:, :, :], xl2[:, 0, :, :].bitcast(F32), ALU.subtract).then_inc(S["xll"], 1)
            dve.wait_ge(S["wl_done"], 6)
            dve.memset(probs[:, :, KEYS:KT * P], 0.0)

            def stage(name, b, p):
                n = b + 1
                bank, cnt = tile_use(name, b)
                tile = tiles[:, bank, :]
                if name in ("v0", "v1", "v2"):
                    return
                if name == "o":
                    dve.wait_ge(tile_ready[bank], cnt + 1)
                    dve.wait_ge(S["xr_ob"], b)
                    dve.tensor_tensor(x1[0:L, :], tile[0:L, :], xr[0:L, :], ALU.add).then_inc(tile_free[bank], 1)
                    dve.wait_ge(tile_free[bank], cnt + 1)
                    ln_stats(b, x1, st2, mv2, "ln2")
                    return
                if name == "rb":
                    dve.wait_ge(tile_ready[bank], cnt + 1)
                    for c in range(NC):
                        q, k = qn[:, 1 - p, c, :], kn[:, 1 - p, c, :]
                        dve.scalar_tensor_tensor(q, q, nq[:, c:c + 1], tile[:, 0:L], ALU.mult, ALU.mult)
                        dve.scalar_tensor_tensor(k[:, 0:IMG], k[:, 0:IMG], vec[:, V_NKI, c:c + 1], tile[:, L:L + IMG], ALU.mult, ALU.mult)
                        last = dve.scalar_tensor_tensor(k[:, IMG:KEYS], k[:, IMG:KEYS], vec[:, V_NK, c:c + 1], tile[:, L + IMG:TOK],
                                                        ALU.mult, ALU.mult)
                    last.then_inc(tile_free[bank], 1)
                    return
                if name == "xT":
                    dve.wait_ge(S["xh_done"], n + 1)
                    dve.tensor_tensor(xs2[:, 1, :, :], tile[:, 0:NC * L].rearrange("p (c q) -> p c q", c=NC),
                                      xs2[:, 0, :, :].bitcast(F32), ALU.subtract).then_inc(tile_free[bank], 1)
                    return
                dve.wait_ge(tile_ready[bank], cnt + 1)
                if name == "q":
                    dve.tensor_tensor(qn[:, 1 - p, :, :], tile[:, 0:NC * L].rearrange("p (c q) -> p c q", c=NC),
                                      vec[:, V_QB, :].unsqueeze(2).to_broadcast([P, NC, L]), ALU.add).then_inc(tile_free[bank], 1)
                elif name == "ms":
                    dve.tensor_scalar(msb[:, :], tile[:, 0:4], 1.0 / D, RMS_EPS, ALU.mult, ALU.add).then_inc(tile_free[bank], 1)
                else:
                    c = int(name[1])
                    dve.tensor_scalar(kn[:, 1 - p, c, 0:IMG], tile[:, 0:IMG], vec[:, V_KIB, c:c + 1], None, ALU.add)
                    dve.tensor_scalar(kn[:, 1 - p, c, IMG:KEYS], tile[:, IMGE:IMGE + TXT], vec[:, V_KB, c:c + 1], None,
                                      ALU.add).then_inc(tile_free[bank], 1)

            def maxima(b, h):
                dve.wait_ge(S["s_ready"], NH * b + h + 1)
                dve.tensor_reduce(nmax[0:L, h % 4, 0:1], scores[0:L, h % 2, 0:IMG], AX.X, ALU.max, negate=True)
                dve.tensor_reduce(nmax[0:L, h % 4, 1:2], scores[0:L, h % 2, IMG:KEYS], AX.X, ALU.max, negate=True).then_inc(S["max_done"], 1)

            def normalise(b, h):
                s = h % 4
                dve.wait_ge(S["exp_done"], NH * b + h + 1)
                dve.reciprocal(rsum[0:L, s, :], sums[0:L, s, :]).then_inc(S["rsum_done"], 1)
                dve.wait_ge(S["rsum_done"], NH * b + h + 1)
                dve.tensor_scalar(probs[0:L, s, 0:IMG], probs[0:L, s, 0:IMG], rsum[0:L, s, 0:1], None, ALU.mult)
                dve.tensor_scalar(probs[0:L, s, IMG:KEYS], probs[0:L, s, IMG:KEYS], rsum[0:L, s, 1:2], None,
                                  ALU.mult).then_inc(S["p_ready"], 1)

            def attended_low(b, g):
                dve.wait_ge(S["ah_done"], NC * b + g + 1)
                dve.scalar_tensor_tensor(a2[:, 1, g, :], pvb[:, 0:L], vbias[:, g:g + 1], a2[:, 0, g, :].bitcast(F32),
                                         ALU.add, ALU.subtract).then_inc(S["al_done"], 1)

            def body(b, p):
                for h in range(NH):
                    if has_heads(b):
                        maxima(b, h)
                    if h == 0:
                        if has_tail(b):
                            normalise(b - 1, NH - 1)
                    elif has_heads(b):
                        normalise(b, h - 1)
                    if h == 2 and has_tail(b):
                        attended_low(b - 1, 3)
                    if h in (6, 10, 14) and has_heads(b):
                        attended_low(b, (h - 6) // 4)
                    if h == 0 and has_prep(b):
                        if not fixed(b, -1):
                            split_ctx_low(b + 2)
                        dve.wait_ge(S["x_in"], 16 * (b + 2))
                        ln_stats(b + 2, xb, st1, mv1, "ln1")
                    if h == 2 and has_prep(b):
                        ln_apply(b + 2, xn[0:L, :], xb, mv1, rs1, "ln1", "xn_done")
                    for name in STAGE_AT.get(h, ()):
                        if (name == "o" and has_tail(b)) or (name != "o" and has_prep(b)):
                            stage(name, b, p)
                    if h == 7 and has_tail(b):
                        if fixed(b, LAST) or fixed(b, DONE):
                            dst = xn2[0:L, b - 1, :]
                        else:
                            dst = xn2[0:L, bass.ds(b - 1, 1), :].rearrange("p a d -> p (a d)")
                            dve.wait_ge(S["zero_stored"], 16 * ZERO_STORES)
                        ln_apply(b, dst, x1, mv2, rs2, "ln2", "xn2_done")
                    if h == NH - 1 and has_tail(b):
                        dve.wait_ge(S["x1_stored"], 16 * b)

            bodies(dve, body)

            steps = [0]

            def after(ins):
                steps[0] += 1
                ins.then_inc(S["route"], 1)
                dve.wait_ge(S["route"], steps[0])

            bc = lambda ap, shape: ap.to_broadcast(shape)
            full = [L, B, E]
            dve.wait_ge(S["gate_ready"], B)
            dve.wait_ge(S["small_in"], 64)
            after(dve.tensor_tensor(lg[0:L], scores[0:L, 0, 0:B * E].rearrange("p (b e) -> p b e", b=B),
                                    bc(bgr[0:L, :].unsqueeze(1), full), ALU.add))
            after(dve.tensor_reduce(mx[0:L, :], lg[0:L], AX.X, ALU.max))
            after(dve.tensor_tensor(lg[0:L], lg[0:L], bc(mx[0:L, :].unsqueeze(2), full), ALU.subtract))
            dve.wait_ge(S["g_exp"], 1)
            after(dve.tensor_reduce(sm[0:L, :], ex[0:L], AX.X, ALU.add))
            after(dve.reciprocal(rc[0:L, :], sm[0:L, :]))
            after(dve.tensor_tensor(gw[0:L], ex[0:L], bc(rc[0:L, :].unsqueeze(2), full), ALU.mult))
            for b in range(B):
                last = dve.max(top[0:L, b, :], gw[0:L, b, :])
            after(last)
            for b in range(B):
                last = dve.max_index(topi[0:L, b, :], top[0:L, b, :], gw[0:L, b, :])
            after(last)
            after(dve.tensor_copy(tif[0:L], topi[0:L, :, :]))
            dve.tensor_copy(topw[0:L, 0, :], top[0:L, :, 0])
            dve.tensor_copy(topw[0:L, 1, :], top[0:L, :, 1])
            number = bc(iota[0:L, 0:E].unsqueeze(1), full)
            dve.tensor_tensor(sel1[0:L], bc(tif[0:L, :, 0:1], full), number, ALU.is_equal)
            after(dve.tensor_tensor(sel2[0:L], bc(tif[0:L, :, 1:2], full), number, ALU.is_equal))
            after(dve.tensor_tensor(msk[0:L], sel1[0:L], sel2[0:L], ALU.add))
            mask_made = steps[0]
            dve.wait_ge(S["rank_ready"], 1)
            after(dve.memset(pre[:, 0, :], 0.0))
            totals = ptb[:, 0, 0:B * E].rearrange("p (b e) -> p b e", b=B)
            for b in range(B):
                after(dve.tensor_tensor(pre[:, b + 1, :], totals[:, b, :], pre[:, b, :], ALU.add))
            count = pre[:, B, :]
            after(dve.tensor_scalar(nblk, count, 0.0, None, ALU.is_gt))
            for k in range(1, -(-T // BLOCK)):
                after(dve.scalar_tensor_tensor(nblk, count, float(k * BLOCK), nblk, ALU.is_gt, ALU.add))
            after(dve.tensor_copy(ends, nblk))
            for k in range(1, E):
                after(dve.tensor_tensor(ends[:, k:k + 1], ends[:, k:k + 1], ends[:, k - 1:k], ALU.add))
            after(dve.tensor_tensor(base, ends, nblk, ALU.subtract))
            after(dve.tensor_scalar(base, base, float(BLOCK), None, ALU.mult))
            after(dve.tensor_tensor(slotm[0:L], scores[0:L, 1, 0:B * E].rearrange("p (b e) -> p b e", b=B), pre[0:L, 0:B, :], ALU.add))
            after(dve.tensor_tensor(slotm[0:L], slotm[0:L], bc(base[0:L, :].unsqueeze(1), full), ALU.add))
            dve.tensor_tensor(tmp1[0:L], slotm[0:L], sel1[0:L], ALU.mult)
            after(dve.tensor_tensor(tmp2[0:L], slotm[0:L], sel2[0:L], ALU.mult))
            dve.tensor_reduce(slotf[0:L, 0, :], tmp1[0:L], AX.X, ALU.add)
            after(dve.tensor_reduce(slotf[0:L, 1, :], tmp2[0:L], AX.X, ALU.add))
            dve.tensor_copy(slotu[0:L, :, :], slotf[0:L])
            after(dve.tensor_tensor(cmpb[0:1], bc(ends[0:1, :].unsqueeze(1), [1, 16, E]), bc(iota[0:1, 0:16].unsqueeze(2), [1, 16, E]), ALU.is_le))
            after(dve.tensor_reduce(ebf[0:1, :], cmpb[0:1], AX.X, ALU.add))
            after(dve.tensor_scalar(ebf[0:1, :], ebf[0:1, :], float(E - 1), None, ALU.min))
            after(dve.tensor_copy(ebf[0:1, MAX_BLOCKS + 1:MAX_BLOCKS + 2], ends[0:1, E - 1:E]))
            dve.tensor_copy(ebi[0:1, :], ebf[0:1, :]).then_inc(S["slots_done"], 1)

            def convert(q, slot):
                dve.wait_ge(S["eh_done"], q + 1)
                dve.tensor_tensor(EL[slot], raw[slot], EH[slot].bitcast(F32), ALU.subtract).then_inc(S["el_done"], 1)

            def split_input(j):
                dve.wait_ge(S["xTh_done"], j + 1)
                dve.tensor_tensor(xTL, xTb[:, :, :].rearrange("p b (c n) -> p (b c) n", n=BLOCK), xTH.bitcast(F32), ALU.subtract).then_inc(S["xTl_done"], 1)

            dve.memset(gel[:, :, :], 0.0).then_inc(S["hl_done"], 4)
            for pc in range(4):
                convert(pc, pc)
            split_input(0)
            dve.wait_ge(S["b3_in"], 16)
            used = dve.value_load(ebi[0:1, MAX_BLOCKS + 1:MAX_BLOCKS + 2], min_val=1, max_val=MAX_BLOCKS)
            with dve.Fori(0, MAX_BLOCKS) as j:
                with dve.If(j < used):
                    e = dve.value_load(ebi[0:1, bass.ds(j, 1)], min_val=0, max_val=E - 1)
                    for pc in range(PIECES):
                        if pc < 6:
                            for m in CHUNKS[pc]:
                                lay, c = m // 8, m % 8
                                dve.wait_ge(S["gel_done"], 16 * j + m + 5)
                                dve.tensor_copy(hH[lay][:, c, :], gel[:, m % 4, :]).then_inc(S["hh_done"], 1)
                                dve.wait_ge(S["hh_done"], 16 * j + m + 1)
                                dve.tensor_tensor(hL[lay][:, c, :], gel[:, m % 4, :], hH[lay][:, c, :].bitcast(F32),
                                                  ALU.subtract).then_inc(S["hl_done"], 1)
                        convert(PIECES * j + pc + 4, pc % 4)
                        if pc == 5:
                            split_input(j + 1)
                    dve.wait_ge(S["y_piece"], 2 * j + 2)
                    dve.tensor_tensor(ys, yb[:, :, :], b3s[:, bass.ds(e, 1), :].to_broadcast([P, 2, D]), ALU.add).then_inc(S["y_sb"], 1)

            for b in range(B):
                dve.wait_ge(fin_in[b % 4], 32 * (b // 4 + 1))
                dve.wait_ge(x1_in[b % 4], 16 * (b // 4 + 1))
                f = fin[b % 4]
                dve.scalar_tensor_tensor(f[0][0:L, :], f[1][0:L, :], topw[0:L, 0, b:b + 1], f[0][0:L, :], ALU.mult, ALU.add).then_inc(S["fin_a"], 1)
                dve.wait_ge(S["fin_a"], b + 1)
                dve.scalar_tensor_tensor(f[0][0:L, :], f[2][0:L, :], topw[0:L, 1, b:b + 1], f[0][0:L, :], ALU.mult, ALU.add).then_inc(S["fin_b"], 1)

        @block.tensor
        def _(pe):
            def three(out, wh, wl, xh, xl, start, stop):
                pe.matmul(out, wh, xh, start=start, stop=False)
                pe.matmul(out, wh, xl, start=False, stop=False)
                return pe.matmul(out, wl, xh, start=False, stop=stop)

            def stage(name, b, p):
                n = b + 1
                bank, cnt = tile_use(name, b)
                tile = tiles[:, bank, :]
                pe.wait_ge(tile_free[bank], cnt)
                if name == "xT":
                    pe.wait_ge(S["xn_done"], n + 1)
                    for c in range(NC):
                        mm = pe.transpose(tile[:, c * L:(c + 1) * L], xn[0:L, c * P:(c + 1) * P], ident[0:L, 0:L])
                elif name == "q":
                    taken(pe, "xT", b)
                    wh, wl = wv(WQ)
                    for o in range(NC):
                        for c in range(NC):
                            mm = three(tile[:, o * L:(o + 1) * L], wh[:, c, o * P:(o + 1) * P], wl[:, c, o * P:(o + 1) * P],
                                       xs2[:, 0, c, :], xs2[:, 1, c, :], c == 0, c == NC - 1)
                elif name[0] == "k":
                    o = int(name[1])
                    pe.wait_ge(S["cl_done"], n + 1)
                    for m, lo, cols, at in ((WKI, 0, IMGE, 0), (WK, IMG, TXT, IMGE)):
                        wh, wl = wv(m)
                        for c in range(NC):
                            mm = three(tile[:, at:at + cols], wh[:, c, o * P:(o + 1) * P], wl[:, c, o * P:(o + 1) * P],
                                       cH[:, c, lo:lo + cols], cL[:, c, lo:lo + cols], c == 0, c == NC - 1)
                elif name[0] == "v":
                    t = int(name[1])
                    rows = P if t < 2 else TAIL
                    wh, wl = wv(WVI if t < 2 else WV)
                    for c in range(NC):
                        ch, cl = cH[:, c, t * P:t * P + rows], cL[:, c, t * P:t * P + rows]
                        pe.matmul(tile[0:rows, :], ch, wh[:, c, :], start=(c == 0), stop=False)
                        pe.matmul(tile[0:rows, :], ch, wl[:, c, :], start=False, stop=False)
                        mm = pe.matmul(tile[0:rows, :], cl, wh[:, c, :], start=False, stop=(c == NC - 1))
                elif name == "ms":
                    pe.wait_ge(S["sum_b"], n + 1)
                    for t in range(4):
                        mm = pe.matmul(tile[:, t:t + 1], ssum[:, t * P:(t + 1) * P], ones[:, 0:1], start=True, stop=True)
                elif name == "rb":
                    pe.wait_ge(S["diag_done"], n + 1)
                    mm = pe.matmul(tile[:, :], ones[:, :], diag, start=True, stop=True)
                elif name == "o":
                    pe.wait_ge(S["al_done"], NC * b)
                    wh, wl = wv(WO)
                    for c in range(NC):
                        pe.matmul(tile[0:L, :], a2[:, 0, c, :], wh[:, c, :], start=(c == 0), stop=False)
                        pe.matmul(tile[0:L, :], a2[:, 0, c, :], wl[:, c, :], start=False, stop=False)
                        mm = pe.matmul(tile[0:L, :], a2[:, 1, c, :], wh[:, c, :], start=False, stop=(c == NC - 1))
                mm.then_inc(tile_ready[bank], 1)

            def score(b, p, h):
                if h == 0:
                    taken(pe, "rb", b - 1)
                if not (fixed(b, 0) and h < 2):
                    pe.wait_ge(S["exp_done"], NH * b + h - 1)
                r = slice(HD * (h % 4), HD * (h % 4) + HD)
                pe.matmul(scores[0:L, h % 2, 0:KEYS], qn[r, p, h // 4, :], kn[r, p, h // 4, :], start=True, stop=True).then_inc(S["s_ready"], 1)

            def transpose(b, h):
                pe.wait_ge(S["p_ready"], NH * b + h + 1)
                if not (fixed(b, 0) and h < 2):
                    pe.wait_ge(S["pt_done"], NH * b + h - 1)
                for t in range(KT):
                    mm = pe.transpose(ptb[:, h % 2, t * L:(t + 1) * L], probs[0:L, h % 4, t * P:(t + 1) * P], ident[0:L, 0:L])
                mm.then_inc(S["t_ready"], 1)

            def attend(b, p, g):
                pe.wait_ge(S["pt_done"], NH * b + 4 * g + 4)
                if g == 0:
                    pe.wait_ge(S["vrow_in"], 16 * (b + 1))
                pe.wait_ge(S["al_done"], NC * b + g)
                for t in range(KT):
                    rows = P if t < 2 else TAIL
                    for i in range(4):
                        h = 4 * g + i
                        mm = pe.matmul(pvb[HD * i:HD * i + HD, 0:L], vn[0:rows, p, t, HD * h:HD * h + HD],
                                       probT[0:rows, h % 8, t, :], start=(t == 0), stop=(t == KT - 1))
                mm.then_inc(S["pv_ready"], 1)

            def body(b, p):
                if fixed(b, -1):
                    pe.wait_ge(S["nq_done"], 3)
                    pe.wait_ge(S["wl_done"], 2)
                for h in range(NH):
                    if has_heads(b):
                        score(b, p, h)
                    for name in STAGE_AT.get(h, ()):
                        if (name == "o" and has_tail(b)) or (name != "o" and has_prep(b)):
                            if fixed(b, -1) and name == "q":
                                pe.wait_ge(S["wl_done"], 3)
                            if fixed(b, -1) and name == "v0":
                                pe.wait_ge(S["wl_done"], 5)
                            stage(name, b, p)
                    if h < LAG:
                        if has_tail(b):
                            transpose(b - 1, NH - LAG + h)
                    elif has_heads(b):
                        transpose(b, h - LAG)
                    if h == 2 and has_tail(b):
                        attend(b - 1, 1 - p, 3)
                    if h in (6, 10, 14) and has_heads(b):
                        attend(b, p, (h - 6) // 4)
                if fixed(b, -1):
                    pe.wait_ge(S["xll"], 1)
                    pe.wait_ge(S["wl_done"], 6)
                    wh, wl = wv(WVI)
                    for c in range(NC):
                        pe.matmul(pvb[0:B, :], xl2[:, 0, c, :], wh[:, c, :], start=(c == 0), stop=False)
                        pe.matmul(pvb[0:B, :], xl2[:, 0, c, :], wl[:, c, :], start=False, stop=False)
                        mm = pe.matmul(pvb[0:B, :], xl2[:, 1, c, :], wh[:, c, :], start=False, stop=(c == NC - 1))
                    mm.then_inc(S["vlast_mm"], 1)
                    pe.wait_ge(S["vlast_sb"], 1)

            bodies(pe, body)

            pe.wait_ge(S["small_in"], 64)

            def gate_in(b):
                g = AFTER + b
                pe.wait_ge(S["xn2_done"], b + 1)
                pe.wait_ge(tile_free[g % 3], g // 3)
                for c in range(NC):
                    mm = pe.transpose(tiles[:, g % 3, c * L:(c + 1) * L], xn2[0:L, b, c * P:(c + 1) * P], ident[0:L, 0:L])
                mm.then_inc(tile_ready[g % 3], 1)

            def gate(b):
                g = AFTER + b
                pe.wait_ge(tile_free[g % 3], g // 3 + 1)
                for c in range(NC):
                    mm = pe.matmul(scores[0:L, 0, b * E:(b + 1) * E], xt[:, b % 2, c, :], wgs[:, c, :], start=(c == 0), stop=(c == NC - 1))
                mm.then_inc(S["gate_ready"], 1)

            gate_in(0)
            for b in range(B):
                if b + 1 < B:
                    gate_in(b + 1)
                gate(b)
            pe.wait_ge(S["route"], 11)
            pe.matmul(scores[0:L, 1, 0:B * E], upper[0:L, 0:L], msk[0:L].rearrange("p b e -> p (b e)"), start=True, stop=True)
            pe.matmul(ptb[:, 0, 0:B * E], ones[0:L, :], msk[0:L].rearrange("p b e -> p (b e)"), start=True, stop=True).then_inc(S["rank_ready"], 1)

            pe.wait_ge(S["slots_done"], 1)

            def turn(j):
                pe.wait_ge(S["xs_in"], 16 * (j + 1))
                pe.wait_ge(S["xTl_done"], j)
                for c in range(NC):
                    for t in range(2):
                        mm = pe.transpose(xTb[:, c // 2, (c % 2) * BLOCK + t * P:(c % 2) * BLOCK + (t + 1) * P],
                                          xs[:, t, c * P:(c + 1) * P], ident[:, :])
                mm.then_inc(S["xT_ready"], 1)

            turn(0)
            used = pe.value_load(ebi[0:1, MAX_BLOCKS + 1:MAX_BLOCKS + 2], min_val=1, max_val=MAX_BLOCKS)
            with pe.Fori(0, MAX_BLOCKS) as j:
                with pe.If(j < used):
                    pe.wait_ge(S["xTl_done"], j + 1)
                    for pc in range(PIECES):
                        pe.wait_ge(S["el_done"], PIECES * j + pc + 1)
                        slot = pc % 4
                        if pc < 6:
                            width, K, per = (512, NC, 4) if pc < 2 else (256, 8, 2)
                            wh = EH[slot].rearrange("p (c n) -> p c n", n=width)
                            wl = EL[slot].rearrange("p (c n) -> p c n", n=width)
                            vh, vl = (xTH, xTL) if pc < 2 else (hH[0], hL[0])
                            for i in range(per):
                                m = 4 * pc + i if pc < 2 else 8 + 2 * (pc - 2) + i
                                pe.wait_ge(S["gel_done"], 16 * j + m + 1)
                                for c in range(K):
                                    if pc == 2 and i == 0:
                                        pe.wait_ge(S["hl_done"], 16 * j + c + 5)
                                    mm = three(hid[m % 4][:, 0:BLOCK], wh[:, c, i * P:(i + 1) * P], wl[:, c, i * P:(i + 1) * P],
                                               vh[:, c, :], vl[:, c, :], c == 0, c == K - 1)
                                mm.then_inc(S["hid_ready"], 1)
                        else:
                            if pc == 6:
                                turn(j + 1)
                            wh = EH[slot].rearrange("p (c n) -> p c n", n=D)
                            wl = EL[slot].rearrange("p (c n) -> p c n", n=D)
                            for i in range(4):
                                f = 4 * (pc - 6) + i
                                pe.wait_ge(S["hl_done"], 16 * j + 8 + f + 5)
                                for t in range(2):
                                    h_hi, h_lo = hH[1][:, f, t * P:(t + 1) * P], hL[1][:, f, t * P:(t + 1) * P]
                                    pe.matmul(yb[:, t, :], h_hi, wh[:, i, :], start=(f == 0), stop=False)
                                    pe.matmul(yb[:, t, :], h_hi, wl[:, i, :], start=False, stop=False)
                                    mm = pe.matmul(yb[:, t, :], h_lo, wh[:, i, :], start=False, stop=(f == 7))
                            mm.then_inc(S["y_piece"], 1)


def kernel(**inputs):
    import numpy as _np
    import concourse.bacc as _bacc
    from concourse import mybir as _mybir
    from concourse.bass_utils import run_bass_kernel_spmd as _run

    nc = _bacc.Bacc("TRN2", target_bir_lowering=False, num_devices=1)
    a = {k: _np.asarray(v) for k, v in inputs.items()}

    def col(v):
        return v.reshape(NC, P).T

    def wt(w):
        return w.T.reshape(NC, P, D).transpose(1, 0, 2).reshape(P, NC * D)

    names = [a["L0_xattn_" + n] for n in ("q_w", "k_img_w", "k_w", "v_img_w", "v_w", "o_w")]
    vecs = [a["L0_xattn_" + n] for n in ("q_b", "k_b", "k_img_b", "v_b", "v_img_b", "norm_q_w", "norm_k_w", "norm_k_img_w")]
    ctx = a["ctx_2048"]
    W1 = a["L0_ffn_W1"].reshape(E, NC, P, 2, 512).transpose(0, 3, 2, 1, 4).reshape(E, 2, P, PIECE)
    W2 = a["L0_ffn_W2"].reshape(E, 8, P, 4, 256).transpose(0, 3, 2, 1, 4).reshape(E, 4, P, PIECE)
    W3 = a["L0_ffn_W3"].reshape(E, 2, 4, P, D).transpose(0, 1, 3, 2, 4).reshape(E, 2, P, PIECE)
    b1, b2 = (a["L0_ffn_" + n].reshape(E, 8, P).transpose(2, 0, 1) for n in ("b1", "b2"))
    ins = [
        a["x"],
        ctx.reshape(B, KEYS, NC, P).transpose(0, 3, 2, 1),
        ctx[:, IMG - 1].reshape(B, NC, P).transpose(2, 1, 0),
        _np.stack([wt(w) for w in names]),
        _np.stack([col(v) for v in vecs], axis=1),
        a["L0_xattn_o_b"],
        a["L0_ffn_Wg"].reshape(NC, P, E).transpose(1, 0, 2),
        a["L0_ffn_bg"],
        _np.concatenate([W1, W2, W3], axis=1),
        _np.concatenate([b1, b2], axis=2),
        a["L0_ffn_b3"],
    ]
    arrays, args = {}, []
    for i, v in enumerate(ins):
        v = _np.ascontiguousarray(v)
        arrays[f"in_{i}_dram"] = v
        args.append(nc.dram_tensor(f"in_{i}_dram", v.shape, _mybir.dt.from_np(v.dtype), kind="ExternalInput").ap())
    args.append(nc.dram_tensor("out_0_dram", (B, L, D), _mybir.dt.float32, kind="ExternalOutput").ap())
    cross_attention_moe(nc, *args)
    r = _run(nc, [arrays], core_ids=[0])
    return r.results[0]["out_0_dram"]
```

```python
from contextlib import ExitStack

import concourse.bass as bass
from concourse import mybir

F32 = mybir.dt.float32
F32R = mybir.dt.float32r
U32 = mybir.dt.uint32
I32 = mybir.dt.int32
ALU = mybir.AluOpType
ACT = mybir.ActivationFunctionType
AX = mybir.AxisListType

P = 128
B, L, D = 8, 112, 512
NC = D // P
NH, HD = 16, 32
IMG, KEYS = 257, 375
TXT = KEYS - IMG
IMGE = IMG + 1
KT = 3
TAIL = KEYS - 2 * P
TOK = L + KEYS
E, H = 8, 1024
T = B * L
BLOCK = 256
MAX_BLOCKS = (2 * T - E) // BLOCK + E
PIECE = 2048
PIECES = 8
LN_EPS, RMS_EPS = 1e-5, 1e-6
WQ, WKI, WK, WVI, WV, WO = range(6)
V_QB, V_KB, V_KIB, V_VB, V_VIB, V_NQ, V_NK, V_NKI = range(8)
SLOT = {n: i for i, n in enumerate(("v2", "k0", "o", "xT", "k1", "qt", "k2", "q", "kt", "kx", "k3", "v0", "ms", "v1", "rb"))}
FILL = {0: [("v2", 0, 2)], 1: [("v2", 2, 4)], 2: [("k0", 0, 4)], 3: [("o", 0, 2)], 4: [("o", 2, 4), ("xT", 0, 1)],
        5: [("k1", 0, 4)], 6: [("qt", 0, 2)], 7: [("qt", 2, 4)], 8: [("k2", 0, 4)], 9: [("q", 0, 1), ("kt", 0, 2)],
        10: [("kt", 2, 4)], 11: [("kx", 0, 1), ("k3", 0, 4)], 12: [("v0", 0, 2)], 13: [("v0", 2, 4), ("ms", 0, 1)],
        14: [("v1", 0, 1), ("rb", 0, 1), ("v1", 1, 2)], 15: [("v1", 2, 4)]}
GROUPS = {n: 1 if n in ("xT", "q", "kx", "ms", "rb") else 4 for n in SLOT}
STAGE_AT = {h: [n for n, lo, hi in f if hi == GROUPS[n]] for h, f in FILL.items()}
CHUNKS = [range(0, 4), range(4, 8)] + [range(8 + 2 * i, 10 + 2 * i) for i in range(4)]
KEYS_AT = {15: (1, 0), 0: (2, -1), 1: (3, -1)}
LAG = 2
FIRST, LAST, DONE = 0, B - 1, B


def tile_use(name, b):
    i = SLOT[name]
    before_o = i - (i > SLOT["o"])
    if isinstance(b, int) and b < FIRST:
        g = before_o - 1
    elif isinstance(b, int) and b == FIRST:
        g = len(SLOT) - 2 + before_o
    elif isinstance(b, int) and b >= LAST:
        g = 15 * LAST + 12 + {"v2": 0, "o": b - LAST + 1}[name]
    else:
        return i % 3, 5 * b + 4 + i // 3
    return g % 3, g // 3


AFTER = 15 * LAST + 15
PARTS = (slice(0, 2 * P), slice(2 * P, KEYS))
ROWS = (MAX_BLOCKS + 1) * BLOCK // P
ZERO_STORES = 2 * -(-ROWS // B)


def cross_attention_moe(nc, x, ctxT, ctx_last, wT, vecs, o_b, wg, bg, experts, b12, b3, out):
    with ExitStack() as ctx:
        def sb(name, shape, dt=F32):
            return ctx.enter_context(nc.sbuf_tensor(name, shape, dt))

        def psum(name, shape):
            return ctx.enter_context(nc.psum_tensor(name, shape, F32))

        def sem(name):
            return ctx.enter_context(nc.semaphore(name))

        slots_d = nc.dram_tensor("slots_d", ((MAX_BLOCKS + 1) * BLOCK, D), F32).ap()
        y_d = nc.dram_tensor("y_d", (MAX_BLOCKS * BLOCK, D), F32).ap()
        x1_d = nc.dram_tensor("x1_d", (B, L, D), F32).ap()
        vlast_d = nc.dram_tensor("vlast_d", (B, D), F32).ap()

        w2 = sb("w2", [P, 12 * PIECE], F32R)
        c2 = sb("c2", [P, 3000], F32R)
        scr = sb("scr", [P, 14768])
        xn2 = sb("xn2", [P, B, D])
        xb, xn, xr, x1 = sb("xb", [P, D]), sb("xn", [P, D]), sb("xr", [P, D]), sb("x1", [P, D])
        xs2 = sb("xs2", [P, 2, NC, L], F32R)
        qn = sb("qn", [P, 2, NC, L])
        a2 = sb("a2", [P, 2, NC, L], F32R)
        ident, ones = sb("ident", [P, P]), sb("ones", [P, P])
        upper, iota = sb("upper", [P, P]), sb("iota", [P, P])
        vec = sb("vec", [P, 8, NC])
        vbias, nq = sb("vbias", [P, NC]), sb("nq", [P, NC])
        obr = sb("obr", [P, D])
        wgs, bgr = sb("wgs", [P, NC, E]), sb("bgr", [P, E])
        b12s = sb("b12s", [P, E, 16])
        pidx, lneps, mhalf = sb("pidx", [P, 1]), sb("lneps", [P, 1]), sb("mhalf", [P, 4])
        st1, mv1, ve1, rs1 = sb("st1", [P, 6]), sb("mv1", [P, 2]), sb("ve1", [P, 1]), sb("rs1", [P, 1])
        st2, mv2, ve2, rs2 = sb("st2", [P, 6]), sb("mv2", [P, 2]), sb("ve2", [P, 1]), sb("rs2", [P, 1])
        msb, rr = sb("msb", [P, 4]), sb("rr", [P, 4])
        nmax, sums, rsum = sb("nmax", [P, 4, 2]), sb("sums", [P, 4, 2]), sb("rsum", [P, 4, 2])
        xlT = sb("xlT", [P, NC, B])
        xl2 = sb("xl2", [P, 2, NC, B], F32R)
        vlast = x1[0:B, :]

        off = [0]

        def part(n):
            off[0] += n
            return scr[:, off[0] - n:off[0]]

        kn = part(2 * NC * KEYS).rearrange("p (b c k) -> p b c k", b=2, c=NC)
        vn = part(2 * KT * D).rearrange("p (b t d) -> p b t d", b=2, t=KT)
        cr = part(NC * KEYS).rearrange("p (c k) -> p c k", c=NC)
        sq = part(NC * TOK).rearrange("p (c k) -> p c k", c=NC)
        qz = part(2 * 4 * L).rearrange("p (c j q) -> p c j q", c=2, j=4)
        sqf = sq.rearrange("p c k -> p (c k)")
        ssum = sqf[:, 0:512]
        diag = sqf[:, 2 * TOK:2 * TOK + 512]
        probs_at = off[0]
        probs = part(4 * KT * P).rearrange("p (s k) -> p s k", s=4)
        probT = part(8 * KT * L).rearrange("p (s t q) -> p s t q", s=8, t=KT)
        assert off[0] <= 14768
        raw_w = [scr[:, probs_at + i * PIECE:probs_at + (i + 1) * PIECE] for i in range(2)]

        wH = lambda m: w2[:, 2 * m * PIECE:(2 * m + 1) * PIECE]
        wL = lambda m: w2[:, (2 * m + 1) * PIECE:(2 * m + 2) * PIECE]
        wv = lambda m: (wH(m).rearrange("p (c o) -> p c o", c=NC), wL(m).rearrange("p (c o) -> p c o", c=NC))
        cH = c2[:, 0:1500].rearrange("p (c k) -> p c k", c=NC)
        cL = c2[:, 1500:3000].rearrange("p (c k) -> p c k", c=NC)

        lg, ex, gw = (scr[:, 64 * i:64 * i + 64].rearrange("p (b e) -> p b e", b=B) for i in range(3))
        mx, sm, rc = (scr[:, 192 + 8 * i:200 + 8 * i] for i in range(3))
        top = scr[:, 256:320].rearrange("p (b e) -> p b e", b=B)
        tif, sel1, sel2, msk, slotm, tmp1, tmp2 = (
            scr[:, 320 + 64 * i:384 + 64 * i].rearrange("p (b e) -> p b e", b=B) for i in range(7))
        pre = scr[:, 768:840].rearrange("p (b e) -> p b e", b=B + 1)
        nblk, ends, base = scr[:, 840:848], scr[:, 848:856], scr[:, 856:864]
        slotf = scr[:, 864:880].rearrange("p (c b) -> p c b", c=2)
        cmpb = scr[:, 896:896 + 16 * E].rearrange("p (j e) -> p j e", e=E)
        ebf = scr[:, 1024:1040]
        xt = scr[:, 1056:1056 + 2 * NC * L].rearrange("p (s c q) -> p s c q", s=2, c=NC)
        topi = sb("topi", [P, B, E], U32)
        slotu = sb("slotu", [P, 2, B], U32)
        topw = sb("topw", [P, 2, B])
        rows_of = sb("rows_of", [P, 4])
        ebi = sb("ebi", [1, 16], I32)

        off[0] = 2048
        raw = [part(PIECE) for _ in range(4)]
        xs = part(2 * D).rearrange("p (t d) -> p t d", t=2)
        ys = part(2 * D).rearrange("p (t d) -> p t d", t=2)
        gel = part(4 * BLOCK).rearrange("p (s n) -> p s n", s=4)
        assert off[0] <= 14768
        EH = [w2[:, i * PIECE:(i + 1) * PIECE] for i in range(4)]
        EL = [w2[:, (4 + i) * PIECE:(5 + i) * PIECE] for i in range(4)]
        hH = [w2[:, (8 + 2 * i) * PIECE:(9 + 2 * i) * PIECE].rearrange("p (c n) -> p c n", c=8) for i in range(2)]
        hL = [w2[:, (9 + 2 * i) * PIECE:(10 + 2 * i) * PIECE].rearrange("p (c n) -> p c n", c=8) for i in range(2)]
        xTH = c2[:, 0:1024].rearrange("p (c n) -> p c n", c=NC)
        xTL = c2[:, 1024:2048].rearrange("p (c n) -> p c n", c=NC)
        b3s = xn2
        fin = [[scr[:, 2048 + (3 * s + i) * D:2048 + (3 * s + i + 1) * D] for i in range(3)] for s in range(4)]

        tiles = psum("tiles", [P, 3, 512])
        scores = psum("scores", [P, 2, 512])
        ptb = psum("ptb", [P, 2, 512])
        pvb = psum("pvb", [P, 512])
        hid = [tiles[:, 0, :], tiles[:, 1, :], tiles[:, 2, :], pvb[:, :]]
        xTb = scores
        yb = ptb

        S = {n: sem(n) for n in (
            "vec_in", "small_in", "aggr", "rows_done", "held", "experts_over", "wh_done", "wl_done", "xl_in", "xlh", "xll", "consts", "zeroed", "zero_stored",
            "vbias_done", "nq_done", "vlast_mm", "vlast_sb", "vlast_out",
            "x_in", "c_in", "ch_done", "cl_done", "xr_in", "xr_ob", "ln1_stats", "ln1_mv", "ln1_var", "ln1_rstd", "xn_done",
            "ln2_stats", "ln2_mv", "ln2_var", "ln2_rstd", "xn2_done", "xh_done", "xl_done",
            "squares", "sum_a", "sum_b", "r_done", "diag_done", "q_done", "k_done", "qz_done",
            "vrow_in", "s_ready", "max_done", "exp_done", "rsum_done", "p_ready", "t_ready", "pt_done",
            "pv_ready", "ah_done", "al_done", "x1_stored",
            "xt_done", "gate_ready", "route", "g_exp", "rank_ready", "slots_done", "scattered", "b3_in",
            "eh_done", "el_done", "y_piece", "hid_ready", "gel_done", "hh_done", "hl_done",
            "xs_in", "xT_ready", "xTh_done", "xTl_done", "y_sb", "y_out", "fin_a", "fin_b")}
        tile_ready = [sem(f"tile_ready{i}") for i in range(3)]
        tile_free = [sem(f"tile_free{i}") for i in range(3)]

        wraw_in = [sem(f"wraw_in{i}") for i in range(2)]
        raw_in = [sem(f"raw_in{i}") for i in range(4)]
        fin_in = [sem(f"fin_in{i}") for i in range(4)]
        x1_in = [sem(f"x1_in{i}") for i in range(4)]
        out_done = [sem(f"out_done{i}") for i in range(4)]

        def taken(eng, name, b):
            bank, cnt = tile_use(name, b)
            eng.wait_ge(tile_free[bank], cnt + 1)

        block = ctx.enter_context(nc.Block())

        def bodies(eng, body):
            body(-1, 1)
            body(FIRST, 0)
            with eng.Fori(0, (B - 2) // 2) as i:
                body(2 * i + 1, 1)
                body(2 * i + 2, 0)
            body(LAST, 1)
            body(DONE, 0)

        fixed = lambda b, v: isinstance(b, int) and b == v
        has_prep = lambda b: not (fixed(b, LAST) or fixed(b, DONE))
        has_tail = lambda b: not (fixed(b, -1) or fixed(b, FIRST))
        has_heads = lambda b: not (fixed(b, -1) or fixed(b, DONE))
        has = lambda name, b: {"o": has_tail, "v2": has_heads}.get(name, has_prep)(b)

        def split_ctx(act, n, i):
            act.wait_ge(S["c_in"], 16 * n)
            act.activation(cH[:, :, PARTS[i]], cr[:, :, PARTS[i]], ACT.Copy).then_inc(S["ch_done"], 1)

        @block.sync
        def _(sp):
            sp.dma_start(vec[:, :, :], vecs).then_inc(S["vec_in"], 16)
            order = (WKI, WQ, WK, WVI, WV, WO)
            for i, m in enumerate(order):
                if i >= 2:
                    sp.wait_ge(S["wh_done"], i - 1)
                    sp.wait_ge(S["wl_done"], i - 1)
                sp.dma_start(raw_w[i % 2], wT[m]).then_inc(wraw_in[i % 2], 16)
                if i == 0:
                    sp.dma_start(cr, ctxT[0]).then_inc(S["c_in"], 16)
                if i == 1:
                    sp.dma_start(xb[0:L, :], x[0]).then_inc(S["x_in"], 16)
                    sp.dma_start(xlT[:, :, :], ctx_last).then_inc(S["xl_in"], 16)
            sp.wait_ge(S["zeroed"], 1)
            zero = xn2[:, :, :].rearrange("p b d -> p (b d)")
            for dst in (slots_d, y_d):
                rows = dst.shape[0] // P
                flat = dst.rearrange("(p r) d -> p (r d)", r=rows)
                for r in range(0, rows, B):
                    n = min(B, rows - r) * D
                    sp.dma_start(flat[:, r * D:r * D + n], zero[:, 0:n]).then_inc(S["zero_stored"], 16)

            def body(b, p):
                if has_prep(b):
                    if not isinstance(b, int) or b < LAST - 1:
                        sp.wait_ge(S["ch_done"], 2 * (b + 2))
                        sp.wait_ge(S["cl_done"], 2 * (b + 2))
                        sp.dma_start(cr, ctxT[bass.ds(b + 2, 1)].rearrange("a p c k -> (a p) c k")).then_inc(S["c_in"], 16)
                        sp.wait_ge(S["xn_done"], b + 2)
                        sp.dma_start(xb[0:L, :], x[bass.ds(b + 2, 1)].rearrange("a p d -> (a p) d")).then_inc(S["x_in"], 16)
                if fixed(b, -1):
                    sp.wait_ge(S["vlast_sb"], 1)
                    sp.dma_start(vlast_d, vlast).then_inc(S["vlast_out"], 16)
                    sp.wait_ge(S["vlast_out"], 16)
                if has_heads(b):
                    taken(sp, "v2", b)
                    sp.dma_start(vn[0:1, p, KT - 1, :], vlast_d[bass.ds(b, 1), :]).then_inc(S["vrow_in"], 16)
                if has_tail(b):
                    taken(sp, "o", b)
                    sp.dma_start(x1_d[bass.ds(b - 1, 1)].rearrange("a p d -> (a p) d"), x1[0:L, :]).then_inc(S["x1_stored"], 16)
                if has_heads(b):
                    sp.dma_start(xr[0:L, :], x[bass.ds(b, 1)].rearrange("a p d -> (a p) d")).then_inc(S["xr_in"], 16)

            body(-1, 1)
            body(FIRST, 0)
            with sp.Fori(0, (B - 2) // 2 - 1) as i:
                body(2 * i + 1, 1)
                body(2 * i + 2, 0)
            body(LAST - 2, 1)
            body(LAST - 1, 0)
            body(LAST, 1)
            body(DONE, 0)

            sp.wait_ge(S["scattered"], 16 * 2 * B)
            sp.dma_start(b3s[:, :, :].rearrange("p e d -> p (e d)"), b3.rearrange("(a e) d -> a (e d)", a=1).partition_broadcast(P)).then_inc(S["b3_in"], 16)
            sp.dma_start(xs, slots_d[0:BLOCK, :].rearrange("(t p) d -> p t d", p=P)).then_inc(S["xs_in"], 16)
            e0 = sp.value_load(ebi[0:1, 0:1], min_val=0, max_val=E - 1)
            for pc in range(PIECES):
                if pc >= 4:
                    sp.wait_ge(S["eh_done"], pc - 3)
                    sp.wait_ge(S["el_done"], pc - 3)
                sp.dma_start(raw[pc % 4], experts[bass.ds(e0, 1), pc].rearrange("a p n -> (a p) n")).then_inc(raw_in[pc % 4], 16)
            used = sp.value_load(ebi[0:1, MAX_BLOCKS + 1:MAX_BLOCKS + 2], min_val=1, max_val=MAX_BLOCKS)
            with sp.Fori(0, MAX_BLOCKS) as j:
                with sp.If(j < used):
                    e = sp.value_load(ebi[0:1, bass.ds(j + 1, 1)], min_val=0, max_val=E - 1)
                    sp.wait_ge(S["xT_ready"], j + 1)
                    sp.dma_start(xs, slots_d[bass.ds((j + 1) * BLOCK, BLOCK), :].rearrange("(t p) d -> p t d", p=P)).then_inc(S["xs_in"], 16)
                    for pc in range(PIECES):
                        sp.wait_ge(S["eh_done"], PIECES * j + pc + 5)
                        sp.wait_ge(S["el_done"], PIECES * j + pc + 5)
                        sp.dma_start(raw[pc % 4], experts[bass.ds(e, 1), pc].rearrange("a p n -> (a p) n")).then_inc(raw_in[pc % 4], 16)
                    sp.wait_ge(S["y_sb"], j + 1)
                    sp.dma_start(y_d[bass.ds(j * BLOCK, BLOCK), :].rearrange("(t p) d -> p t d", p=P), ys).then_inc(S["y_out"], 16)
                    sp.wait_ge(S["y_out"], 16 * (j + 1))
                    sp.sem_inc(S["held"], 1)
            for slot in range(4):
                sp.wait_ge(raw_in[slot], 16 * 2 * (used + 1))
                sp.sem_inc(S["held"], 1)
            for name, value in (("xs_in", 16 * (used + 1)), ("xT_ready", used + 1), ("el_done", PIECES * used + 4),
                                ("hl_done", 16 * used + 4), ("y_out", 16 * used)):
                sp.wait_ge(S[name], value)
                sp.sem_inc(S["held"], 1)
            sp.sem_inc(S["experts_over"], 1)
            for b in range(B):
                if b >= 4:
                    sp.wait_ge(S["fin_b"], b - 3)
                    sp.wait_ge(out_done[b % 4], 16)
                sp.dma_start(fin[b % 4][0][0:L, :], x1_d[b]).then_inc(x1_in[b % 4], 16)
                if b >= 2:
                    sp.wait_ge(S["fin_b"], b - 1)
                    sp.dma_start(out[b - 2], fin[(b - 2) % 4][0][0:L, :]).then_inc(out_done[(b - 2) % 4], 16)
            for b in (B - 2, B - 1):
                sp.wait_ge(S["fin_b"], b + 1)
                sp.dma_start(out[b], fin[b % 4][0][0:L, :]).then_inc(out_done[b % 4], 16)
            for i in range(4):
                sp.wait_ge(out_done[i], 16 * B // 4)

        @block.gpsimd
        def _(pool):
            pool.memset(xn2[:, :, :], 0.0).then_inc(S["zeroed"], 1)
            pool.iota(iota[:, :], [[1, P]], base=0, channel_multiplier=0, allow_small_or_imprecise_dtypes=True)
            pool.iota(pidx[:, :], [[1, 1]], base=0, channel_multiplier=1, allow_small_or_imprecise_dtypes=True)
            pool.memset(ones[:, :], 1.0)
            pool.memset(mhalf[:, :], -0.5)
            pool.memset(lneps[:, :], LN_EPS)
            pool.dma_start(obr[:, :], o_b.rearrange("(a d) -> a d", a=1).partition_broadcast(P)).then_inc(S["small_in"], 16)
            pool.dma_start(wgs[:, :, :], wg).then_inc(S["small_in"], 16)
            pool.dma_start(bgr[:, :], bg.rearrange("(a d) -> a d", a=1).partition_broadcast(P)).then_inc(S["small_in"], 16)
            pool.dma_start(b12s[:, :, :], b12).then_inc(S["small_in"], 16)
            pool.memset(rs1[:, :], 0.0).then_inc(S["consts"], 1)
            pool.wait_ge(S["consts"], 1)

            def rstd(b_count, mv, ve, rs, tag):
                pool.wait_ge(S[tag + "_mv"], b_count)
                pool.tensor_tensor(ve[0:L, :], mv[0:L, 1:2], lneps[0:L, :], ALU.add).then_inc(S[tag + "_var"], 1)
                pool.wait_ge(S[tag + "_var"], b_count)
                pool.tensor_tensor(rs[0:L, :], ve[0:L, :], mhalf[0:L, 0:1], ALU.pow).then_inc(S[tag + "_rstd"], 1)

            def head_queries(b, p, c):
                pool.wait_ge(S["q_done"], b + 1)
                if not (fixed(b, 0) and c < 2):
                    pool.wait_ge(S["s_ready"], NH * b + 4 * (c - 1))
                pool.tensor_tensor(qz[:, c % 2, :, :], qn[:, p, c:c + 1, :].to_broadcast([P, 4, L]),
                                   rows_of[:, :].unsqueeze(2).to_broadcast([P, 4, L]), ALU.mult).then_inc(S["qz_done"], 1)

            def body(b, p):
                if has_heads(b):
                    head_queries(b, p, 1)
                if has_prep(b):
                    rstd(b + 2, mv1, ve1, rs1, "ln1")
                if has_heads(b):
                    if fixed(b, FIRST):
                        pool.wait_ge(S["small_in"], 64)
                    pool.wait_ge(S["xr_in"], 16 * (b + 1))
                    pool.tensor_tensor(xr[0:L, :], xr[0:L, :], obr[0:L, :], ALU.add).then_inc(S["xr_ob"], 1)
                    head_queries(b, p, 2)
                if has_tail(b):
                    rstd(b, mv2, ve2, rs2, "ln2")
                if has_heads(b):
                    head_queries(b, p, 3)
                if has_prep(b):
                    n = b + 1
                    pool.wait_ge(S["squares"], (NC + 2) * (n + 1))
                    pool.tensor_tensor(sq[:, 0:2, :], sq[:, 0:2, :], sq[:, 2:4, :], ALU.add).then_inc(S["sum_a"], 1)
                    pool.wait_ge(S["sum_a"], n + 1)
                    pool.tensor_tensor(sq[:, 0, :], sq[:, 0, :], sq[:, 1, :], ALU.add).then_inc(S["sum_b"], 1)
                    taken(pool, "ms", b)
                    pool.tensor_tensor(rr[:, :], msb[:, :], mhalf[:, :], ALU.pow).then_inc(S["r_done"], 1)
                    pool.wait_ge(S["r_done"], n + 1)
                    if fixed(b, -1):
                        pool.wait_ge(S["nq_done"], 3)
                    pool.tensor_tensor(diag.rearrange("p (t n) -> p t n", t=4), ident[:, :].unsqueeze(1).to_broadcast([P, 4, P]),
                                       rr[:, :].unsqueeze(2).to_broadcast([P, 4, P]), ALU.mult).then_inc(S["diag_done"], 1)
                    head_queries(b + 1, 1 - p, 0)

            bodies(pool, body)

            pool.wait_ge(S["slots_done"], 1)
            pool.wait_ge(S["zero_stored"], 16 * ZERO_STORES)
            for c in range(2):
                for b in range(B):
                    pool.indirect_dma_start(
                        out=slots_d, out_offset=bass.IndirectOffsetOnAxis(ap=slotu[0:L, c, b:b + 1], axis=0),
                        in_=xn2[0:L, b, :], in_offset=None).then_inc(S["scattered"], 16)
            pool.wait_ge(S["experts_over"], 1)
            for b in range(B):
                if b >= 4:
                    pool.wait_ge(S["fin_b"], b - 3)
                for c in range(2):
                    pool.indirect_dma_start(
                        out=fin[b % 4][1 + c][0:L, :], out_offset=None, in_=y_d,
                        in_offset=bass.IndirectOffsetOnAxis(ap=slotu[0:L, c, b:b + 1], axis=0)).then_inc(fin_in[b % 4], 16)

        @block.scalar
        def _(act):
            for i, m in enumerate((WKI, WQ, WK, WVI, WV, WO)):
                act.wait_ge(wraw_in[i % 2], 16 * (i // 2 + 1))
                act.activation(wH(m), raw_w[i % 2], ACT.Copy).then_inc(S["wh_done"], 1)
                if i == 0:
                    split_ctx(act, 1, 0)
                    split_ctx(act, 1, 1)
                if i == 1:
                    act.wait_ge(S["xl_in"], 16)
                    act.activation(xl2[:, 0, :, :], xlT[:, :, :], ACT.Copy).then_inc(S["xlh"], 1)

            def stage(name, b, p):
                n = b + 1
                if name == "o":
                    return
                bank, cnt = tile_use(name, b)
                if name == "xT":
                    act.wait_ge(tile_ready[bank], cnt + 1)
                    act.activation(xs2[:, 0, :, :], tiles[:, bank, 0:NC * L].rearrange("p (c q) -> p c q", c=NC),
                                   ACT.Copy).then_inc(S["xh_done"], 1)
                if name in ("v0", "v1", "v2"):
                    t = int(name[1])
                    rows = P if t < 2 else TAIL
                    act.wait_ge(tile_ready[bank], cnt + 1)
                    act.activation(vn[0:rows, p if t == 2 else 1 - p, t, :], tiles[0:rows, bank, :], ACT.Copy).then_inc(tile_free[bank], 1)
                if name == "q":
                    taken(act, "q", b)
                    act.activation(sq[:, :, 0:L], qn[:, 1 - p, :, :], ACT.Square).then_inc(S["squares"], 1)
                if name in ("qt", "kt"):
                    rows = L if name == "qt" else TXT
                    act.wait_ge(tile_ready[bank], cnt + 1)
                    act.activation(xn[0:rows, :], tiles[0:rows, bank, :], ACT.Copy).then_inc(tile_free[bank], 1)
                if name in ("k0", "k1", "k2", "k3"):
                    taken(act, name, b)
                    c = int(name[1])
                    act.activation(sq[:, c, L:L + IMG], kn[:, 1 - p, c, 0:IMG], ACT.Square).then_inc(S["squares"], 1)
                if name == "kx":
                    taken(act, "kx", b)
                    act.activation(sq[:, :, L + IMG:TOK], kn[:, 1 - p, :, IMG:KEYS], ACT.Square).then_inc(S["squares"], 1)

            def weigh(b, p, h):
                s = h % 4
                act.wait_ge(S["max_done"], NH * b + h + 1)
                act.activation(probs[0:L, s, 0:IMG], scores[0:L, h % 2, 0:IMG], ACT.Exp,
                               bias=nmax[0:L, s, 0:1], accum_out=sums[0:L, s, 0:1])
                act.activation(probs[0:L, s, IMG:KEYS], scores[0:L, h % 2, IMG:KEYS], ACT.Exp,
                               bias=nmax[0:L, s, 1:2], accum_out=sums[0:L, s, 1:2]).then_inc(S["exp_done"], 1)

            def take_transposed(b, h):
                act.wait_ge(S["t_ready"], NH * b + h + 1)
                if not (fixed(b, 0) and h < 8):
                    act.wait_ge(S["pv_ready"], NC * b + h // 4 - 1)
                act.activation(probT[:, h % 8, :, :], ptb[:, h % 2, 0:KT * L].rearrange("p (t q) -> p t q", t=KT),
                               ACT.Copy).then_inc(S["pt_done"], 1)

            def take_attended(b, g):
                act.wait_ge(S["pv_ready"], NC * b + g + 1)
                act.activation(a2[:, 0, g, :], pvb[:, 0:L], ACT.Identity, bias=vbias[:, g:g + 1]).then_inc(S["ah_done"], 1)

            def body(b, p):
                for h in range(NH):
                    if h == 0 and has_prep(b) and not fixed(b, -1):
                        split_ctx(act, b + 2, 0)
                    if h == 2 and has_tail(b):
                        take_attended(b - 1, 3)
                    if has_heads(b):
                        weigh(b, p, h)
                    if h < LAG:
                        if has_tail(b):
                            take_transposed(b - 1, NH - LAG + h)
                    elif has_heads(b):
                        take_transposed(b, h - LAG)
                    if h in (6, 10, 14) and has_heads(b):
                        take_attended(b, (h - 6) // 4)
                    for name in STAGE_AT[h]:
                        if has(name, b):
                            stage(name, b, p)
                    if h == 1 and has_prep(b) and not fixed(b, -1):
                        split_ctx(act, b + 2, 1)
                    if fixed(b, -1) and h == 15:
                        act.wait_ge(S["vlast_mm"], 1)
                        act.activation(vlast, pvb[0:B, :], ACT.Copy).then_inc(S["vlast_sb"], 1)
                        act.wait_ge(S["vbias_done"], 1)

            bodies(act, body)

            for b in range(B):
                g = AFTER + b
                act.wait_ge(tile_ready[g % 3], g // 3 + 1)
                if b >= 2:
                    act.wait_ge(S["gate_ready"], b - 1)
                act.activation(xt[:, b % 2, :, :], tiles[:, g % 3, 0:NC * L].rearrange("p (c q) -> p c q", c=NC),
                               ACT.Copy).then_inc(tile_free[g % 3], 1)
            act.wait_ge(S["route"], 3)
            act.activation(ex[0:L], lg[0:L], ACT.Exp).then_inc(S["g_exp"], 1)

            act.wait_ge(S["slots_done"], 1)
            e = act.value_load(ebi[0:1, 0:1], min_val=0, max_val=E - 1)

            def convert(use, slot):
                act.wait_ge(raw_in[slot], 16 * (use + 1))
                act.activation(EH[slot], raw[slot], ACT.Copy).then_inc(S["eh_done"], 1)

            def split_input(j):
                act.wait_ge(S["xT_ready"], j + 1)
                act.activation(xTH, xTb[:, :, :].rearrange("p b (c n) -> p (b c) n", n=BLOCK), ACT.Copy).then_inc(S["xTh_done"], 1)

            act.sem_inc(S["gel_done"], 4)
            for pc in range(4):
                convert(0, pc)
            split_input(0)
            act.wait_ge(S["small_in"], 64)
            used = act.value_load(ebi[0:1, MAX_BLOCKS + 1:MAX_BLOCKS + 2], min_val=1, max_val=MAX_BLOCKS)
            with act.Fori(0, MAX_BLOCKS) as j:
                with act.If(j < used):
                    e = act.value_load(ebi[0:1, bass.ds(j, 1)], min_val=0, max_val=E - 1)
                    for pc in range(PIECES):
                        if pc < 6:
                            for m in CHUNKS[pc]:
                                act.wait_ge(S["hid_ready"], 16 * j + m + 1)
                                act.wait_ge(S["hl_done"], 16 * j + m + 1)
                                act.activation(gel[:, m % 4, :], hid[m % 4][:, 0:BLOCK], ACT.Gelu,
                                               bias=b12s[:, bass.ds(e, 1), m:m + 1].rearrange("p a o -> p (a o)")
                                               ).then_inc(S["gel_done"], 1)
                        if pc < 6:
                            act.wait_ge(S["hid_ready"], 16 * j + CHUNKS[pc][-1] + 1)
                        else:
                            act.wait_ge(S["y_piece"], 2 * j + pc - 5)
                        convert(2 * j + pc // 4 + 1, pc % 4)
                        if pc == 5:
                            split_input(j + 1)

        @block.vector
        def _(dve):
            dve.wait_ge(S["consts"], 1)
            dve.memset(rows_of[:, :], 0.0).then_inc(S["rows_done"], 1)
            dve.wait_ge(S["rows_done"], 1)
            for j in range(4):
                dve.memset(rows_of[HD * j:HD * j + HD, j:j + 1], 1.0)
            dve.tensor_scalar(ident[:, :], iota[:, :], pidx[:, 0:1], None, ALU.is_equal).then_inc(S["nq_done"], 1)
            dve.tensor_scalar(upper[:, :], iota[:, :], pidx[:, 0:1], None, ALU.is_gt).then_inc(S["nq_done"], 1)
            dve.wait_ge(S["vec_in"], 16)
            dve.tensor_scalar(nq[:, :], vec[:, V_NQ, :], float(HD) ** -0.5, None, ALU.mult).then_inc(S["nq_done"], 1)
            dve.tensor_tensor(vbias[:, :], vec[:, V_VB, :], vec[:, V_VIB, :], ALU.add).then_inc(S["vbias_done"], 1)

            def split_ctx_low(n, i):
                dve.wait_ge(S["ch_done"], 2 * n - 1 + i)
                dve.tensor_tensor(cL[:, :, PARTS[i]], cr[:, :, PARTS[i]], cH[:, :, PARTS[i]].bitcast(F32), ALU.subtract).then_inc(S["cl_done"], 1)

            def ln_stats(count, src, st, mv, tag):
                dve.bn_stats(st[0:L, :], src[0:L, :]).then_inc(S[tag + "_stats"], 1)
                dve.wait_ge(S[tag + "_stats"], count)
                dve.sem_inc(S["aggr"], 1)
                dve.bn_aggr(mv[0:L, :], st[0:L, :]).then_inc(S[tag + "_mv"], 1)

            def ln_apply(count, dst, src, mv, rs, tag, done):
                dve.wait_ge(S[tag + "_rstd"], count)
                dve.tensor_scalar(dst, src[0:L, :], mv[0:L, 0:1], rs[0:L, 0:1], ALU.subtract, ALU.mult).then_inc(S[done], 1)

            for i, m in enumerate((WKI, WQ, WK, WVI, WV, WO)):
                dve.wait_ge(S["wh_done"], i + 1)
                dve.tensor_tensor(wL(m), raw_w[i % 2], wH(m).bitcast(F32), ALU.subtract).then_inc(S["wl_done"], 1)
                if i == 0:
                    split_ctx_low(1, 0)
                    split_ctx_low(1, 1)
                if i == 1:
                    dve.wait_ge(S["xlh"], 1)
                    dve.tensor_tensor(xl2[:, 1, :, :], xlT[:, :, :], xl2[:, 0, :, :].bitcast(F32), ALU.subtract).then_inc(S["xll"], 1)
            dve.wait_ge(S["wl_done"], 6)
            dve.memset(probs[:, :, KEYS:KT * P], 0.0)

            def normalise_keys(tile, p, c):
                k = kn[:, p, c, :]
                dve.scalar_tensor_tensor(k[:, 0:IMG], k[:, 0:IMG], vec[:, V_NKI, c:c + 1], tile[:, L:L + IMG], ALU.mult, ALU.mult)
                dve.scalar_tensor_tensor(k[:, IMG:KEYS], k[:, IMG:KEYS], vec[:, V_NK, c:c + 1], tile[:, L + IMG:TOK],
                                         ALU.mult, ALU.mult).then_inc(S["k_done"], 1)

            def stage(name, b, p):
                n = b + 1
                bank, cnt = tile_use(name, b)
                tile = tiles[:, bank, :]
                if name in ("v0", "v1", "v2", "qt", "kt"):
                    return
                if name == "o":
                    dve.wait_ge(tile_ready[bank], cnt + 1)
                    dve.wait_ge(S["xr_ob"], b)
                    dve.tensor_tensor(x1[0:L, :], tile[0:L, :], xr[0:L, :], ALU.add).then_inc(tile_free[bank], 1)
                    return
                if name == "rb":
                    dve.wait_ge(tile_ready[bank], cnt + 1)
                    for c in range(NC):
                        q = qn[:, 1 - p, c, :]
                        last = dve.scalar_tensor_tensor(q, q, nq[:, c:c + 1], tile[:, 0:L], ALU.mult, ALU.mult)
                    last.then_inc(S["q_done"], 1)
                    normalise_keys(tile, 1 - p, 0)
                    return
                if name == "xT":
                    dve.wait_ge(S["xh_done"], n + 1)
                    dve.tensor_tensor(xs2[:, 1, :, :], tile[:, 0:NC * L].rearrange("p (c q) -> p c q", c=NC),
                                      xs2[:, 0, :, :].bitcast(F32), ALU.subtract).then_inc(tile_free[bank], 1)
                    return
                dve.wait_ge(tile_ready[bank], cnt + 1)
                if name == "q":
                    dve.tensor_tensor(qn[:, 1 - p, :, :], tile[:, 0:NC * L].rearrange("p (c q) -> p c q", c=NC),
                                      vec[:, V_QB, :].unsqueeze(2).to_broadcast([P, NC, L]), ALU.add).then_inc(tile_free[bank], 1)
                elif name == "ms":
                    dve.tensor_scalar(msb[:, :], tile[:, 0:4], 1.0 / D, RMS_EPS, ALU.mult, ALU.add).then_inc(tile_free[bank], 1)
                elif name == "kx":
                    dve.tensor_tensor(kn[:, 1 - p, :, IMG:KEYS], tile[:, 0:NC * TXT].rearrange("p (c k) -> p c k", c=NC),
                                      vec[:, V_KB, :].unsqueeze(2).to_broadcast([P, NC, TXT]), ALU.add).then_inc(tile_free[bank], 1)
                else:
                    c = int(name[1])
                    dve.tensor_scalar(kn[:, 1 - p, c, 0:IMG], tile[:, 0:IMG], vec[:, V_KIB, c:c + 1], None, ALU.add).then_inc(tile_free[bank], 1)

            def maxima(b, h):
                dve.wait_ge(S["s_ready"], NH * b + h + 1)
                dve.tensor_reduce(nmax[0:L, h % 4, 0:1], scores[0:L, h % 2, 0:IMG], AX.X, ALU.max, negate=True)
                dve.tensor_reduce(nmax[0:L, h % 4, 1:2], scores[0:L, h % 2, IMG:KEYS], AX.X, ALU.max, negate=True).then_inc(S["max_done"], 1)

            def normalise(b, h):
                s = h % 4
                dve.wait_ge(S["exp_done"], NH * b + h + 1)
                dve.reciprocal(rsum[0:L, s, :], sums[0:L, s, :]).then_inc(S["rsum_done"], 1)
                dve.wait_ge(S["rsum_done"], NH * b + h + 1)
                dve.tensor_scalar(probs[0:L, s, 0:IMG], probs[0:L, s, 0:IMG], rsum[0:L, s, 0:1], None, ALU.mult)
                dve.tensor_scalar(probs[0:L, s, IMG:KEYS], probs[0:L, s, IMG:KEYS], rsum[0:L, s, 1:2], None,
                                  ALU.mult).then_inc(S["p_ready"], 1)

            def attended_low(b, g):
                dve.wait_ge(S["ah_done"], NC * b + g + 1)
                dve.scalar_tensor_tensor(a2[:, 1, g, :], pvb[:, 0:L], vbias[:, g:g + 1], a2[:, 0, g, :].bitcast(F32),
                                         ALU.add, ALU.subtract).then_inc(S["al_done"], 1)

            def body(b, p):
                for h in range(NH):
                    if has_heads(b):
                        maxima(b, h)
                    if h == 0:
                        if has_tail(b):
                            normalise(b - 1, NH - 1)
                    elif has_heads(b):
                        normalise(b, h - 1)
                    if h in (6, 10, 14) and has_heads(b):
                        attended_low(b, (h - 6) // 4)
                    if h in KEYS_AT and (has_prep if h == 15 else has_heads)(b):
                        c, step = KEYS_AT[h]
                        bank = tile_use("rb", b + step)[0]
                        normalise_keys(tiles[:, bank, :], p if step else 1 - p, c)
                        if c == NC - 1:
                            dve.wait_ge(S["k_done"], NC * (b + 1))
                            dve.sem_inc(tile_free[bank], 1)
                    if h in (0, 2) and has_prep(b) and not fixed(b, -1):
                        split_ctx_low(b + 2, h // 2)
                    if h == 2 and has_tail(b):
                        attended_low(b - 1, 3)
                    if h == 2 and has_prep(b):
                        dve.wait_ge(S["x_in"], 16 * (b + 2))
                        ln_stats(b + 2, xb, st1, mv1, "ln1")
                    if h == 3 and has_prep(b):
                        ln_apply(b + 2, xn[0:L, :], xb, mv1, rs1, "ln1", "xn_done")
                    if h == 5 and has_tail(b):
                        dve.wait_ge(tile_free[tile_use("o", b)[0]], tile_use("o", b)[1] + 1)
                        ln_stats(b, x1, st2, mv2, "ln2")
                    for name in STAGE_AT[h]:
                        if has(name, b):
                            stage(name, b, p)
                    if h == 7 and has_tail(b):
                        if fixed(b, LAST) or fixed(b, DONE):
                            dst = xn2[0:L, b - 1, :]
                        else:
                            dst = xn2[0:L, bass.ds(b - 1, 1), :].rearrange("p a d -> p (a d)")
                            dve.wait_ge(S["zero_stored"], 16 * ZERO_STORES)
                        ln_apply(b, dst, x1, mv2, rs2, "ln2", "xn2_done")
                    if h == NH - 1 and has_tail(b):
                        dve.wait_ge(S["x1_stored"], 16 * b)

            bodies(dve, body)

            steps = [0]

            def after(ins):
                steps[0] += 1
                ins.then_inc(S["route"], 1)
                dve.wait_ge(S["route"], steps[0])

            bc = lambda ap, shape: ap.to_broadcast(shape)
            full = [L, B, E]
            dve.wait_ge(S["gate_ready"], B)
            dve.wait_ge(S["small_in"], 64)
            after(dve.tensor_tensor(lg[0:L], scores[0:L, 0, 0:B * E].rearrange("p (b e) -> p b e", b=B),
                                    bc(bgr[0:L, :].unsqueeze(1), full), ALU.add))
            after(dve.tensor_reduce(mx[0:L, :], lg[0:L], AX.X, ALU.max))
            after(dve.tensor_tensor(lg[0:L], lg[0:L], bc(mx[0:L, :].unsqueeze(2), full), ALU.subtract))
            dve.wait_ge(S["g_exp"], 1)
            after(dve.tensor_reduce(sm[0:L, :], ex[0:L], AX.X, ALU.add))
            after(dve.reciprocal(rc[0:L, :], sm[0:L, :]))
            after(dve.tensor_tensor(gw[0:L], ex[0:L], bc(rc[0:L, :].unsqueeze(2), full), ALU.mult))
            for b in range(B):
                last = dve.max(top[0:L, b, :], gw[0:L, b, :])
            after(last)
            for b in range(B):
                last = dve.max_index(topi[0:L, b, :], top[0:L, b, :], gw[0:L, b, :])
            after(last)
            after(dve.tensor_copy(tif[0:L], topi[0:L, :, :]))
            dve.tensor_copy(topw[0:L, 0, :], top[0:L, :, 0])
            dve.tensor_copy(topw[0:L, 1, :], top[0:L, :, 1])
            number = bc(iota[0:L, 0:E].unsqueeze(1), full)
            dve.tensor_tensor(sel1[0:L], bc(tif[0:L, :, 0:1], full), number, ALU.is_equal)
            after(dve.tensor_tensor(sel2[0:L], bc(tif[0:L, :, 1:2], full), number, ALU.is_equal))
            after(dve.tensor_tensor(msk[0:L], sel1[0:L], sel2[0:L], ALU.add))
            mask_made = steps[0]
            dve.wait_ge(S["rank_ready"], 1)
            after(dve.memset(pre[:, 0, :], 0.0))
            totals = ptb[:, 0, 0:B * E].rearrange("p (b e) -> p b e", b=B)
            for b in range(B):
                after(dve.tensor_tensor(pre[:, b + 1, :], totals[:, b, :], pre[:, b, :], ALU.add))
            count = pre[:, B, :]
            after(dve.tensor_scalar(nblk, count, 0.0, None, ALU.is_gt))
            for k in range(1, -(-T // BLOCK)):
                after(dve.scalar_tensor_tensor(nblk, count, float(k * BLOCK), nblk, ALU.is_gt, ALU.add))
            after(dve.tensor_copy(ends, nblk))
            for k in range(1, E):
                after(dve.tensor_tensor(ends[:, k:k + 1], ends[:, k:k + 1], ends[:, k - 1:k], ALU.add))
            after(dve.tensor_tensor(base, ends, nblk, ALU.subtract))
            after(dve.tensor_scalar(base, base, float(BLOCK), None, ALU.mult))
            after(dve.tensor_tensor(slotm[0:L], scores[0:L, 1, 0:B * E].rearrange("p (b e) -> p b e", b=B), pre[0:L, 0:B, :], ALU.add))
            after(dve.tensor_tensor(slotm[0:L], slotm[0:L], bc(base[0:L, :].unsqueeze(1), full), ALU.add))
            dve.tensor_tensor(tmp1[0:L], slotm[0:L], sel1[0:L], ALU.mult)
            after(dve.tensor_tensor(tmp2[0:L], slotm[0:L], sel2[0:L], ALU.mult))
            dve.tensor_reduce(slotf[0:L, 0, :], tmp1[0:L], AX.X, ALU.add)
            after(dve.tensor_reduce(slotf[0:L, 1, :], tmp2[0:L], AX.X, ALU.add))
            dve.tensor_copy(slotu[0:L, :, :], slotf[0:L])
            after(dve.tensor_tensor(cmpb[0:1], bc(ends[0:1, :].unsqueeze(1), [1, 16, E]), bc(iota[0:1, 0:16].unsqueeze(2), [1, 16, E]), ALU.is_le))
            after(dve.tensor_reduce(ebf[0:1, :], cmpb[0:1], AX.X, ALU.add))
            after(dve.tensor_scalar(ebf[0:1, :], ebf[0:1, :], float(E - 1), None, ALU.min))
            after(dve.tensor_copy(ebf[0:1, MAX_BLOCKS + 1:MAX_BLOCKS + 2], ends[0:1, E - 1:E]))
            dve.tensor_copy(ebi[0:1, :], ebf[0:1, :]).then_inc(S["slots_done"], 1)

            def convert(q, slot):
                dve.wait_ge(S["eh_done"], q + 1)
                dve.tensor_tensor(EL[slot], raw[slot], EH[slot].bitcast(F32), ALU.subtract).then_inc(S["el_done"], 1)

            def split_input(j):
                dve.wait_ge(S["xTh_done"], j + 1)
                dve.tensor_tensor(xTL, xTb[:, :, :].rearrange("p b (c n) -> p (b c) n", n=BLOCK), xTH.bitcast(F32), ALU.subtract).then_inc(S["xTl_done"], 1)

            dve.memset(gel[:, :, :], 0.0).then_inc(S["hl_done"], 4)
            for pc in range(4):
                convert(pc, pc)
            split_input(0)
            dve.wait_ge(S["b3_in"], 16)
            used = dve.value_load(ebi[0:1, MAX_BLOCKS + 1:MAX_BLOCKS + 2], min_val=1, max_val=MAX_BLOCKS)
            with dve.Fori(0, MAX_BLOCKS) as j:
                with dve.If(j < used):
                    e = dve.value_load(ebi[0:1, bass.ds(j, 1)], min_val=0, max_val=E - 1)
                    for pc in range(PIECES):
                        if pc < 6:
                            for m in CHUNKS[pc]:
                                lay, c = m // 8, m % 8
                                dve.wait_ge(S["gel_done"], 16 * j + m + 5)
                                dve.tensor_copy(hH[lay][:, c, :], gel[:, m % 4, :]).then_inc(S["hh_done"], 1)
                                dve.wait_ge(S["hh_done"], 16 * j + m + 1)
                                dve.tensor_tensor(hL[lay][:, c, :], gel[:, m % 4, :], hH[lay][:, c, :].bitcast(F32),
                                                  ALU.subtract).then_inc(S["hl_done"], 1)
                        convert(PIECES * j + pc + 4, pc % 4)
                        if pc == 5:
                            split_input(j + 1)
                    dve.wait_ge(S["y_piece"], 2 * j + 2)
                    dve.tensor_tensor(ys, yb[:, :, :], b3s[:, bass.ds(e, 1), :].to_broadcast([P, 2, D]), ALU.add).then_inc(S["y_sb"], 1)

            for b in range(B):
                dve.wait_ge(fin_in[b % 4], 32 * (b // 4 + 1))
                dve.wait_ge(x1_in[b % 4], 16 * (b // 4 + 1))
                f = fin[b % 4]
                dve.scalar_tensor_tensor(f[0][0:L, :], f[1][0:L, :], topw[0:L, 0, b:b + 1], f[0][0:L, :], ALU.mult, ALU.add).then_inc(S["fin_a"], 1)
                dve.wait_ge(S["fin_a"], b + 1)
                dve.scalar_tensor_tensor(f[0][0:L, :], f[2][0:L, :], topw[0:L, 1, b:b + 1], f[0][0:L, :], ALU.mult, ALU.add).then_inc(S["fin_b"], 1)

        @block.tensor
        def _(pe):
            def three(out, wh, wl, xh, xl, start, stop):
                pe.matmul(out, wh, xh, start=start, stop=False)
                pe.matmul(out, wh, xl, start=False, stop=False)
                return pe.matmul(out, wl, xh, start=False, stop=stop)

            def stage(name, lo, hi, b, p):
                n = b + 1
                bank, cnt = tile_use(name, b)
                tile = tiles[:, bank, :]
                if lo == 0:
                    pe.wait_ge(tile_free[bank], cnt)
                if name in ("xT", "q", "kx"):
                    if name == "xT":
                        pe.wait_ge(S["xn_done"], n + 1)
                    else:
                        taken(pe, "qt" if name == "q" else "kt", b)
                    rows = TXT if name == "kx" else L
                    for c in range(NC):
                        mm = pe.transpose(tile[:, c * rows:(c + 1) * rows], xn[0:rows, c * P:(c + 1) * P], ident[0:rows, 0:rows])
                elif name in ("qt", "kt"):
                    if lo == 0 and name == "qt":
                        taken(pe, "xT", b)
                    wh, wl = wv(WQ if name == "qt" else WK)
                    rows = L if name == "qt" else TXT
                    for c in range(lo, hi):
                        if name == "qt":
                            vh, vl = xs2[:, 0, c, :], xs2[:, 1, c, :]
                        else:
                            vh, vl = cH[:, c, IMG:KEYS], cL[:, c, IMG:KEYS]
                        pe.matmul(tile[0:rows, :], vh, wh[:, c, :], start=(c == 0), stop=False)
                        pe.matmul(tile[0:rows, :], vh, wl[:, c, :], start=False, stop=False)
                        mm = pe.matmul(tile[0:rows, :], vl, wh[:, c, :], start=False, stop=(c == NC - 1))
                elif name[0] == "k":
                    o = int(name[1])
                    if lo == 0:
                        pe.wait_ge(S["cl_done"], 2 * (n + 1))
                    wh, wl = wv(WKI)
                    for c in range(lo, hi):
                        mm = three(tile[:, 0:IMGE], wh[:, c, o * P:(o + 1) * P], wl[:, c, o * P:(o + 1) * P],
                                   cH[:, c, 0:IMGE], cL[:, c, 0:IMGE], c == 0, c == NC - 1)
                elif name[0] == "v":
                    t = int(name[1])
                    rows = P if t < 2 else TAIL
                    wh, wl = wv(WVI if t < 2 else WV)
                    for c in range(lo, hi):
                        ch, cl = cH[:, c, t * P:t * P + rows], cL[:, c, t * P:t * P + rows]
                        pe.matmul(tile[0:rows, :], ch, wh[:, c, :], start=(c == 0), stop=False)
                        pe.matmul(tile[0:rows, :], ch, wl[:, c, :], start=False, stop=False)
                        mm = pe.matmul(tile[0:rows, :], cl, wh[:, c, :], start=False, stop=(c == NC - 1))
                elif name == "ms":
                    pe.wait_ge(S["sum_b"], n + 1)
                    for t in range(4):
                        mm = pe.matmul(tile[:, t:t + 1], ssum[:, t * P:(t + 1) * P], ones[:, 0:1], start=True, stop=True)
                elif name == "rb":
                    pe.wait_ge(S["diag_done"], n + 1)
                    mm = pe.matmul(tile[:, :], ones[:, :], diag, start=True, stop=True)
                elif name == "o":
                    if lo == 0:
                        pe.wait_ge(S["al_done"], NC * b)
                    wh, wl = wv(WO)
                    for c in range(lo, hi):
                        pe.matmul(tile[0:L, :], a2[:, 0, c, :], wh[:, c, :], start=(c == 0), stop=False)
                        pe.matmul(tile[0:L, :], a2[:, 0, c, :], wl[:, c, :], start=False, stop=False)
                        mm = pe.matmul(tile[0:L, :], a2[:, 1, c, :], wh[:, c, :], start=False, stop=(c == NC - 1))
                if hi == GROUPS[name]:
                    mm.then_inc(tile_ready[bank], 1)

            def score(b, p, h):
                if h % 4 == 0:
                    pe.wait_ge(S["qz_done"], NC * b + h // 4 + 1)
                    pe.wait_ge(S["k_done"], NC * b + h // 4 + 1)
                if not (fixed(b, 0) and h < 2):
                    pe.wait_ge(S["exp_done"], NH * b + h - 1)
                pe.matmul(scores[0:L, h % 2, 0:KEYS], qz[:, (h // 4) % 2, h % 4, :], kn[:, p, h // 4, :], start=True, stop=True).then_inc(S["s_ready"], 1)

            def transpose(b, h):
                pe.wait_ge(S["p_ready"], NH * b + h + 1)
                if not (fixed(b, 0) and h < 2):
                    pe.wait_ge(S["pt_done"], NH * b + h - 1)
                for t in range(KT):
                    mm = pe.transpose(ptb[:, h % 2, t * L:(t + 1) * L], probs[0:L, h % 4, t * P:(t + 1) * P], ident[0:L, 0:L])
                mm.then_inc(S["t_ready"], 1)

            def attend(b, p, g):
                pe.wait_ge(S["pt_done"], NH * b + 4 * g + 4)
                if g == 0:
                    pe.wait_ge(S["vrow_in"], 16 * (b + 1))
                pe.wait_ge(S["al_done"], NC * b + g)
                for t in range(KT):
                    rows = P if t < 2 else TAIL
                    for i in range(4):
                        h = 4 * g + i
                        mm = pe.matmul(pvb[HD * i:HD * i + HD, 0:L], vn[0:rows, p, t, HD * h:HD * h + HD],
                                       probT[0:rows, h % 8, t, :], start=(t == 0), stop=(t == KT - 1))
                mm.then_inc(S["pv_ready"], 1)

            def body(b, p):
                if fixed(b, -1):
                    pe.wait_ge(S["nq_done"], 3)
                    pe.wait_ge(S["wl_done"], 1)
                for h in range(NH):
                    if has_heads(b):
                        score(b, p, h)
                    if h < LAG:
                        if has_tail(b):
                            transpose(b - 1, NH - LAG + h)
                    elif has_heads(b):
                        transpose(b, h - LAG)
                    if h == 2 and has_tail(b):
                        attend(b - 1, 1 - p, 3)
                    if h in (6, 10, 14) and has_heads(b):
                        attend(b, p, (h - 6) // 4)
                    for name, lo, hi in FILL[h]:
                        if has(name, b):
                            if fixed(b, -1) and lo == 0 and name in ("qt", "kt", "v0"):
                                pe.wait_ge(S["wl_done"], 2 + ("qt", "kt", "v0").index(name))
                            stage(name, lo, hi, b, p)
                if fixed(b, -1):
                    pe.wait_ge(S["xll"], 1)
                    pe.wait_ge(S["wl_done"], 6)
                    wh, wl = wv(WVI)
                    for c in range(NC):
                        pe.matmul(pvb[0:B, :], xl2[:, 0, c, :], wh[:, c, :], start=(c == 0), stop=False)
                        pe.matmul(pvb[0:B, :], xl2[:, 0, c, :], wl[:, c, :], start=False, stop=False)
                        mm = pe.matmul(pvb[0:B, :], xl2[:, 1, c, :], wh[:, c, :], start=False, stop=(c == NC - 1))
                    mm.then_inc(S["vlast_mm"], 1)
                    pe.wait_ge(S["vlast_sb"], 1)

            bodies(pe, body)

            pe.wait_ge(S["small_in"], 64)

            def gate_in(b):
                g = AFTER + b
                pe.wait_ge(S["xn2_done"], b + 1)
                pe.wait_ge(tile_free[g % 3], g // 3)
                for c in range(NC):
                    mm = pe.transpose(tiles[:, g % 3, c * L:(c + 1) * L], xn2[0:L, b, c * P:(c + 1) * P], ident[0:L, 0:L])
                mm.then_inc(tile_ready[g % 3], 1)

            def gate(b):
                g = AFTER + b
                pe.wait_ge(tile_free[g % 3], g // 3 + 1)
                for c in range(NC):
                    mm = pe.matmul(scores[0:L, 0, b * E:(b + 1) * E], xt[:, b % 2, c, :], wgs[:, c, :], start=(c == 0), stop=(c == NC - 1))
                mm.then_inc(S["gate_ready"], 1)

            gate_in(0)
            for b in range(B):
                if b + 1 < B:
                    gate_in(b + 1)
                gate(b)
            pe.wait_ge(S["route"], 11)
            pe.matmul(scores[0:L, 1, 0:B * E], upper[0:L, 0:L], msk[0:L].rearrange("p b e -> p (b e)"), start=True, stop=True)
            pe.matmul(ptb[:, 0, 0:B * E], ones[0:L, :], msk[0:L].rearrange("p b e -> p (b e)"), start=True, stop=True).then_inc(S["rank_ready"], 1)

            pe.wait_ge(S["slots_done"], 1)

            def turn(j):
                pe.wait_ge(S["xs_in"], 16 * (j + 1))
                pe.wait_ge(S["xTl_done"], j)
                for c in range(NC):
                    for t in range(2):
                        mm = pe.transpose(xTb[:, c // 2, (c % 2) * BLOCK + t * P:(c % 2) * BLOCK + (t + 1) * P],
                                          xs[:, t, c * P:(c + 1) * P], ident[:, :])
                mm.then_inc(S["xT_ready"], 1)

            turn(0)
            used = pe.value_load(ebi[0:1, MAX_BLOCKS + 1:MAX_BLOCKS + 2], min_val=1, max_val=MAX_BLOCKS)
            with pe.Fori(0, MAX_BLOCKS) as j:
                with pe.If(j < used):
                    pe.wait_ge(S["xTl_done"], j + 1)
                    for pc in range(PIECES):
                        pe.wait_ge(S["el_done"], PIECES * j + pc + 1)
                        slot = pc % 4
                        if pc < 6:
                            width, K, per = (512, NC, 4) if pc < 2 else (256, 8, 2)
                            wh = EH[slot].rearrange("p (c n) -> p c n", n=width)
                            wl = EL[slot].rearrange("p (c n) -> p c n", n=width)
                            vh, vl = (xTH, xTL) if pc < 2 else (hH[0], hL[0])
                            for i in range(per):
                                m = 4 * pc + i if pc < 2 else 8 + 2 * (pc - 2) + i
                                pe.wait_ge(S["gel_done"], 16 * j + m + 1)
                                for c in range(K):
                                    if pc == 2 and i == 0:
                                        pe.wait_ge(S["hl_done"], 16 * j + c + 5)
                                    mm = three(hid[m % 4][:, 0:BLOCK], wh[:, c, i * P:(i + 1) * P], wl[:, c, i * P:(i + 1) * P],
                                               vh[:, c, :], vl[:, c, :], c == 0, c == K - 1)
                                mm.then_inc(S["hid_ready"], 1)
                        else:
                            if pc == 6:
                                turn(j + 1)
                            wh = EH[slot].rearrange("p (c n) -> p c n", n=D)
                            wl = EL[slot].rearrange("p (c n) -> p c n", n=D)
                            for i in range(4):
                                f = 4 * (pc - 6) + i
                                pe.wait_ge(S["hl_done"], 16 * j + 8 + f + 5)
                                for t in range(2):
                                    h_hi, h_lo = hH[1][:, f, t * P:(t + 1) * P], hL[1][:, f, t * P:(t + 1) * P]
                                    pe.matmul(yb[:, t, :], h_hi, wh[:, i, :], start=(f == 0), stop=False)
                                    pe.matmul(yb[:, t, :], h_hi, wl[:, i, :], start=False, stop=False)
                                    mm = pe.matmul(yb[:, t, :], h_lo, wh[:, i, :], start=False, stop=(f == 7))
                            mm.then_inc(S["y_piece"], 1)


def kernel(**inputs):
    import numpy as _np
    import concourse.bacc as _bacc
    from concourse import mybir as _mybir
    from concourse.bass_utils import run_bass_kernel_spmd as _run

    nc = _bacc.Bacc("TRN2", target_bir_lowering=False, num_devices=1)
    a = {k: _np.asarray(v) for k, v in inputs.items()}

    def col(v):
        return v.reshape(NC, P).T

    def wt(w):
        return w.T.reshape(NC, P, D).transpose(1, 0, 2).reshape(P, NC * D)

    names = [a["L0_xattn_" + n] for n in ("q_w", "k_img_w", "k_w", "v_img_w", "v_w", "o_w")]
    vecs = [a["L0_xattn_" + n] for n in ("q_b", "k_b", "k_img_b", "v_b", "v_img_b", "norm_q_w", "norm_k_w", "norm_k_img_w")]
    ctx = a["ctx_2048"]
    W1 = a["L0_ffn_W1"].reshape(E, NC, P, 2, 512).transpose(0, 3, 2, 1, 4).reshape(E, 2, P, PIECE)
    W2 = a["L0_ffn_W2"].reshape(E, 8, P, 4, 256).transpose(0, 3, 2, 1, 4).reshape(E, 4, P, PIECE)
    W3 = a["L0_ffn_W3"].reshape(E, 2, 4, P, D).transpose(0, 1, 3, 2, 4).reshape(E, 2, P, PIECE)
    b1, b2 = (a["L0_ffn_" + n].reshape(E, 8, P).transpose(2, 0, 1) for n in ("b1", "b2"))
    ins = [
        a["x"],
        ctx.reshape(B, KEYS, NC, P).transpose(0, 3, 2, 1),
        ctx[:, IMG - 1].reshape(B, NC, P).transpose(2, 1, 0),
        _np.stack([wt(w) for w in names]),
        _np.stack([col(v) for v in vecs], axis=1),
        a["L0_xattn_o_b"],
        a["L0_ffn_Wg"].reshape(NC, P, E).transpose(1, 0, 2),
        a["L0_ffn_bg"],
        _np.concatenate([W1, W2, W3], axis=1),
        _np.concatenate([b1, b2], axis=2),
        a["L0_ffn_b3"],
    ]
    arrays, args = {}, []
    for i, v in enumerate(ins):
        v = _np.ascontiguousarray(v)
        arrays[f"in_{i}_dram"] = v
        args.append(nc.dram_tensor(f"in_{i}_dram", v.shape, _mybir.dt.from_np(v.dtype), kind="ExternalInput").ap())
    args.append(nc.dram_tensor("out_0_dram", (B, L, D), _mybir.dt.float32, kind="ExternalOutput").ap())
    cross_attention_moe(nc, *args)
    r = _run(nc, [arrays], core_ids=[0])
    return r.results[0]["out_0_dram"]
```

```python
from contextlib import ExitStack

import concourse.bass as bass
from concourse import mybir

F32 = mybir.dt.float32
F32R = mybir.dt.float32r
U32 = mybir.dt.uint32
I32 = mybir.dt.int32
ALU = mybir.AluOpType
ACT = mybir.ActivationFunctionType
AX = mybir.AxisListType

P = 128
B, L, D = 8, 112, 512
NC = D // P
NH, HD = 16, 32
IMG, KEYS = 257, 375
TXT = KEYS - IMG
IMGE = IMG + 1
KT = 3
TAIL = KEYS - 2 * P
KP = KEYS + 1
TOK = L + KEYS
E, H = 8, 1024
T = B * L
BLOCK = 256
MAX_BLOCKS = (2 * T - E) // BLOCK + E
PIECE = 2048
PIECES = 8
LN_EPS, RMS_EPS = 1e-5, 1e-6
WQ, WKI, WK, WVI, WV, WO = range(6)
V_QB, V_KB, V_KIB, V_VB, V_VIB, V_NQ, V_NK, V_NKI = range(8)
SLOT = {n: i for i, n in enumerate(("v2", "k0", "o", "xT", "k1", "qt", "k2", "q", "kt", "kx", "k3", "v0", "ms", "rb", "v1"))}
FILL = {0: [("v2", 0, 2)], 1: [("v2", 2, 4)], 2: [("k0", 0, 4)], 3: [("o", 0, 2)], 4: [("o", 2, 4), ("xT", 0, 1)],
        5: [("k1", 0, 4)], 6: [("qt", 0, 2)], 7: [("qt", 2, 4)], 8: [("k2", 0, 4)], 9: [("q", 0, 1), ("kt", 0, 2)],
        10: [("kt", 2, 4)], 11: [("kx", 0, 1), ("k3", 0, 4)], 12: [("v0", 0, 2), ("ms", 0, 1)], 13: [("v0", 2, 4), ("rb", 0, 1)],
        14: [("v1", 0, 2)], 15: [("v1", 2, 4)]}
GROUPS = {n: 1 if n in ("xT", "q", "kx", "ms", "rb") else 4 for n in SLOT}
STAGE_AT = {h: [n for n, lo, hi in f if hi == GROUPS[n]] for h, f in FILL.items()}
CHUNKS = [range(0, 4), range(4, 8)] + [range(8 + 2 * i, 10 + 2 * i) for i in range(4)]
KEYS_AT = {15: (1, 0), 0: (2, -1), 1: (3, -1)}
ORDER = (WKI, WQ, WK, WVI, WV, WO)
WEIGHTS_AT = {4: 2, 7: 3, 13: 4, 15: 5}
KEYS_HIGH_AT = {1: 1, 5: 2, 8: 3}
KEYS_LOW_AT = {2: 1, 6: 2, 10: 3}
LAG = 2
FIRST, LAST, DONE = 0, B - 1, B


def tile_use(name, b):
    i = SLOT[name]
    before_o = i - (i > SLOT["o"])
    if isinstance(b, int) and b < FIRST:
        g = before_o - 1
    elif isinstance(b, int) and b == FIRST:
        g = len(SLOT) - 2 + before_o
    elif isinstance(b, int) and b >= LAST:
        g = 15 * LAST + 12 + {"v2": 0, "o": b - LAST + 1}[name]
    else:
        return i % 3, 5 * b + 4 + i // 3
    return g % 3, g // 3


FULL = -(-T // BLOCK)
PARTS = (slice(0, IMGE), slice(2 * P, KEYS))
ROWS = (MAX_BLOCKS + 1) * BLOCK // P
ZERO_STORES = -(-ROWS // B)


def cross_attention_moe(nc, x, ctxT, ctx_last, wT, vecs, o_b, wg, bg, experts, b12, b3, out):
    with ExitStack() as ctx:
        def sb(name, shape, dt=F32):
            return ctx.enter_context(nc.sbuf_tensor(name, shape, dt))

        def psum(name, shape):
            return ctx.enter_context(nc.psum_tensor(name, shape, F32))

        def sem(name):
            return ctx.enter_context(nc.semaphore(name))

        slots_d = nc.dram_tensor("slots_d", ((MAX_BLOCKS + 1) * BLOCK, D), F32).ap()
        xn2_d = nc.dram_tensor("xn2_d", (B, L, D), F32).ap()
        x1_d = nc.dram_tensor("x1_d", (B, L, D), F32).ap()
        vlast_d = nc.dram_tensor("vlast_d", (B, D), F32).ap()

        w2 = sb("w2", [P, 12 * PIECE], F32R)
        c2 = sb("c2", [P, 2 * NC * (IMGE + TAIL)], F32R)
        scr = sb("scr", [P, 14368])
        kq = sb("kq", [P, 4 * KP + 2 * NC * L + 4 * 4 * L], F32R)
        xb, xn, xr, x1 = sb("xb", [P, D]), sb("xn", [P, D]), sb("xr", [P, D]), sb("x1", [P, D])
        xs2 = sb("xs2", [P, 2, NC, L], F32R)
        qn = sb("qn", [P, 2, NC, L])
        a2 = sb("a2", [P, 2, NC, L], F32R)
        ident, ones = sb("ident", [P, P]), sb("ones", [P, P])
        upper, iota = sb("upper", [P, P]), sb("iota", [P, P])
        vec = sb("vec", [P, 8, NC])
        vbias, nq = sb("vbias", [P, NC]), sb("nq", [P, NC])
        obr = sb("obr", [P, D])
        wgs, bgr = sb("wgs", [P, NC, E]), sb("bgr", [P, E])
        b12s = sb("b12s", [P, E, 16])
        pidx, lneps, mhalf = sb("pidx", [P, 1]), sb("lneps", [P, 1]), sb("mhalf", [P, 4])
        st1, mv1, ve1, rs1 = sb("st1", [P, 6]), sb("mv1", [P, 2]), sb("ve1", [P, 1]), sb("rs1", [P, 1])
        st2, mv2, ve2, rs2 = sb("st2", [P, 6]), sb("mv2", [P, 2]), sb("ve2", [P, 1]), sb("rs2", [P, 1])
        msb, rr = sb("msb", [P, 4]), sb("rr", [P, 4])
        nmax, sums, rsum = sb("nmax", [P, 4, 2]), sb("sums", [P, 4, 2]), sb("rsum", [P, 4, 2])
        xlT = sb("xlT", [P, NC, B])
        xl2 = sb("xl2", [P, 2, NC, B], F32R)
        vlast = x1[0:B, :]

        off = [0]

        def part(n):
            off[0] += n
            return scr[:, off[0] - n:off[0]]

        kn, vn = [None, None], [None, None]
        for i in (1, 0):
            even_at = off[0]
            kn[i] = part(NC * KP).rearrange("p (c k) -> p c k", c=NC)
            vn[i] = part(KT * D).rearrange("p (t d) -> p t d", t=KT)
        cr = part(NC * KEYS).rearrange("p (c k) -> p c k", c=NC)
        sq = part(NC * TOK).rearrange("p (c k) -> p c k", c=NC)
        kH = kq[:, 0:2 * KP].rearrange("p (c k) -> p c k", c=2)
        kL = kq[:, 2 * KP:4 * KP].rearrange("p (c k) -> p c k", c=2)
        qH, qL = (kq[:, 4 * KP + i * NC * L:4 * KP + (i + 1) * NC * L].rearrange("p (c q) -> p c q", c=NC) for i in range(2))
        qz_at = 4 * KP + 2 * NC * L
        qzH, qzL = (kq[:, qz_at + i * 8 * L:qz_at + (i + 1) * 8 * L].rearrange("p (c j q) -> p c j q", c=2, j=4) for i in range(2))
        sqf = sq.rearrange("p c k -> p (c k)")
        ssum = sqf[:, 0:512]
        diag = sqf[:, 2 * TOK:2 * TOK + 512]
        probs_at = off[0]
        probs = part(4 * KT * P).rearrange("p (s k) -> p s k", s=4)
        probT = part(8 * KT * L).rearrange("p (s t q) -> p s t q", s=8, t=KT)
        assert off[0] <= 14304
        lg = scr[:, 14304:14368].rearrange("p (b e) -> p b e", b=B)
        xt = xr[:, 0:NC * L].rearrange("p (c q) -> p c q", c=NC)
        raw_w = [scr[:, probs_at + i * PIECE:probs_at + (i + 1) * PIECE] for i in range(2)]

        wH = lambda m: w2[:, 2 * m * PIECE:(2 * m + 1) * PIECE]
        wL = lambda m: w2[:, (2 * m + 1) * PIECE:(2 * m + 2) * PIECE]
        wv = lambda m: (wH(m).rearrange("p (c o) -> p c o", c=NC), wL(m).rearrange("p (c o) -> p c o", c=NC))
        halves = c2[:, :].rearrange("p (i n) -> p i n", i=2)
        cH, cL = ((halves[:, i, 0:NC * IMGE].rearrange("p (c k) -> p c k", c=NC),
                   halves[:, i, NC * IMGE:].rearrange("p (c k) -> p c k", c=NC)) for i in range(2))

        ex, gw = (scr[:, 64 * i:64 * i + 64].rearrange("p (b e) -> p b e", b=B) for i in range(1, 3))
        mx, sm, rc = (scr[:, 192 + 8 * i:200 + 8 * i] for i in range(3))
        top = scr[:, 256:320].rearrange("p (b e) -> p b e", b=B)
        tif, sel1, sel2, msk, slotm, tmp1, tmp2 = (
            scr[:, 320 + 64 * i:384 + 64 * i].rearrange("p (b e) -> p b e", b=B) for i in range(7))
        notbelow = scr[:, 768:768 + E * E].rearrange("p (a b) -> p a b", a=E)
        upto = scr[:, 1056:1056 + E * E].rearrange("p (a b) -> p a b", a=E)
        begun = scr[:, 1120:1120 + E * FULL].rearrange("p (a b) -> p a b", a=E)
        multiples, count = scr[:, 1200:1200 + FULL], scr[:, 1208:1208 + E]
        nblk, ends, base = scr[:, 840:848], scr[:, 848:856], scr[:, 856:864]
        slotf = scr[:, 864:880].rearrange("p (c b) -> p c b", c=2)
        cmpb = scr[:, 896:896 + 16 * E].rearrange("p (j e) -> p j e", e=E)
        ebf = scr[:, 1024:1040]
        topi = sb("topi", [P, B, E], U32)
        slotu = sb("slotu", [P, 2, B], U32)
        topw = sb("topw", [P, 2, B])
        rows_of = sb("rows_of", [P, 4])
        ebi = sb("ebi", [1, 16], I32)

        off[0] = even_at
        raw = [part(PIECE) for _ in range(4)]
        back = scr[:, off[0]:off[0] + 6 * D].rearrange("p (b d) -> p b d", b=6)
        rows_n = [back[:, i, :] for i in range(6)] + [xb, x1]
        xs = part(2 * D).rearrange("p (t d) -> p t d", t=2)
        ys = part(2 * D).rearrange("p (t d) -> p t d", t=2)
        gel = part(4 * BLOCK).rearrange("p (s n) -> p s n", s=4)
        assert even_at + 3 * PIECE <= probs_at and off[0] <= 14304
        EH = [w2[:, i * PIECE:(i + 1) * PIECE] for i in range(4)]
        EL = [w2[:, (4 + i) * PIECE:(5 + i) * PIECE] for i in range(4)]
        hH = [w2[:, (8 + 2 * i) * PIECE:(9 + 2 * i) * PIECE].rearrange("p (c n) -> p c n", c=8) for i in range(2)]
        hL = [w2[:, (9 + 2 * i) * PIECE:(10 + 2 * i) * PIECE].rearrange("p (c n) -> p c n", c=8) for i in range(2)]
        xTH = c2[:, 0:1024].rearrange("p (c n) -> p c n", c=NC)
        xTL = c2[:, 1024:2048].rearrange("p (c n) -> p c n", c=NC)
        b3s = xn
        rows_y = [scr[:, even_at + i * D:even_at + (i + 1) * D] for i in range(12)] + [xs[:, 0, :], xs[:, 1, :]] + [
            gel[:, 2 * i:2 * i + 2, :].rearrange("p s n -> p (s n)") for i in range(2)]
        rows_x = [scr[:, i * D:(i + 1) * D] for i in range(5)] + [ys[:, 0, :], ys[:, 1, :], xb]

        tiles = psum("tiles", [P, 3, 512])
        scores = psum("scores", [P, 2, 512])
        ptb = psum("ptb", [P, 2, 512])
        pvb = psum("pvb", [P, 512])
        hid = [tiles[:, 0, :], tiles[:, 1, :], tiles[:, 2, :], pvb[:, :]]
        xTb = scores
        yb = ptb

        S = {n: sem(n) for n in (
            "vec_in", "small_in", "aggr", "rows_done", "held", "experts_over", "wh_done", "wl_done", "xl_in", "xlh", "xll", "consts", "zeroed", "zero_stored",
            "vbias_done", "nq_done", "vlast_mm", "vlast_sb", "vlast_out",
            "x_in", "c_in", "ch_done", "cl_done", "xr_in", "xr_ob", "ln1_stats", "ln1_mv", "ln1_var", "ln1_rstd", "xn_done",
            "ln2_stats", "ln2_mv", "ln2_var", "ln2_rstd", "xh_done",
            "squares", "sum_a", "sum_b", "r_done", "diag_done", "q_done", "k_done", "qz_done", "qh_done", "ql_done", "kh_done", "kl_done", "rows_stored", "rows_in",
            "vrow_in", "s_ready", "max_done", "exp_done", "rsum_done", "p_ready", "t_ready", "pt_done",
            "pv_ready", "ah_done", "al_done", "x1_stored",
            "xg_done", "gate_in", "lg_done", "xt_done", "gate_ready", "route", "g_exp", "rank_ready", "slotu_done", "slots_done", "scattered", "b3_in",
            "eh_done", "el_done", "y_piece", "hid_ready", "gel_done", "hh_done", "hl_done",
            "xs_in", "xT_ready", "xTh_done", "xTl_done", "y_sb", "y_out", "x1_in", "fin_a", "fin_b", "out_done")}
        tile_ready = [sem(f"tile_ready{i}") for i in range(3)]
        tile_free = [sem(f"tile_free{i}") for i in range(3)]

        wraw_in = [sem(f"wraw_in{i}") for i in range(2)]
        raw_in = [sem(f"raw_in{i}") for i in range(4)]
        fin_in = [sem(f"fin_in{i}") for i in range(B)]

        def taken(eng, name, b):
            bank, cnt = tile_use(name, b)
            eng.wait_ge(tile_free[bank], cnt + 1)

        block = ctx.enter_context(nc.Block())

        def bodies(eng, body):
            body(-1, 1)
            body(FIRST, 0)
            with eng.Fori(0, (B - 2) // 2) as i:
                body(2 * i + 1, 1)
                body(2 * i + 2, 0)
            body(LAST, 1)
            body(DONE, 0)

        fixed = lambda b, v: isinstance(b, int) and b == v
        has_prep = lambda b: not (fixed(b, LAST) or fixed(b, DONE))
        has_tail = lambda b: not (fixed(b, -1) or fixed(b, FIRST))
        has_heads = lambda b: not (fixed(b, -1) or fixed(b, DONE))
        has = lambda name, b: {"o": has_tail, "v2": has_heads}.get(name, has_prep)(b)

        def split_ctx(act, n, i):
            act.wait_ge(S["c_in"], 16 * n)
            act.activation(cH[i], cr[:, :, PARTS[i]], ACT.Copy).then_inc(S["ch_done"], 1)

        @block.sync
        def _(sp):
            sp.dma_start(vec[:, :, :], vecs).then_inc(S["vec_in"], 16)
            for i, m in enumerate(ORDER):
                if i >= 2:
                    sp.wait_ge(S["wh_done"], i - 1)
                    sp.wait_ge(S["wl_done"], i - 1)
                sp.dma_start(raw_w[i % 2], wT[m]).then_inc(wraw_in[i % 2], 16)
                if i == 0:
                    sp.dma_start(cr, ctxT[0]).then_inc(S["c_in"], 16)
                if i == 1:
                    sp.dma_start(xb[0:L, :], x[0]).then_inc(S["x_in"], 16)
                    sp.dma_start(xlT[:, :, :], ctx_last).then_inc(S["xl_in"], 16)

            def body(b, p):
                if has_prep(b):
                    if not isinstance(b, int) or b < LAST - 1:
                        sp.wait_ge(S["ch_done"], 2 * (b + 2))
                        sp.wait_ge(S["cl_done"], 2 * (b + 2))
                        sp.dma_start(cr, ctxT[bass.ds(b + 2, 1)].rearrange("a p c k -> (a p) c k")).then_inc(S["c_in"], 16)
                        sp.wait_ge(S["xn_done"], b + 2)
                        sp.dma_start(xb[0:L, :], x[bass.ds(b + 2, 1)].rearrange("a p d -> (a p) d")).then_inc(S["x_in"], 16)
                if fixed(b, -1):
                    sp.wait_ge(S["zeroed"], 1)
                    by_partition = slots_d.rearrange("(p r) d -> p r d", p=P)
                    for r in range(0, ROWS, B):
                        n = min(B, ROWS - r)
                        sp.dma_start(by_partition[:, r:r + n, :], xr[:, :].unsqueeze(1).to_broadcast([P, n, D])).then_inc(S["zero_stored"], 16)
                    sp.wait_ge(S["vlast_sb"], 1)
                    sp.dma_start(vlast_d, vlast).then_inc(S["vlast_out"], 16)
                    sp.wait_ge(S["vlast_out"], 16)
                if has_heads(b):
                    taken(sp, "v2", b)
                    sp.dma_start(vn[p][0:1, KT - 1, :], vlast_d[bass.ds(b, 1), :]).then_inc(S["vrow_in"], 16)
                if fixed(b, LAST):
                    sp.wait_ge(S["pv_ready"], NC * LAST)
                    sp.wait_ge(S["cl_done"], 2 * B)
                    sp.wait_ge(S["k_done"], NC * B)
                    for pc in range(3):
                        sp.dma_start(raw[pc], experts[0, pc]).then_inc(raw_in[pc], 16)
                if has_tail(b):
                    taken(sp, "o", b)
                    sp.dma_start(x1_d[bass.ds(b - 1, 1)].rearrange("a p d -> (a p) d"), x1[0:L, :]).then_inc(S["x1_stored"], 16)
                    if fixed(b, DONE):
                        sp.wait_ge(S["pv_ready"], NC * B)
                        sp.wait_ge(S["rows_stored"], 16 * LAST)
                        sp.dma_start(back[0:L], xn2_d[0:6].rearrange("b l d -> l b d")).then_inc(S["rows_in"], 16)
                        sp.dma_start(xb[0:L, :], xn2_d[6]).then_inc(S["rows_in"], 16)
                    else:
                        sp.wait_ge(S["xg_done"], b)
                        sp.dma_start(xn2_d[bass.ds(b - 1, 1)].rearrange("a p d -> (a p) d"), x1[0:L, :]).then_inc(S["rows_stored"], 16)
                if has_heads(b):
                    if has_tail(b):
                        sp.wait_ge(S["gate_ready"], b)
                    if fixed(b, FIRST):
                        sp.wait_ge(S["zero_stored"], 16 * ZERO_STORES)
                    sp.dma_start(xr[0:L, :], x[bass.ds(b, 1)].rearrange("a p d -> (a p) d")).then_inc(S["xr_in"], 16)

            body(-1, 1)
            body(FIRST, 0)
            with sp.Fori(0, (B - 2) // 2 - 1) as i:
                body(2 * i + 1, 1)
                body(2 * i + 2, 0)
            body(LAST - 2, 1)
            body(LAST - 1, 0)
            body(LAST, 1)
            body(DONE, 0)

            sp.wait_ge(S["pv_ready"], NC * B)
            for pc in range(3, PIECES):
                if pc >= 4:
                    sp.wait_ge(S["eh_done"], pc - 3)
                    sp.wait_ge(S["el_done"], pc - 3)
                sp.dma_start(raw[pc % 4], experts[0, pc]).then_inc(raw_in[pc % 4], 16)
            sp.wait_ge(S["scattered"], 16 * 2 * B)
            sp.dma_start(xs, slots_d[0:BLOCK, :].rearrange("(t p) d -> p t d", p=P)).then_inc(S["xs_in"], 16)
            sp.dma_start(b3s[:, :], b3[0:1, :].rearrange("e d -> (e d)").partition_broadcast(P)).then_inc(S["b3_in"], 16)
            used = sp.value_load(ebi[0:1, MAX_BLOCKS + 1:MAX_BLOCKS + 2], min_val=1, max_val=MAX_BLOCKS)
            with sp.Fori(0, MAX_BLOCKS) as j:
                with sp.If(j < used):
                    e = sp.value_load(ebi[0:1, bass.ds(j + 1, 1)], min_val=0, max_val=E - 1)
                    sp.wait_ge(S["xT_ready"], j + 1)
                    sp.dma_start(xs, slots_d[bass.ds((j + 1) * BLOCK, BLOCK), :].rearrange("(t p) d -> p t d", p=P)).then_inc(S["xs_in"], 16)
                    for pc in range(PIECES):
                        if pc == PIECES - 1:
                            sp.wait_ge(S["y_sb"], j + 1)
                            sp.dma_start(slots_d[bass.ds(j * BLOCK, BLOCK), :].rearrange("(t p) d -> p t d", p=P), ys).then_inc(S["y_out"], 16)
                            sp.dma_start(b3s[:, :], b3[bass.ds(e, 1), :].rearrange("e d -> (e d)").partition_broadcast(P)).then_inc(S["b3_in"], 16)
                        sp.wait_ge(S["eh_done"], PIECES * j + pc + 5)
                        sp.wait_ge(S["el_done"], PIECES * j + pc + 5)
                        sp.dma_start(raw[pc % 4], experts[bass.ds(e, 1), pc].rearrange("a p n -> (a p) n")).then_inc(raw_in[pc % 4], 16)
                    sp.wait_ge(S["y_out"], 16 * (j + 1))
                    sp.sem_inc(S["held"], 1)
            for slot in range(3):
                sp.wait_ge(raw_in[slot], 16 * 2 * (used + 1))
                sp.sem_inc(S["held"], 1)
            for name, value in (("xs_in", 16 * (used + 1)), ("xT_ready", used + 1), ("el_done", PIECES * used + 3),
                                ("hl_done", 16 * used + 4), ("y_out", 16 * used)):
                sp.wait_ge(S[name], value)
                sp.sem_inc(S["held"], 1)
            sp.sem_inc(S["experts_over"], 1)
            for b in range(B):
                sp.dma_start(rows_x[b][0:L, :], x1_d[b]).then_inc(S["x1_in"], 16)
            for b in range(B):
                sp.wait_ge(S["fin_b"], b + 1)
                sp.dma_start(out[b], rows_x[b][0:L, :]).then_inc(S["out_done"], 16)
            sp.wait_ge(raw_in[3], 16 * 2 * (used + 1))
            sp.sem_inc(S["held"], 1)
            sp.wait_ge(S["b3_in"], 16 * (used + 1))
            sp.sem_inc(S["held"], 1)
            sp.wait_ge(S["out_done"], 16 * B)

        @block.gpsimd
        def _(pool):
            pool.iota(iota[:, :], [[1, P]], base=0, channel_multiplier=0, allow_small_or_imprecise_dtypes=True)
            pool.iota(pidx[:, :], [[1, 1]], base=0, channel_multiplier=1, allow_small_or_imprecise_dtypes=True)
            pool.memset(ones[:, :], 1.0)
            pool.memset(mhalf[:, :], -0.5)
            pool.memset(lneps[:, :], LN_EPS).then_inc(S["consts"], 1)
            pool.dma_start(obr[:, :], o_b.rearrange("(a d) -> a d", a=1).partition_broadcast(P)).then_inc(S["small_in"], 16)
            pool.dma_start(wgs[:, :, :], wg).then_inc(S["small_in"], 16)
            pool.dma_start(bgr[:, :], bg.rearrange("(a d) -> a d", a=1).partition_broadcast(P)).then_inc(S["small_in"], 16)
            pool.dma_start(b12s[:, :, :], b12).then_inc(S["small_in"], 16)
            pool.memset(xr[:, :], 0.0).then_inc(S["zeroed"], 1)
            pool.wait_ge(S["consts"], 1)

            def rstd(b_count, mv, ve, rs, tag):
                pool.wait_ge(S[tag + "_mv"], b_count)
                pool.tensor_tensor(ve[0:L, :], mv[0:L, 1:2], lneps[0:L, :], ALU.add).then_inc(S[tag + "_var"], 1)
                pool.wait_ge(S[tag + "_var"], b_count)
                pool.tensor_tensor(rs[0:L, :], ve[0:L, :], mhalf[0:L, 0:1], ALU.pow).then_inc(S[tag + "_rstd"], 1)

            def head_queries(b, p, c):
                if not (fixed(b, 0) and c < 2):
                    pool.wait_ge(S["s_ready"], NH * b + 4 * (c - 1))
                for dst, src, ready in ((qzH, qH, "qh_done"), (qzL, qL, "ql_done")):
                    pool.wait_ge(S[ready], b + 1)
                    last = pool.tensor_tensor(dst[:, c % 2, :, :], src[:, c:c + 1, :].bitcast(F32).to_broadcast([P, 4, L]),
                                              rows_of[:, :].unsqueeze(2).to_broadcast([P, 4, L]), ALU.mult)
                last.then_inc(S["qz_done"], 1)

            def body(b, p):
                if has_heads(b):
                    head_queries(b, p, 1)
                if has_prep(b):
                    rstd(b + 2, mv1, ve1, rs1, "ln1")
                if has_heads(b):
                    head_queries(b, p, 2)
                if has_tail(b):
                    rstd(b, mv2, ve2, rs2, "ln2")
                if has_heads(b):
                    head_queries(b, p, 3)
                if has_prep(b):
                    n = b + 1
                    taken(pool, "ms", b)
                    pool.tensor_tensor(rr[:, :], msb[:, :], mhalf[:, :], ALU.pow).then_inc(S["r_done"], 1)
                    pool.wait_ge(S["r_done"], n + 1)
                    if fixed(b, -1):
                        pool.wait_ge(S["nq_done"], 3)
                    pool.tensor_tensor(diag.rearrange("p (t n) -> p t n", t=4), ident[:, :].unsqueeze(1).to_broadcast([P, 4, P]),
                                       rr[:, :].unsqueeze(2).to_broadcast([P, 4, P]), ALU.mult).then_inc(S["diag_done"], 1)
                    head_queries(b + 1, 1 - p, 0)
                if has_heads(b):
                    if fixed(b, FIRST):
                        pool.wait_ge(S["small_in"], 64)
                    pool.wait_ge(S["xr_in"], 16 * (b + 1))
                    pool.tensor_tensor(xr[0:L, :], xr[0:L, :], obr[0:L, :], ALU.add).then_inc(S["xr_ob"], 1)

            bodies(pool, body)

            pool.wait_ge(S["slotu_done"], 1)
            pool.wait_ge(S["zero_stored"], 16 * ZERO_STORES)
            pool.wait_ge(S["rows_in"], 32)
            for c in range(2):
                for b in range(B):
                    pool.indirect_dma_start(
                        out=slots_d, out_offset=bass.IndirectOffsetOnAxis(ap=slotu[0:L, c, b:b + 1], axis=0),
                        in_=rows_n[b][0:L, :], in_offset=None).then_inc(S["scattered"], 16)
            pool.wait_ge(S["experts_over"], 1)
            for b in range(B):
                for c in range(2):
                    pool.indirect_dma_start(
                        out=rows_y[2 * b + c][0:L, :], out_offset=None, in_=slots_d,
                        in_offset=bass.IndirectOffsetOnAxis(ap=slotu[0:L, c, b:b + 1], axis=0)).then_inc(fin_in[b], 16)

        @block.scalar
        def _(act):
            def split_weights(i):
                act.wait_ge(wraw_in[i % 2], 16 * (i // 2 + 1))
                act.activation(wH(ORDER[i]), raw_w[i % 2], ACT.Copy).then_inc(S["wh_done"], 1)

            split_weights(0)
            split_ctx(act, 1, 0)
            split_ctx(act, 1, 1)
            split_weights(1)
            act.wait_ge(S["xl_in"], 16)
            act.activation(xl2[:, 0, :, :], xlT[:, :, :], ACT.Copy).then_inc(S["xlh"], 1)

            def stage(name, b, p):
                n = b + 1
                if name == "o":
                    return
                bank, cnt = tile_use(name, b)
                if name == "xT":
                    act.wait_ge(tile_ready[bank], cnt + 1)
                    act.activation(xs2[:, 0, :, :], tiles[:, bank, 0:NC * L].rearrange("p (c q) -> p c q", c=NC),
                                   ACT.Copy).then_inc(S["xh_done"], 1)
                if name in ("v0", "v1", "v2"):
                    t = int(name[1])
                    rows = P if t < 2 else TAIL
                    act.wait_ge(tile_ready[bank], cnt + 1)
                    act.activation(vn[p if t == 2 else 1 - p][0:rows, t, :], tiles[0:rows, bank, :], ACT.Copy).then_inc(tile_free[bank], 1)
                if name == "q":
                    taken(act, "q", b)
                    act.activation(sq[:, :, 0:L], qn[:, 1 - p, :, :], ACT.Square).then_inc(S["squares"], 1)
                if name in ("qt", "kt"):
                    rows = L if name == "qt" else TXT
                    act.wait_ge(tile_ready[bank], cnt + 1)
                    act.activation(xn[0:rows, :], tiles[0:rows, bank, :], ACT.Copy).then_inc(tile_free[bank], 1)
                if name in ("k0", "k1", "k2", "k3"):
                    act.wait_ge(tile_ready[bank], cnt + 1)
                    c = int(name[1])
                    bias = vec[:, V_KIB, c:c + 1]
                    act.activation(sq[:, c, L:L + IMG], tiles[:, bank, 0:IMG], ACT.Square, bias=bias).then_inc(S["squares"], 1)
                    act.activation(kn[1 - p][:, c, 0:IMG], tiles[:, bank, 0:IMG], ACT.Identity, bias=bias).then_inc(tile_free[bank], 1)
                if name == "kx":
                    taken(act, "kx", b)
                    act.activation(sq[:, :, L + IMG:TOK], kn[1 - p][:, :, IMG:KEYS], ACT.Square).then_inc(S["squares"], 1)

            def split_keys(b, p, c):
                act.wait_ge(S["k_done"], NC * b + c + 1)
                if not (fixed(b, 0) and c < 2):
                    act.wait_ge(S["s_ready"], NH * b + 4 * (c - 1))
                act.activation(kH[:, c % 2, :], kn[p][:, c, :], ACT.Copy).then_inc(S["kh_done"], 1)

            def split_queries(b, p):
                act.wait_ge(S["q_done"], b + 1)
                if not fixed(b, 0):
                    act.wait_ge(S["qz_done"], NC * b)
                act.activation(qH, qn[:, p, :, :], ACT.Copy).then_inc(S["qh_done"], 1)

            def weigh(b, p, h):
                s = h % 4
                act.wait_ge(S["max_done"], NH * b + h + 1)
                act.activation(probs[0:L, s, 0:IMG], scores[0:L, h % 2, 0:IMG], ACT.Exp,
                               bias=nmax[0:L, s, 0:1], accum_out=sums[0:L, s, 0:1])
                act.activation(probs[0:L, s, IMG:KEYS], scores[0:L, h % 2, IMG:KEYS], ACT.Exp,
                               bias=nmax[0:L, s, 1:2], accum_out=sums[0:L, s, 1:2]).then_inc(S["exp_done"], 1)

            def take_transposed(b, h):
                act.wait_ge(S["t_ready"], NH * b + h + 1)
                if not (fixed(b, 0) and h < 8):
                    act.wait_ge(S["pv_ready"], NC * b + h // 4 - 1)
                act.activation(probT[:, h % 8, :, :], ptb[:, h % 2, 0:KT * L].rearrange("p (t q) -> p t q", t=KT),
                               ACT.Copy).then_inc(S["pt_done"], 1)

            def take_attended(b, g):
                act.wait_ge(S["pv_ready"], NC * b + g + 1)
                act.activation(a2[:, 0, g, :], pvb[:, 0:L], ACT.Identity, bias=vbias[:, g:g + 1]).then_inc(S["ah_done"], 1)

            def convert(use, slot):
                act.wait_ge(raw_in[slot], 16 * (use + 1))
                act.activation(EH[slot], raw[slot], ACT.Copy).then_inc(S["eh_done"], 1)

            def body(b, p):
                for h in range(NH):
                    if h == 9 and has_tail(b):
                        act.wait_ge(S["gate_in"], b)
                        act.activation(xt, pvb[:, 0:NC * L].rearrange("p (c q) -> p c q", c=NC), ACT.Copy).then_inc(S["xt_done"], 1)
                    if h == 14 and has_prep(b):
                        split_queries(b + 1, 1 - p)
                        split_keys(b + 1, 1 - p, 0)
                    if fixed(b, -1) and h in WEIGHTS_AT:
                        split_weights(WEIGHTS_AT[h])
                    if h == 2 and has_tail(b):
                        take_attended(b - 1, 3)
                    if has_heads(b):
                        weigh(b, p, h)
                    if h < LAG:
                        if has_tail(b):
                            take_transposed(b - 1, NH - LAG + h)
                    elif has_heads(b):
                        take_transposed(b, h - LAG)
                    if h in (6, 10, 14) and has_heads(b):
                        take_attended(b, (h - 6) // 4)
                    if h in KEYS_HIGH_AT and has_heads(b):
                        split_keys(b, p, KEYS_HIGH_AT[h])
                    if h == 0 and has_prep(b) and not fixed(b, -1):
                        split_ctx(act, b + 2, 0)
                    for name in STAGE_AT[h]:
                        if has(name, b):
                            stage(name, b, p)
                    if h == 2 and has_prep(b) and not fixed(b, -1):
                        split_ctx(act, b + 2, 1)
                    if fixed(b, DONE) and h == 3:
                        for pc in range(3):
                            convert(0, pc)
                    if fixed(b, -1) and h == 15:
                        act.wait_ge(S["vlast_mm"], 1)
                        act.activation(vlast, pvb[0:B, :], ACT.Copy).then_inc(S["vlast_sb"], 1)
                        act.wait_ge(S["vbias_done"], 1)

            bodies(act, body)

            act.wait_ge(S["route"], 3)
            act.activation(ex[0:L], lg[0:L], ACT.Exp).then_inc(S["g_exp"], 1)

            def split_input(j):
                act.wait_ge(S["xT_ready"], j + 1)
                act.activation(xTH, xTb[:, :, :].rearrange("p b (c n) -> p (b c) n", n=BLOCK), ACT.Copy).then_inc(S["xTh_done"], 1)

            act.sem_inc(S["gel_done"], 4)
            convert(0, 3)
            act.wait_ge(S["slots_done"], 1)
            split_input(0)
            act.wait_ge(S["small_in"], 64)
            used = act.value_load(ebi[0:1, MAX_BLOCKS + 1:MAX_BLOCKS + 2], min_val=1, max_val=MAX_BLOCKS)
            with act.Fori(0, MAX_BLOCKS) as j:
                with act.If(j < used):
                    e = act.value_load(ebi[0:1, bass.ds(j, 1)], min_val=0, max_val=E - 1)
                    for pc in range(PIECES):
                        if pc < 6:
                            for m in CHUNKS[pc]:
                                act.wait_ge(S["hid_ready"], 16 * j + m + 1)
                                act.wait_ge(S["hl_done"], 16 * j + m + 1)
                                act.activation(gel[:, m % 4, :], hid[m % 4][:, 0:BLOCK], ACT.Gelu,
                                               bias=b12s[:, bass.ds(e, 1), m:m + 1].rearrange("p a o -> p (a o)")
                                               ).then_inc(S["gel_done"], 1)
                        if pc < 6:
                            act.wait_ge(S["hid_ready"], 16 * j + CHUNKS[pc][-1] + 1)
                        else:
                            act.wait_ge(S["y_piece"], 2 * j + pc - 5)
                        convert(2 * j + pc // 4 + 1, pc % 4)
                        if pc == 5:
                            split_input(j + 1)

        @block.vector
        def _(dve):
            dve.wait_ge(S["consts"], 1)
            dve.memset(rows_of[:, :], 0.0).then_inc(S["rows_done"], 1)
            dve.wait_ge(S["rows_done"], 1)
            for i in range(2):
                dve.memset(kn[i][:, :, KEYS:KP], 0.0)
            for j in range(4):
                dve.memset(rows_of[HD * j:HD * j + HD, j:j + 1], 1.0)
            dve.tensor_scalar(ident[:, :], iota[:, :], pidx[:, 0:1], None, ALU.is_equal).then_inc(S["nq_done"], 1)
            dve.tensor_scalar(upper[:, :], iota[:, :], pidx[:, 0:1], None, ALU.is_gt).then_inc(S["nq_done"], 1)
            dve.wait_ge(S["vec_in"], 16)
            dve.tensor_scalar(nq[:, :], vec[:, V_NQ, :], float(HD) ** -0.5, None, ALU.mult).then_inc(S["nq_done"], 1)
            dve.tensor_tensor(vbias[:, :], vec[:, V_VB, :], vec[:, V_VIB, :], ALU.add).then_inc(S["vbias_done"], 1)

            def split_ctx_low(n, i):
                dve.wait_ge(S["ch_done"], 2 * n - 1 + i)
                dve.tensor_tensor(cL[i], cr[:, :, PARTS[i]], cH[i].bitcast(F32), ALU.subtract).then_inc(S["cl_done"], 1)

            def ln_stats(count, src, st, mv, tag):
                dve.bn_stats(st[0:L, :], src[0:L, :]).then_inc(S[tag + "_stats"], 1)
                dve.wait_ge(S[tag + "_stats"], count)
                dve.sem_inc(S["aggr"], 1)
                dve.bn_aggr(mv[0:L, :], st[0:L, :]).then_inc(S[tag + "_mv"], 1)

            def ln_apply(count, dst, src, mv, rs, tag, done):
                dve.wait_ge(S[tag + "_rstd"], count)
                dve.tensor_scalar(dst, src[0:L, :], mv[0:L, 0:1], rs[0:L, 0:1], ALU.subtract, ALU.mult).then_inc(S[done], 1)

            def split_weights(i):
                dve.wait_ge(S["wh_done"], i + 1)
                dve.tensor_tensor(wL(ORDER[i]), raw_w[i % 2], wH(ORDER[i]).bitcast(F32), ALU.subtract).then_inc(S["wl_done"], 1)

            split_weights(0)
            split_ctx_low(1, 0)
            split_ctx_low(1, 1)
            dve.wait_ge(S["x_in"], 16)
            ln_stats(1, xb, st1, mv1, "ln1")
            split_weights(1)
            ln_apply(1, xn[0:L, :], xb, mv1, rs1, "ln1", "xn_done")
            dve.wait_ge(S["xlh"], 1)
            dve.tensor_tensor(xl2[:, 1, :, :], xlT[:, :, :], xl2[:, 0, :, :].bitcast(F32), ALU.subtract).then_inc(S["xll"], 1)

            def normalise_keys(tile, p, c):
                k = kn[p][:, c, :]
                dve.scalar_tensor_tensor(k[:, 0:IMG], k[:, 0:IMG], vec[:, V_NKI, c:c + 1], tile[:, L:L + IMG], ALU.mult, ALU.mult)
                dve.scalar_tensor_tensor(k[:, IMG:KEYS], k[:, IMG:KEYS], vec[:, V_NK, c:c + 1], tile[:, L + IMG:TOK],
                                         ALU.mult, ALU.mult).then_inc(S["k_done"], 1)

            def stage(name, b, p):
                n = b + 1
                bank, cnt = tile_use(name, b)
                tile = tiles[:, bank, :]
                if name in ("v0", "v1", "v2", "qt", "kt", "k0", "k1", "k2", "k3"):
                    return
                if name == "o":
                    dve.wait_ge(tile_ready[bank], cnt + 1)
                    dve.wait_ge(S["xr_ob"], b)
                    dve.tensor_tensor(x1[0:L, :], tile[0:L, :], xr[0:L, :], ALU.add).then_inc(tile_free[bank], 1)
                    return
                if name == "rb":
                    dve.wait_ge(tile_ready[bank], cnt + 1)
                    taken(dve, "k3", b)
                    for c in range(NC):
                        q = qn[:, 1 - p, c, :]
                        last = dve.scalar_tensor_tensor(q, q, nq[:, c:c + 1], tile[:, 0:L], ALU.mult, ALU.mult)
                    last.then_inc(S["q_done"], 1)
                    normalise_keys(tile, 1 - p, 0)
                    return
                if name == "xT":
                    dve.wait_ge(S["xh_done"], n + 1)
                    dve.tensor_tensor(xs2[:, 1, :, :], tile[:, 0:NC * L].rearrange("p (c q) -> p c q", c=NC),
                                      xs2[:, 0, :, :].bitcast(F32), ALU.subtract).then_inc(tile_free[bank], 1)
                    return
                dve.wait_ge(tile_ready[bank], cnt + 1)
                if name == "q":
                    dve.tensor_tensor(qn[:, 1 - p, :, :], tile[:, 0:NC * L].rearrange("p (c q) -> p c q", c=NC),
                                      vec[:, V_QB, :].unsqueeze(2).to_broadcast([P, NC, L]), ALU.add).then_inc(tile_free[bank], 1)
                elif name == "ms":
                    dve.tensor_scalar(msb[:, :], tile[:, 0:4], 1.0 / D, RMS_EPS, ALU.mult, ALU.add).then_inc(tile_free[bank], 1)
                elif name == "kx":
                    dve.tensor_tensor(kn[1 - p][:, :, IMG:KEYS], tile[:, 0:NC * TXT].rearrange("p (c k) -> p c k", c=NC),
                                      vec[:, V_KB, :].unsqueeze(2).to_broadcast([P, NC, TXT]), ALU.add).then_inc(tile_free[bank], 1)

            def split_keys_low(b, p, c):
                dve.wait_ge(S["kh_done"], NC * b + c + 1)
                dve.tensor_tensor(kL[:, c % 2, :], kn[p][:, c, :], kH[:, c % 2, :].bitcast(F32), ALU.subtract).then_inc(S["kl_done"], 1)

            def split_queries_low(b, p):
                dve.wait_ge(S["qh_done"], b + 1)
                dve.tensor_tensor(qL, qn[:, p, :, :], qH.bitcast(F32), ALU.subtract).then_inc(S["ql_done"], 1)

            def maxima(b, h):
                dve.wait_ge(S["s_ready"], NH * b + h + 1)
                dve.tensor_reduce(nmax[0:L, h % 4, 0:1], scores[0:L, h % 2, 0:IMG], AX.X, ALU.max, negate=True)
                dve.tensor_reduce(nmax[0:L, h % 4, 1:2], scores[0:L, h % 2, IMG:KEYS], AX.X, ALU.max, negate=True).then_inc(S["max_done"], 1)

            def normalise(b, h):
                s = h % 4
                dve.wait_ge(S["exp_done"], NH * b + h + 1)
                dve.reciprocal(rsum[0:L, s, :], sums[0:L, s, :]).then_inc(S["rsum_done"], 1)
                dve.wait_ge(S["rsum_done"], NH * b + h + 1)
                dve.tensor_scalar(probs[0:L, s, 0:IMG], probs[0:L, s, 0:IMG], rsum[0:L, s, 0:1], None, ALU.mult)
                dve.tensor_scalar(probs[0:L, s, IMG:KEYS], probs[0:L, s, IMG:KEYS], rsum[0:L, s, 1:2], None,
                                  ALU.mult).then_inc(S["p_ready"], 1)

            def attended_low(b, g):
                dve.wait_ge(S["ah_done"], NC * b + g + 1)
                dve.scalar_tensor_tensor(a2[:, 1, g, :], pvb[:, 0:L], vbias[:, g:g + 1], a2[:, 0, g, :].bitcast(F32),
                                         ALU.add, ALU.subtract).then_inc(S["al_done"], 1)

            def convert(q, slot):
                dve.wait_ge(S["eh_done"], q + 1)
                dve.tensor_tensor(EL[slot], raw[slot], EH[slot].bitcast(F32), ALU.subtract).then_inc(S["el_done"], 1)

            def body(b, p):
                for h in range(NH):
                    if fixed(b, -1) and h in WEIGHTS_AT:
                        split_weights(WEIGHTS_AT[h])
                    if fixed(b, -1) and h == 15:
                        dve.wait_ge(S["wl_done"], 6)
                        dve.memset(probs[:, :, KEYS:KT * P], 0.0)
                    if h == 12 and has_prep(b):
                        dve.wait_ge(S["squares"], (NC + 2) * (b + 2))
                        dve.tensor_tensor(sq[:, 1, :], sq[:, 1, :], sq[:, 3, :], ALU.add).then_inc(S["sum_a"], 1)
                        dve.wait_ge(S["sum_a"], 2 * (b + 2))
                        dve.tensor_tensor(sq[:, 0, :], sq[:, 0, :], sq[:, 1, :], ALU.add).then_inc(S["sum_b"], 1)
                    if has_heads(b):
                        maxima(b, h)
                    if h == 0:
                        if has_tail(b):
                            normalise(b - 1, NH - 1)
                    elif has_heads(b):
                        normalise(b, h - 1)
                    if h == 14 and has_prep(b):
                        split_queries_low(b + 1, 1 - p)
                        split_keys_low(b + 1, 1 - p, 0)
                    if h in (6, 10, 14) and has_heads(b):
                        attended_low(b, (h - 6) // 4)
                    if h in KEYS_AT and (has_prep if h > 1 else has_heads)(b):
                        c, step = KEYS_AT[h]
                        bank = tile_use("rb", b + step)[0]
                        normalise_keys(tiles[:, bank, :], p if step else 1 - p, c)
                        if c == NC - 1:
                            dve.wait_ge(S["k_done"], NC * (b + 1))
                            dve.sem_inc(tile_free[bank], 1)
                    if h in KEYS_LOW_AT and has_heads(b):
                        split_keys_low(b, p, KEYS_LOW_AT[h])
                    if h in (1, 3) and has_prep(b) and not fixed(b, -1):
                        split_ctx_low(b + 2, h // 2)
                    if h == 2 and has_tail(b):
                        attended_low(b - 1, 3)
                    if h == 2 and has_prep(b) and not fixed(b, -1):
                        dve.wait_ge(S["x_in"], 16 * (b + 2))
                        ln_stats(b + 2, xb, st1, mv1, "ln1")
                    if h == 3 and has_prep(b) and not fixed(b, -1):
                        ln_apply(b + 2, xn[0:L, :], xb, mv1, rs1, "ln1", "xn_done")
                    if h == 5 and has_prep(b):
                        stage("xT", b, p)
                    if h == 5 and has_tail(b):
                        dve.wait_ge(tile_free[tile_use("o", b)[0]], tile_use("o", b)[1] + 1)
                        ln_stats(b, x1, st2, mv2, "ln2")
                    for name in STAGE_AT[h]:
                        if name != "xT" and has(name, b):
                            stage(name, b, p)
                    if h == 11 and has_prep(b):
                        dve.wait_ge(S["squares"], (NC + 2) * (b + 2) - 1)
                        dve.tensor_tensor(sq[:, 0, :], sq[:, 0, :], sq[:, 2, :], ALU.add).then_inc(S["sum_a"], 1)
                    if h == 7 and has_tail(b):
                        dve.wait_ge(S["x1_stored"], 16 * b)
                        ln_apply(b, x1[0:L, :], x1, mv2, rs2, "ln2", "xg_done")
                    if h == 15 and has_tail(b) and not fixed(b, DONE):
                        dve.wait_ge(S["rows_stored"], 16 * b)
                    if fixed(b, DONE) and h in (2, 3, 8):
                        convert((2, 3, 8).index(h), (2, 3, 8).index(h))
                    if h == 12 and has_tail(b):
                        dve.wait_ge(S["gate_ready"], b)
                        dst = lg[0:L, b - 1:b, :] if fixed(b, LAST) or fixed(b, DONE) else lg[0:L, bass.ds(b - 1, 1), :]
                        dve.tensor_tensor(dst, pvb[0:L, 0:E].unsqueeze(1), bgr[0:L, :].unsqueeze(1), ALU.add).then_inc(S["lg_done"], 1)
                    if h == 0 and fixed(b, FIRST):
                        dve.wait_ge(S["small_in"], 64)

            bodies(dve, body)

            steps = [0]

            def after(ins):
                steps[0] += 1
                ins.then_inc(S["route"], 1)
                dve.wait_ge(S["route"], steps[0])

            bc = lambda ap, shape: ap.to_broadcast(shape)
            full = [L, B, E]
            number8 = iota[:, 0:E]
            dve.tensor_tensor(notbelow, bc(number8.unsqueeze(2), [P, E, E]), bc(number8.unsqueeze(1), [P, E, E]), ALU.is_ge)
            after(dve.tensor_scalar(multiples, iota[:, 0:FULL], float(BLOCK), None, ALU.mult))
            dve.wait_ge(S["lg_done"], B)
            after(dve.tensor_reduce(mx[0:L, :], lg[0:L], AX.X, ALU.max))
            after(dve.tensor_tensor(lg[0:L], lg[0:L], bc(mx[0:L, :].unsqueeze(2), full), ALU.subtract))
            dve.wait_ge(S["g_exp"], 1)
            after(dve.tensor_reduce(sm[0:L, :], ex[0:L], AX.X, ALU.add))
            after(dve.reciprocal(rc[0:L, :], sm[0:L, :]))
            after(dve.tensor_tensor(gw[0:L], ex[0:L], bc(rc[0:L, :].unsqueeze(2), full), ALU.mult))
            for b in range(B):
                last = dve.max(top[0:L, b, :], gw[0:L, b, :])
            after(last)
            for b in range(B):
                last = dve.max_index(topi[0:L, b, :], top[0:L, b, :], gw[0:L, b, :])
            after(last)
            after(dve.tensor_copy(tif[0:L], topi[0:L, :, :]))
            dve.tensor_copy(topw[0:L, 0, :], top[0:L, :, 0])
            dve.tensor_copy(topw[0:L, 1, :], top[0:L, :, 1])
            number = bc(iota[0:L, 0:E].unsqueeze(1), full)
            dve.tensor_tensor(sel1[0:L], bc(tif[0:L, :, 0:1], full), number, ALU.is_equal)
            after(dve.tensor_tensor(sel2[0:L], bc(tif[0:L, :, 1:2], full), number, ALU.is_equal))
            after(dve.tensor_tensor(msk[0:L], sel1[0:L], sel2[0:L], ALU.add))
            dve.wait_ge(S["rank_ready"], 1)
            after(dve.tensor_reduce(count, ptb[:, 0, 0:B * E].rearrange("p (b e) -> p e b", b=B), AX.X, ALU.add))
            after(dve.tensor_tensor(begun, bc(count.unsqueeze(2), [P, E, FULL]), bc(multiples.unsqueeze(1), [P, E, FULL]), ALU.is_gt))
            after(dve.tensor_reduce(nblk, begun, AX.X, ALU.add))
            after(dve.tensor_scalar(nblk[:, 0:1], nblk[:, 0:1], 1.0, None, ALU.max))
            after(dve.tensor_tensor(upto, notbelow, bc(nblk.unsqueeze(1), [P, E, E]), ALU.mult))
            after(dve.tensor_reduce(ends, upto, AX.X, ALU.add))
            after(dve.tensor_tensor(base, ends, nblk, ALU.subtract))
            after(dve.tensor_scalar(base, base, float(BLOCK), None, ALU.mult))
            after(dve.tensor_tensor(slotm[0:L], scores[0:L, 1, 0:B * E].rearrange("p (b e) -> p b e", b=B), bc(base[0:L, :].unsqueeze(1), full), ALU.add))
            dve.tensor_tensor(tmp1[0:L], slotm[0:L], sel1[0:L], ALU.mult)
            after(dve.tensor_tensor(tmp2[0:L], slotm[0:L], sel2[0:L], ALU.mult))
            dve.tensor_reduce(slotf[0:L, 0, :], tmp1[0:L], AX.X, ALU.add)
            after(dve.tensor_reduce(slotf[0:L, 1, :], tmp2[0:L], AX.X, ALU.add))
            dve.tensor_copy(slotu[0:L, :, :], slotf[0:L]).then_inc(S["slotu_done"], 1)
            after(dve.tensor_tensor(cmpb[0:1], bc(ends[0:1, :].unsqueeze(1), [1, 16, E]), bc(iota[0:1, 0:16].unsqueeze(2), [1, 16, E]), ALU.is_le))
            after(dve.tensor_reduce(ebf[0:1, :], cmpb[0:1], AX.X, ALU.add))
            after(dve.tensor_scalar(ebf[0:1, :], ebf[0:1, :], float(E - 1), None, ALU.min))
            after(dve.tensor_copy(ebf[0:1, MAX_BLOCKS + 1:MAX_BLOCKS + 2], ends[0:1, E - 1:E]))
            dve.tensor_copy(ebi[0:1, :], ebf[0:1, :]).then_inc(S["slots_done"], 1)

            def split_input(j):
                dve.wait_ge(S["xTh_done"], j + 1)
                dve.tensor_tensor(xTL, xTb[:, :, :].rearrange("p b (c n) -> p (b c) n", n=BLOCK), xTH.bitcast(F32), ALU.subtract).then_inc(S["xTl_done"], 1)

            convert(3, 3)
            dve.wait_ge(S["scattered"], 16 * 2 * B)
            dve.memset(gel[:, :, :], 0.0).then_inc(S["hl_done"], 4)
            split_input(0)
            used = dve.value_load(ebi[0:1, MAX_BLOCKS + 1:MAX_BLOCKS + 2], min_val=1, max_val=MAX_BLOCKS)
            with dve.Fori(0, MAX_BLOCKS) as j:
                with dve.If(j < used):
                    for pc in range(PIECES):
                        if pc < 6:
                            for m in CHUNKS[pc]:
                                lay, c = m // 8, m % 8
                                dve.wait_ge(S["gel_done"], 16 * j + m + 5)
                                dve.tensor_copy(hH[lay][:, c, :], gel[:, m % 4, :]).then_inc(S["hh_done"], 1)
                                dve.wait_ge(S["hh_done"], 16 * j + m + 1)
                                dve.tensor_tensor(hL[lay][:, c, :], gel[:, m % 4, :], hH[lay][:, c, :].bitcast(F32),
                                                  ALU.subtract).then_inc(S["hl_done"], 1)
                        if pc == PIECES - 1:
                            dve.wait_ge(S["y_piece"], 2 * j + 2)
                            dve.wait_ge(S["b3_in"], 16 * (j + 1))
                            dve.tensor_tensor(ys, yb[:, :, :], b3s[:, :].unsqueeze(1).to_broadcast([P, 2, D]), ALU.add).then_inc(S["y_sb"], 1)
                        convert(PIECES * j + pc + 4, pc % 4)
                        if pc == 5:
                            split_input(j + 1)

            for b in range(B):
                dve.wait_ge(fin_in[b], 32)
                if b == 0:
                    dve.wait_ge(S["x1_in"], 16 * B)
                row = rows_x[b][0:L, :]
                dve.scalar_tensor_tensor(row, rows_y[2 * b][0:L, :], topw[0:L, 0, b:b + 1], row, ALU.mult, ALU.add).then_inc(S["fin_a"], 1)
                dve.wait_ge(S["fin_a"], b + 1)
                dve.scalar_tensor_tensor(row, rows_y[2 * b + 1][0:L, :], topw[0:L, 1, b:b + 1], row, ALU.mult, ALU.add).then_inc(S["fin_b"], 1)

        @block.tensor
        def _(pe):
            def three(out, wh, wl, xh, xl, start, stop):
                pe.matmul(out, wh, xh, start=start, stop=False)
                pe.matmul(out, wh, xl, start=False, stop=False)
                return pe.matmul(out, wl, xh, start=False, stop=stop)

            def stage(name, lo, hi, b, p):
                n = b + 1
                bank, cnt = tile_use(name, b)
                tile = tiles[:, bank, :]
                if lo == 0:
                    pe.wait_ge(tile_free[bank], cnt)
                if name in ("xT", "q", "kx"):
                    if name == "xT":
                        pe.wait_ge(S["xn_done"], n + 1)
                    else:
                        taken(pe, "qt" if name == "q" else "kt", b)
                    rows = TXT if name == "kx" else L
                    for c in range(NC):
                        mm = pe.transpose(tile[:, c * rows:(c + 1) * rows], xn[0:rows, c * P:(c + 1) * P], ident[0:rows, 0:rows])
                elif name in ("qt", "kt"):
                    if lo == 0 and name == "qt":
                        taken(pe, "xT", b)
                    if lo == 0 and name == "kt":
                        pe.wait_ge(S["cl_done"], 2 * (n + 1))
                    wh, wl = wv(WQ if name == "qt" else WK)
                    rows = L if name == "qt" else TXT
                    for c in range(lo, hi):
                        if name == "qt":
                            vh, vl = xs2[:, 0, c, :], xs2[:, 1, c, :]
                        else:
                            vh, vl = cH[1][:, c, 1:TAIL], cL[1][:, c, 1:TAIL]
                        pe.matmul(tile[0:rows, :], vh, wh[:, c, :], start=(c == 0), stop=False)
                        pe.matmul(tile[0:rows, :], vh, wl[:, c, :], start=False, stop=False)
                        mm = pe.matmul(tile[0:rows, :], vl, wh[:, c, :], start=False, stop=(c == NC - 1))
                elif name[0] == "k":
                    o = int(name[1])
                    if lo == 0:
                        pe.wait_ge(S["cl_done"], 2 * n + 1)
                    wh, wl = wv(WKI)
                    for c in range(lo, hi):
                        mm = three(tile[:, 0:IMGE], wh[:, c, o * P:(o + 1) * P], wl[:, c, o * P:(o + 1) * P],
                                   cH[0][:, c, :], cL[0][:, c, :], c == 0, c == NC - 1)
                elif name[0] == "v":
                    t = int(name[1])
                    rows = P if t < 2 else TAIL
                    wh, wl = wv(WVI if t < 2 else WV)
                    for c in range(lo, hi):
                        ch, cl = (v[1][:, c, :] if t == 2 else v[0][:, c, t * P:(t + 1) * P] for v in (cH, cL))
                        pe.matmul(tile[0:rows, :], ch, wh[:, c, :], start=(c == 0), stop=False)
                        pe.matmul(tile[0:rows, :], ch, wl[:, c, :], start=False, stop=False)
                        mm = pe.matmul(tile[0:rows, :], cl, wh[:, c, :], start=False, stop=(c == NC - 1))
                elif name == "ms":
                    pe.wait_ge(S["sum_b"], n + 1)
                    for t in range(4):
                        mm = pe.matmul(tile[:, t:t + 1], ssum[:, t * P:(t + 1) * P], ones[:, 0:1], start=True, stop=True)
                elif name == "rb":
                    pe.wait_ge(S["diag_done"], n + 1)
                    mm = pe.matmul(tile[:, :], ones[:, :], diag, start=True, stop=True)
                elif name == "o":
                    if lo == 0:
                        pe.wait_ge(S["al_done"], NC * b)
                    wh, wl = wv(WO)
                    for c in range(lo, hi):
                        pe.matmul(tile[0:L, :], a2[:, 0, c, :], wh[:, c, :], start=(c == 0), stop=False)
                        pe.matmul(tile[0:L, :], a2[:, 0, c, :], wl[:, c, :], start=False, stop=False)
                        mm = pe.matmul(tile[0:L, :], a2[:, 1, c, :], wh[:, c, :], start=False, stop=(c == NC - 1))
                if hi == GROUPS[name]:
                    mm.then_inc(tile_ready[bank], 1)

            def score(b, p, h):
                if h % 4 == 0:
                    pe.wait_ge(S["qz_done"], NC * b + h // 4 + 1)
                    pe.wait_ge(S["kl_done"], NC * b + h // 4 + 1)
                if not (fixed(b, 0) and h < 2):
                    pe.wait_ge(S["exp_done"], NH * b + h - 1)
                c = (h // 4) % 2
                three(scores[0:L, h % 2, 0:KP], qzH[:, c, h % 4, :], qzL[:, c, h % 4, :], kH[:, c, :], kL[:, c, :], True, True).then_inc(S["s_ready"], 1)

            def transpose(b, h):
                pe.wait_ge(S["p_ready"], NH * b + h + 1)
                if not (fixed(b, 0) and h < 2):
                    pe.wait_ge(S["pt_done"], NH * b + h - 1)
                for t in range(KT):
                    mm = pe.transpose(ptb[:, h % 2, t * L:(t + 1) * L], probs[0:L, h % 4, t * P:(t + 1) * P], ident[0:L, 0:L])
                mm.then_inc(S["t_ready"], 1)

            def attend(b, p, g):
                pe.wait_ge(S["pt_done"], NH * b + 4 * g + 4)
                if g == 0:
                    pe.wait_ge(S["vrow_in"], 16 * (b + 1))
                pe.wait_ge(S["al_done"], NC * b + g)
                if g in (1, 2) and has_tail(b):
                    pe.wait_ge(S[("xt_done", "lg_done")[g - 1]], b)
                for t in range(KT):
                    rows = P if t < 2 else TAIL
                    for i in range(4):
                        h = 4 * g + i
                        mm = pe.matmul(pvb[HD * i:HD * i + HD, 0:L], vn[p][0:rows, t, HD * h:HD * h + HD],
                                       probT[0:rows, h % 8, t, :], start=(t == 0), stop=(t == KT - 1))
                mm.then_inc(S["pv_ready"], 1)

            def body(b, p):
                if fixed(b, -1):
                    pe.wait_ge(S["nq_done"], 3)
                    pe.wait_ge(S["wl_done"], 1)
                for h in range(NH):
                    if has_heads(b):
                        score(b, p, h)
                    if h < LAG:
                        if has_tail(b):
                            transpose(b - 1, NH - LAG + h)
                    elif has_heads(b):
                        transpose(b, h - LAG)
                    if h == 2 and has_tail(b):
                        attend(b - 1, 1 - p, 3)
                    if h in (6, 10, 14) and has_heads(b):
                        attend(b, p, (h - 6) // 4)
                    for name, lo, hi in FILL[h]:
                        if has(name, b):
                            if fixed(b, FIRST) and (name, lo) == ("v2", 0):
                                pe.wait_ge(S["wl_done"], 5)
                            if fixed(b, -1) and lo == 0 and name in ("qt", "kt", "v0"):
                                pe.wait_ge(S["wl_done"], 2 + ("qt", "kt", "v0").index(name))
                            stage(name, lo, hi, b, p)
                    if h == 8 and has_tail(b):
                        pe.wait_ge(S["xg_done"], b)
                        pe.wait_ge(S["al_done"], NC * b + has_heads(b))
                        for c in range(NC):
                            mm = pe.transpose(pvb[:, c * L:(c + 1) * L], x1[0:L, c * P:(c + 1) * P], ident[0:L, 0:L])
                        mm.then_inc(S["gate_in"], 1)
                    if h == 11 and has_tail(b):
                        pe.wait_ge(S["xt_done"], b)
                        pe.wait_ge(S["al_done"], NC * b + 2 * has_heads(b))
                        for c in range(NC):
                            mm = pe.matmul(pvb[0:L, 0:E], xt[:, c, :], wgs[:, c, :], start=(c == 0), stop=(c == NC - 1))
                        mm.then_inc(S["gate_ready"], 1)
                    if h == 0 and fixed(b, FIRST):
                        pe.wait_ge(S["small_in"], 64)
                    if h == 5 and fixed(b, FIRST):
                        pe.wait_ge(S["wl_done"], 6)
                if fixed(b, -1):
                    pe.wait_ge(S["xll"], 1)
                    wh, wl = wv(WVI)
                    for c in range(NC):
                        pe.matmul(pvb[0:B, :], xl2[:, 0, c, :], wh[:, c, :], start=(c == 0), stop=False)
                        pe.matmul(pvb[0:B, :], xl2[:, 0, c, :], wl[:, c, :], start=False, stop=False)
                        mm = pe.matmul(pvb[0:B, :], xl2[:, 1, c, :], wh[:, c, :], start=False, stop=(c == NC - 1))
                    mm.then_inc(S["vlast_mm"], 1)
                    pe.wait_ge(S["vlast_sb"], 1)

            bodies(pe, body)

            pe.wait_ge(S["route"], 11)
            mask = msk[0:L].rearrange("p b e -> p (b e)")
            pe.matmul(scores[0:L, 1, 0:B * E], upper[0:L, 0:L], mask, start=True, stop=False)
            for b in range(B - 1):
                pe.matmul(scores[0:L, 1, (b + 1) * E:B * E].rearrange("p (b e) -> p b e", e=E), ones[0:L, 0:L],
                          msk[0:L, b:b + 1, :].to_broadcast([L, B - 1 - b, E]), start=False, stop=(b == B - 2))
            pe.matmul(ptb[:, 0, 0:B * E], ones[0:L, :], mask, start=True, stop=True).then_inc(S["rank_ready"], 1)

            pe.wait_ge(S["slots_done"], 1)

            def turn(j):
                pe.wait_ge(S["xs_in"], 16 * (j + 1))
                pe.wait_ge(S["xTl_done"], j)
                for c in range(NC):
                    for t in range(2):
                        mm = pe.transpose(xTb[:, c // 2, (c % 2) * BLOCK + t * P:(c % 2) * BLOCK + (t + 1) * P],
                                          xs[:, t, c * P:(c + 1) * P], ident[:, :])
                mm.then_inc(S["xT_ready"], 1)

            turn(0)
            used = pe.value_load(ebi[0:1, MAX_BLOCKS + 1:MAX_BLOCKS + 2], min_val=1, max_val=MAX_BLOCKS)
            with pe.Fori(0, MAX_BLOCKS) as j:
                with pe.If(j < used):
                    pe.wait_ge(S["xTl_done"], j + 1)
                    for pc in range(PIECES):
                        pe.wait_ge(S["el_done"], PIECES * j + pc + 1)
                        slot = pc % 4
                        if pc < 6:
                            width, K, per = (512, NC, 4) if pc < 2 else (256, 8, 2)
                            wh = EH[slot].rearrange("p (c n) -> p c n", n=width)
                            wl = EL[slot].rearrange("p (c n) -> p c n", n=width)
                            vh, vl = (xTH, xTL) if pc < 2 else (hH[0], hL[0])
                            for i in range(per):
                                m = 4 * pc + i if pc < 2 else 8 + 2 * (pc - 2) + i
                                pe.wait_ge(S["gel_done"], 16 * j + m + 1)
                                for c in range(K):
                                    if pc == 2 and i == 0:
                                        pe.wait_ge(S["hl_done"], 16 * j + c + 5)
                                    mm = three(hid[m % 4][:, 0:BLOCK], wh[:, c, i * P:(i + 1) * P], wl[:, c, i * P:(i + 1) * P],
                                               vh[:, c, :], vl[:, c, :], c == 0, c == K - 1)
                                mm.then_inc(S["hid_ready"], 1)
                        else:
                            if pc == 6:
                                turn(j + 1)
                            wh = EH[slot].rearrange("p (c n) -> p c n", n=D)
                            wl = EL[slot].rearrange("p (c n) -> p c n", n=D)
                            for i in range(4):
                                f = 4 * (pc - 6) + i
                                pe.wait_ge(S["hl_done"], 16 * j + 8 + f + 5)
                                for t in range(2):
                                    h_hi, h_lo = hH[1][:, f, t * P:(t + 1) * P], hL[1][:, f, t * P:(t + 1) * P]
                                    pe.matmul(yb[:, t, :], h_hi, wh[:, i, :], start=(f == 0), stop=False)
                                    pe.matmul(yb[:, t, :], h_hi, wl[:, i, :], start=False, stop=False)
                                    mm = pe.matmul(yb[:, t, :], h_lo, wh[:, i, :], start=False, stop=(f == 7))
                            mm.then_inc(S["y_piece"], 1)


def kernel(**inputs):
    import numpy as _np
    import concourse.bacc as _bacc
    from concourse import mybir as _mybir
    from concourse.bass_utils import run_bass_kernel_spmd as _run

    nc = _bacc.Bacc("TRN2", target_bir_lowering=False, num_devices=1)
    a = {k: _np.asarray(v) for k, v in inputs.items()}

    def col(v):
        return v.reshape(NC, P).T

    def wt(w):
        return w.T.reshape(NC, P, D).transpose(1, 0, 2).reshape(P, NC * D)

    names = [a["L0_xattn_" + n] for n in ("q_w", "k_img_w", "k_w", "v_img_w", "v_w", "o_w")]
    vecs = [a["L0_xattn_" + n] for n in ("q_b", "k_b", "k_img_b", "v_b", "v_img_b", "norm_q_w", "norm_k_w", "norm_k_img_w")]
    ctx = a["ctx_2048"]
    W1 = a["L0_ffn_W1"].reshape(E, NC, P, 2, 512).transpose(0, 3, 2, 1, 4).reshape(E, 2, P, PIECE)
    W2 = a["L0_ffn_W2"].reshape(E, 8, P, 4, 256).transpose(0, 3, 2, 1, 4).reshape(E, 4, P, PIECE)
    W3 = a["L0_ffn_W3"].reshape(E, 2, 4, P, D).transpose(0, 1, 3, 2, 4).reshape(E, 2, P, PIECE)
    b1, b2 = (a["L0_ffn_" + n].reshape(E, 8, P).transpose(2, 0, 1) for n in ("b1", "b2"))
    ins = [
        a["x"],
        ctx.reshape(B, KEYS, NC, P).transpose(0, 3, 2, 1),
        ctx[:, IMG - 1].reshape(B, NC, P).transpose(2, 1, 0),
        _np.stack([wt(w) for w in names]),
        _np.stack([col(v) for v in vecs], axis=1),
        a["L0_xattn_o_b"],
        a["L0_ffn_Wg"].reshape(NC, P, E).transpose(1, 0, 2),
        a["L0_ffn_bg"],
        _np.concatenate([W1, W2, W3], axis=1),
        _np.concatenate([b1, b2], axis=2),
        a["L0_ffn_b3"],
    ]
    arrays, args = {}, []
    for i, v in enumerate(ins):
        v = _np.ascontiguousarray(v)
        arrays[f"in_{i}_dram"] = v
        args.append(nc.dram_tensor(f"in_{i}_dram", v.shape, _mybir.dt.from_np(v.dtype), kind="ExternalInput").ap())
    args.append(nc.dram_tensor("out_0_dram", (B, L, D), _mybir.dt.float32, kind="ExternalOutput").ap())
    cross_attention_moe(nc, *args)
    r = _run(nc, [arrays], core_ids=[0])
    return r.results[0]["out_0_dram"]
```
